# Optimizing a Trainium2 kernel written in Bass

```python
import numpy as np
import jax
import jax.numpy as jnp

def _softmax(x, axis=-1):
    return jax.nn.softmax(x, axis=axis)

def _gelu(x):
    return jax.nn.gelu(x, approximate=True)

def _silu(x):
    return jax.nn.silu(x)

def _sigmoid(x):
    return jax.nn.sigmoid(x)

def _layernorm(x, axis=-1, eps=1e-05):
    m = jnp.mean(x, axis=axis, keepdims=True)
    v = jnp.var(x, axis=axis, keepdims=True)
    return (x - m) / jnp.sqrt(v + eps)

def _scatter_add(tgt, idx, src, axis=0):
    return tgt.at[idx].add(src)

def _segment_sum(src, seg, n):
    return jax.ops.segment_sum(src, seg, n)
kernel_name = 'mk_adj_ffn_d4_adj_r2_5e33c0'

def setup_inputs(seed: int=0):
    np.random.seed(seed)
    _w = jnp.asarray

    def _rec_inputs():
        import jax
        import jax.numpy as jnp
        _gk = jax.random.key(seed)
        x = -0.0002928 + 1 * jax.random.normal(jax.random.fold_in(_gk, 1), (64, 128, 128), jnp.float32)
        _a = jax.random.bernoulli(jax.random.fold_in(_gk, 2), 0.03125, (64, 128, 128))
        _a = jnp.logical_or(_a, jnp.swapaxes(_a, -1, -2))
        _a = jnp.logical_or(_a, jnp.eye(128, dtype=bool))
        _af = _a.astype(jnp.float32)
        _af = _af * jax.random.uniform(jax.random.fold_in(_gk, 3), (64, 128, 128), jnp.float32, 0.05, 1)
        adj = _af
        return (x, adj)
    x, adj = _rec_inputs()

    def _L0_gnn_setup():
        import jax, jax.numpy as jnp
        import numpy as np
        B, N, D, H = (8, 1024, 128, 512)
        RMS_EPS = 1e-06

        def _rmsnorm(h, w, eps=RMS_EPS):
            var = jnp.mean(jnp.square(h), axis=-1, keepdims=True)
            return h * jax.lax.rsqrt(var + eps) * w
        key = jax.random.key(seed)
        ks = jax.random.split(key, 5)
        x = jax.random.normal(ks[0], (B, N, D), dtype=jnp.float32)
        adjacency = jax.random.uniform(ks[1], (B, N, N), dtype=jnp.float32)
        epsilon = jnp.zeros((), dtype=jnp.float32)
        W1 = jax.random.normal(ks[2], (D, H), dtype=jnp.float32) * (1.0 / np.sqrt(D))
        b1 = jnp.zeros((H,), dtype=jnp.float32)
        rms_weight = jnp.ones((H,), dtype=jnp.float32)
        W2 = jax.random.normal(ks[3], (H, D), dtype=jnp.float32) * (1.0 / np.sqrt(H))
        b2 = jnp.zeros((D,), dtype=jnp.float32)
        return {'x': x, 'adjacency': adjacency, 'epsilon': epsilon, 'W1': W1, 'b1': b1, 'rms_weight': rms_weight, 'W2': W2, 'b2': b2}
    _L0_gnn_all = _L0_gnn_setup()
    _L0_gnn_in = {k: v for k, v in _L0_gnn_all.items() if k in ('epsilon', 'W1', 'b1', 'rms_weight', 'W2', 'b2')}
    del _L0_gnn_all

    def _L0_ffn_setup():
        import jax, jax.numpy as jnp
        import numpy as np
        B, N, D = (16, 2048, 128)
        NUM_EXPERTS, TOP_K, HEADS = (4, 2, 4)
        N_EDGES = 524288
        LN_EPS = 1e-05

        def _layernorm(x, g, b):
            mu = x.mean(-1, keepdims=True)
            var = ((x - mu) ** 2).mean(-1, keepdims=True)
            return (x - mu) * jax.lax.rsqrt(var + LN_EPS) * g + b

        def _forward(x, edge_index, W_gat, att_src, att_dst, b_gat, ln_gamma, ln_beta, W1, b1, W2, b2):
            Bc, Nc, Dc = x.shape
            M = Bc * Nc
            x_flat = x.reshape(M, Dc)
            h = (x_flat @ W_gat).reshape(M, HEADS, NUM_EXPERTS)
            loops = jnp.arange(M, dtype=edge_index.dtype)
            src = jnp.concatenate([edge_index[0], loops])
            dst = jnp.concatenate([edge_index[1], loops])
            a_src = (h * att_src).sum(-1)
            a_dst = (h * att_dst).sum(-1)
            e = jax.nn.leaky_relu(a_src[src] + a_dst[dst], negative_slope=0.2)
            e_max = jax.ops.segment_max(e, dst, num_segments=M)
            ee = jnp.exp(e - e_max[dst])
            denom = jax.ops.segment_sum(ee, dst, num_segments=M)
            alpha = ee / (denom[dst] + 1e-16)
            msg = h[src] * alpha[:, :, None]
            agg = jax.ops.segment_sum(msg, dst, num_segments=M).reshape(M, HEADS * NUM_EXPERTS) + b_gat
            scores = _layernorm(agg, ln_gamma, ln_beta).reshape(M, HEADS, NUM_EXPERTS).mean(1)
            scores = scores.reshape(Bc, Nc, NUM_EXPERTS)
            topk_s, topk_i = jax.lax.top_k(scores, TOP_K)
            w = jax.nn.softmax(topk_s, axis=-1)
            out = jnp.zeros_like(x)
            for ei in range(NUM_EXPERTS):
                g = jnp.where(topk_i == ei, w, 0.0).sum(-1)
                hh = jax.nn.gelu(x @ W1[ei] + b1[ei], approximate=False)
                out = out + g[..., None] * (hh @ W2[ei] + b2[ei])
            return out
        key = jax.random.key(seed)
        ks = jax.random.split(key, 8)
        s = 0.05
        return {'x': jax.random.normal(ks[0], (B, N, D), jnp.float32), 'W_gat': jax.random.normal(ks[1], (D, HEADS * NUM_EXPERTS), jnp.float32) * s, 'att_src': jax.random.normal(ks[2], (HEADS, NUM_EXPERTS), jnp.float32) * s, 'att_dst': jax.random.normal(ks[3], (HEADS, NUM_EXPERTS), jnp.float32) * s, 'b_gat': jnp.zeros((HEADS * NUM_EXPERTS,), jnp.float32), 'ln_gamma': jnp.ones((HEADS * NUM_EXPERTS,), jnp.float32), 'ln_beta': jnp.zeros((HEADS * NUM_EXPERTS,), jnp.float32), 'W1': jax.random.normal(ks[4], (NUM_EXPERTS, D, 2 * D), jnp.float32) * s, 'b1': jnp.zeros((NUM_EXPERTS, 2 * D), jnp.float32), 'W2': jax.random.normal(ks[5], (NUM_EXPERTS, 2 * D, D), jnp.float32) * s, 'b2': jnp.zeros((NUM_EXPERTS, D), jnp.float32), 'edge_index': jax.random.randint(ks[6], (2, N_EDGES), 0, B * N, jnp.int32)}
    _L0_ffn_all = _L0_ffn_setup()
    _L0_ffn_in = {k: v for k, v in _L0_ffn_all.items() if k in ('W_gat', 'att_src', 'att_dst', 'b_gat', 'ln_gamma', 'ln_beta', 'W1', 'b1', 'W2', 'b2', 'edge_index')}
    del _L0_ffn_all

    def _L1_gnn_setup():
        import math
        import jax, jax.numpy as jnp
        import numpy as np
        B, N, D, H = (32, 256, 128, 8)
        HD = D // H
        key = jax.random.key(seed)
        ks = jax.random.split(key, 9)
        h = jax.random.normal(ks[0], (B, N, D), dtype=jnp.float32)
        edge = jax.random.normal(ks[1], (B, N, N), dtype=jnp.float32)
        adj = jax.random.uniform(ks[2], (B, N, N)) < 0.5
        adj_mask = adj | jnp.eye(N, dtype=bool)[None]
        s = 1.0 / math.sqrt(D)
        W_q = jax.random.normal(ks[3], (D, D), dtype=jnp.float32) * s
        W_k = jax.random.normal(ks[4], (D, D), dtype=jnp.float32) * s
        W_v = jax.random.normal(ks[5], (D, D), dtype=jnp.float32) * s
        W_e = jax.random.normal(ks[6], (H, 1), dtype=jnp.float32)
        W_o = jax.random.normal(ks[7], (D, D), dtype=jnp.float32) * s
        return {'h': h, 'edge': edge, 'adj_mask': adj_mask, 'W_q': W_q, 'W_k': W_k, 'W_v': W_v, 'W_e': W_e, 'W_o': W_o}
    _L1_gnn_all = _L1_gnn_setup()
    _L1_gnn_in = {k: v for k, v in _L1_gnn_all.items() if k in ('W_q', 'W_k', 'W_v', 'W_e', 'W_o')}
    del _L1_gnn_all

    def _L1_ffn_setup():
        import jax, jax.numpy as jnp
        import numpy as np
        B, T, IN_DIM = (64, 128, 128)
        HID, OUT_DIM = (256, 128)
        N_LAYERS, N_EXPERTS, N_SHARED = (2, 16, 1)
        key = jax.random.key(seed)
        ks = jax.random.split(key, 10)
        s = 0.02
        x = jax.random.normal(ks[0], (B, T, IN_DIM), dtype=jnp.float32)
        route_id = jax.random.randint(ks[1], (B,), 0, N_EXPERTS)
        Wi = jax.random.normal(ks[2], (HID, IN_DIM), dtype=jnp.float32) * s
        bi = jnp.zeros((HID,), dtype=jnp.float32)
        Wr = jax.random.normal(ks[3], (N_LAYERS, N_EXPERTS, HID, HID), dtype=jnp.float32) * s
        br = jax.random.normal(ks[4], (N_LAYERS, N_EXPERTS, HID), dtype=jnp.float32) * s
        Ws = jax.random.normal(ks[5], (N_LAYERS, N_SHARED, HID, HID), dtype=jnp.float32) * s
        bs = jax.random.normal(ks[6], (N_LAYERS, N_SHARED, HID), dtype=jnp.float32) * s
        Wo = jax.random.normal(ks[7], (OUT_DIM, HID), dtype=jnp.float32) * s
        bo = jnp.zeros((OUT_DIM,), dtype=jnp.float32)
        return {'x': x, 'route_id': route_id, 'Wi': Wi, 'bi': bi, 'Wr': Wr, 'br': br, 'Ws': Ws, 'bs': bs, 'Wo': Wo, 'bo': bo}
    _L1_ffn_all = _L1_ffn_setup()
    _L1_ffn_in = {k: v for k, v in _L1_ffn_all.items() if k in ('route_id', 'Wi', 'bi', 'Wr', 'br', 'Ws', 'bs', 'Wo', 'bo')}
    del _L1_ffn_all

    def _L2_gnn_setup():
        import jax, jax.numpy as jnp
        import numpy as np
        B, N, F, OUT = (32, 512, 128, 128)
        key = jax.random.key(seed)
        k1, k2, k3, k4, k5 = jax.random.split(key, 5)
        x = jax.random.normal(k1, (B, N, F), dtype=jnp.float32)
        adjacency_matrix = jax.random.uniform(k2, (B, N, N), dtype=jnp.float32)
        alpha = jax.random.uniform(k3, (1,), dtype=jnp.float32)
        W = jax.random.normal(k4, (OUT, F), dtype=jnp.float32) * (1.0 / np.sqrt(F))
        b = jax.random.normal(k5, (OUT,), dtype=jnp.float32) * 0.01
        return {'x': x, 'adjacency_matrix': adjacency_matrix, 'alpha': alpha, 'W': W, 'b': b}
    _L2_gnn_all = _L2_gnn_setup()
    _L2_gnn_in = {k: v for k, v in _L2_gnn_all.items() if k in ('alpha', 'W', 'b')}
    del _L2_gnn_all

    def _L2_ffn_setup():
        import jax, jax.numpy as jnp
        import numpy as np
        E = 8
        K = 2
        D = 128
        H = 256
        DOUT = 128
        EPS = 1e-05
        key = jax.random.key(seed)
        ks = jax.random.split(key, 9)
        s = 0.02
        return {'x': jax.random.normal(ks[0], (4, 4096, D), jnp.float32), 'gamma': 1.0 + 0.05 * jax.random.normal(ks[1], (D,), jnp.float32), 'beta': 0.05 * jax.random.normal(ks[2], (D,), jnp.float32), 'Wr': 0.01 * jax.random.normal(ks[3], (D, E), jnp.float32), 'br': jnp.zeros((E,), jnp.float32), 'W1': s * jax.random.normal(ks[4], (E, D, H), jnp.float32), 'b1': s * jax.random.normal(ks[5], (E, H), jnp.float32), 'W2': s * jax.random.normal(ks[6], (E, H, DOUT), jnp.float32), 'b2': s * jax.random.normal(ks[7], (E, DOUT), jnp.float32)}
    _L2_ffn_all = _L2_ffn_setup()
    _L2_ffn_in = {k: v for k, v in _L2_ffn_all.items() if k in ('gamma', 'beta', 'Wr', 'br', 'W1', 'b1', 'W2', 'b2')}
    del _L2_ffn_all

    def _L3_gnn_setup():
        import jax, jax.numpy as jnp
        import numpy as np
        D_IN = 128
        D_HID = 256
        key = jax.random.key(seed)
        k1, k2, k3, k4, k5, k6 = jax.random.split(key, 6)
        x = jax.random.normal(k1, (8, 2048, D_IN), dtype=jnp.float32)
        adj = jax.random.uniform(k2, (8, 2048, 2048), dtype=jnp.float32)
        s1 = 1.0 / np.sqrt(D_IN)
        s2 = 1.0 / np.sqrt(D_HID)
        W1 = jax.random.uniform(k3, (D_IN, D_HID), dtype=jnp.float32, minval=-s1, maxval=s1)
        b1 = jax.random.uniform(k4, (D_HID,), dtype=jnp.float32, minval=-s1, maxval=s1)
        W2 = jax.random.uniform(k5, (D_HID, D_IN), dtype=jnp.float32, minval=-s2, maxval=s2)
        b2 = jax.random.uniform(k6, (D_IN,), dtype=jnp.float32, minval=-s2, maxval=s2)
        eps = jnp.zeros((1,), dtype=jnp.float32)
        return {'x': x, 'adj': adj, 'eps': eps, 'W1': W1, 'b1': b1, 'W2': W2, 'b2': b2}
    _L3_gnn_all = _L3_gnn_setup()
    _L3_gnn_in = {k: v for k, v in _L3_gnn_all.items() if k in ('eps', 'W1', 'b1', 'W2', 'b2')}
    del _L3_gnn_all

    def _L3_ffn_setup():
        import jax, jax.numpy as jnp
        import numpy as np
        DIM = 128
        HEADS = 8
        NUM_KEYS = 128
        NUM_KV = NUM_KEYS ** 2
        PK_TOPK = 16
        FINAL_TOPK = 16
        DIM_KEY = DIM // 2
        P = 2

        def _pk(x, Wq_pk, pk_keys):
            b, n, _ = x.shape
            q = (x @ Wq_pk).reshape(b, n, P, HEADS, DIM_KEY).transpose(2, 0, 1, 3, 4)
            sim = jnp.einsum('pbnhd,pkhd->pbnhk', q, pk_keys)
            scores, idx = jax.lax.top_k(sim, PK_TOPK)
            idx0 = idx[0]
            idx1 = idx[1] * NUM_KEYS
            index = (idx0[..., :, None] + idx1[..., None, :]).reshape(b, n, HEADS, PK_TOPK * PK_TOPK)
            score = (scores[0][..., :, None] + scores[1][..., None, :]).reshape(b, n, HEADS, PK_TOPK * PK_TOPK)
            final_scores, pk_idx = jax.lax.top_k(score, FINAL_TOPK)
            final_indices = jnp.take_along_axis(index, pk_idx, axis=-1)
            final_scores = jax.nn.softmax(final_scores, axis=-1)
            return (final_scores, final_indices)
        key = jax.random.key(seed)
        ks = jax.random.split(key, 7)
        b, n = (2, 512)
        std = 0.02
        x = jax.random.normal(ks[0], (b, n, DIM), dtype=jnp.float32)
        Wq_pk = jax.random.normal(ks[1], (DIM, P * HEADS * DIM_KEY), dtype=jnp.float32) * std
        pk_keys = jax.random.normal(ks[2], (P, NUM_KEYS, HEADS, DIM_KEY), dtype=jnp.float32) * std
        Wq = jax.random.normal(ks[3], (DIM, HEADS * DIM), dtype=jnp.float32) * std
        keys_table = jax.random.normal(ks[4], (NUM_KV * HEADS, DIM), dtype=jnp.float32) * std
        values_table = jax.random.normal(ks[5], (NUM_KV * HEADS, DIM), dtype=jnp.float32) * std
        Wo = jax.random.normal(ks[6], (DIM * HEADS, DIM), dtype=jnp.float32) * std
        return {'x': x, 'Wq_pk': Wq_pk, 'pk_keys': pk_keys, 'Wq': Wq, 'keys_table': keys_table, 'values_table': values_table, 'Wo': Wo}
    _L3_ffn_all = _L3_ffn_setup()
    _L3_ffn_in = {k: v for k, v in _L3_ffn_all.items() if k in ('Wq_pk', 'pk_keys', 'Wq', 'keys_table', 'values_table', 'Wo')}
    del _L3_ffn_all
    return {'x': x, 'adj': adj, 'L0_gnn_epsilon': _L0_gnn_in['epsilon'], 'L0_gnn_W1': _L0_gnn_in['W1'], 'L0_gnn_b1': _L0_gnn_in['b1'], 'L0_gnn_rms_weight': _L0_gnn_in['rms_weight'], 'L0_gnn_W2': _L0_gnn_in['W2'], 'L0_gnn_b2': _L0_gnn_in['b2'], 'L0_ffn_W_gat': _L0_ffn_in['W_gat'], 'L0_ffn_att_src': _L0_ffn_in['att_src'], 'L0_ffn_att_dst': _L0_ffn_in['att_dst'], 'L0_ffn_b_gat': _L0_ffn_in['b_gat'], 'L0_ffn_ln_gamma': _L0_ffn_in['ln_gamma'], 'L0_ffn_ln_beta': _L0_ffn_in['ln_beta'], 'L0_ffn_W1': _L0_ffn_in['W1'], 'L0_ffn_b1': _L0_ffn_in['b1'], 'L0_ffn_W2': _L0_ffn_in['W2'], 'L0_ffn_b2': _L0_ffn_in['b2'], 'L0_ffn_edge_index': _L0_ffn_in['edge_index'], 'L1_gnn_W_q': _L1_gnn_in['W_q'], 'L1_gnn_W_k': _L1_gnn_in['W_k'], 'L1_gnn_W_v': _L1_gnn_in['W_v'], 'L1_gnn_W_e': _L1_gnn_in['W_e'], 'L1_gnn_W_o': _L1_gnn_in['W_o'], 'L1_ffn_route_id': _L1_ffn_in['route_id'], 'L1_ffn_Wi': _L1_ffn_in['Wi'], 'L1_ffn_bi': _L1_ffn_in['bi'], 'L1_ffn_Wr': _L1_ffn_in['Wr'], 'L1_ffn_br': _L1_ffn_in['br'], 'L1_ffn_Ws': _L1_ffn_in['Ws'], 'L1_ffn_bs': _L1_ffn_in['bs'], 'L1_ffn_Wo': _L1_ffn_in['Wo'], 'L1_ffn_bo': _L1_ffn_in['bo'], 'L2_gnn_alpha': _L2_gnn_in['alpha'], 'L2_gnn_W': _L2_gnn_in['W'], 'L2_gnn_b': _L2_gnn_in['b'], 'L2_ffn_gamma': _L2_ffn_in['gamma'], 'L2_ffn_beta': _L2_ffn_in['beta'], 'L2_ffn_Wr': _L2_ffn_in['Wr'], 'L2_ffn_br': _L2_ffn_in['br'], 'L2_ffn_W1': _L2_ffn_in['W1'], 'L2_ffn_b1': _L2_ffn_in['b1'], 'L2_ffn_W2': _L2_ffn_in['W2'], 'L2_ffn_b2': _L2_ffn_in['b2'], 'L3_gnn_eps': _L3_gnn_in['eps'], 'L3_gnn_W1': _L3_gnn_in['W1'], 'L3_gnn_b1': _L3_gnn_in['b1'], 'L3_gnn_W2': _L3_gnn_in['W2'], 'L3_gnn_b2': _L3_gnn_in['b2'], 'L3_ffn_Wq_pk': _L3_ffn_in['Wq_pk'], 'L3_ffn_pk_keys': _L3_ffn_in['pk_keys'], 'L3_ffn_Wq': _L3_ffn_in['Wq'], 'L3_ffn_keys_table': _L3_ffn_in['keys_table'], 'L3_ffn_values_table': _L3_ffn_in['values_table'], 'L3_ffn_Wo': _L3_ffn_in['Wo']}

def reference(x, adj, L0_gnn_epsilon, L0_gnn_W1, L0_gnn_b1, L0_gnn_rms_weight, L0_gnn_W2, L0_gnn_b2, L0_ffn_W_gat, L0_ffn_att_src, L0_ffn_att_dst, L0_ffn_b_gat, L0_ffn_ln_gamma, L0_ffn_ln_beta, L0_ffn_W1, L0_ffn_b1, L0_ffn_W2, L0_ffn_b2, L0_ffn_edge_index, L1_gnn_W_q, L1_gnn_W_k, L1_gnn_W_v, L1_gnn_W_e, L1_gnn_W_o, L1_ffn_route_id, L1_ffn_Wi, L1_ffn_bi, L1_ffn_Wr, L1_ffn_br, L1_ffn_Ws, L1_ffn_bs, L1_ffn_Wo, L1_ffn_bo, L2_gnn_alpha, L2_gnn_W, L2_gnn_b, L2_ffn_gamma, L2_ffn_beta, L2_ffn_Wr, L2_ffn_br, L2_ffn_W1, L2_ffn_b1, L2_ffn_W2, L2_ffn_b2, L3_gnn_eps, L3_gnn_W1, L3_gnn_b1, L3_gnn_W2, L3_gnn_b2, L3_ffn_Wq_pk, L3_ffn_pk_keys, L3_ffn_Wq, L3_ffn_keys_table, L3_ffn_values_table, L3_ffn_Wo):
    import jax
    import jax.numpy as jnp

    def _L0_gnn_ref(x, adjacency, epsilon, W1, b1, rms_weight, W2, b2):
        import jax, jax.numpy as jnp
        import numpy as np
        B, N, D, H = (8, 1024, 128, 512)
        RMS_EPS = 1e-06

        def _rmsnorm(h, w, eps=RMS_EPS):
            var = jnp.mean(jnp.square(h), axis=-1, keepdims=True)
            return h * jax.lax.rsqrt(var + eps) * w
        neighbor_sum = jnp.einsum('bnm,bmd->bnd', adjacency, x)
        agg = epsilon * x + neighbor_sum
        h = jnp.einsum('bnd,dh->bnh', agg, W1) + b1
        h = jax.nn.silu(_rmsnorm(h, rms_weight))
        out = jnp.einsum('bnh,hd->bnd', h, W2) + b2
        return out

    def _L0_ffn_ref(x, W_gat, att_src, att_dst, b_gat, ln_gamma, ln_beta, W1, b1, W2, b2, edge_index):
        import jax, jax.numpy as jnp
        import numpy as np
        B, N, D = (16, 2048, 128)
        NUM_EXPERTS, TOP_K, HEADS = (4, 2, 4)
        N_EDGES = 524288
        LN_EPS = 1e-05

        def _layernorm(x, g, b):
            mu = x.mean(-1, keepdims=True)
            var = ((x - mu) ** 2).mean(-1, keepdims=True)
            return (x - mu) * jax.lax.rsqrt(var + LN_EPS) * g + b

        def _forward(x, edge_index, W_gat, att_src, att_dst, b_gat, ln_gamma, ln_beta, W1, b1, W2, b2):
            Bc, Nc, Dc = x.shape
            M = Bc * Nc
            x_flat = x.reshape(M, Dc)
            h = (x_flat @ W_gat).reshape(M, HEADS, NUM_EXPERTS)
            loops = jnp.arange(M, dtype=edge_index.dtype)
            src = jnp.concatenate([edge_index[0], loops])
            dst = jnp.concatenate([edge_index[1], loops])
            a_src = (h * att_src).sum(-1)
            a_dst = (h * att_dst).sum(-1)
            e = jax.nn.leaky_relu(a_src[src] + a_dst[dst], negative_slope=0.2)
            e_max = jax.ops.segment_max(e, dst, num_segments=M)
            ee = jnp.exp(e - e_max[dst])
            denom = jax.ops.segment_sum(ee, dst, num_segments=M)
            alpha = ee / (denom[dst] + 1e-16)
            msg = h[src] * alpha[:, :, None]
            agg = jax.ops.segment_sum(msg, dst, num_segments=M).reshape(M, HEADS * NUM_EXPERTS) + b_gat
            scores = _layernorm(agg, ln_gamma, ln_beta).reshape(M, HEADS, NUM_EXPERTS).mean(1)
            scores = scores.reshape(Bc, Nc, NUM_EXPERTS)
            topk_s, topk_i = jax.lax.top_k(scores, TOP_K)
            w = jax.nn.softmax(topk_s, axis=-1)
            out = jnp.zeros_like(x)
            for ei in range(NUM_EXPERTS):
                g = jnp.where(topk_i == ei, w, 0.0).sum(-1)
                hh = jax.nn.gelu(x @ W1[ei] + b1[ei], approximate=False)
                out = out + g[..., None] * (hh @ W2[ei] + b2[ei])
            return out
        return _forward(x, edge_index, W_gat, att_src, att_dst, b_gat, ln_gamma, ln_beta, W1, b1, W2, b2)

    def _L1_gnn_ref(h, edge, adj_mask, W_q, W_k, W_v, W_e, W_o):
        import math
        import jax, jax.numpy as jnp
        import numpy as np
        B, N, D, H = (32, 256, 128, 8)
        HD = D // H
        b, n, _ = h.shape
        q = (h @ W_q.T).reshape(b, n, H, HD).transpose(0, 2, 1, 3)
        k = (h @ W_k.T).reshape(b, n, H, HD).transpose(0, 2, 1, 3)
        v = (h @ W_v.T).reshape(b, n, H, HD).transpose(0, 2, 1, 3)
        edge_bias = jnp.einsum('bij,h->bhij', edge, W_e[:, 0])
        scores = jnp.einsum('bhid,bhjd->bhij', q, k) / math.sqrt(HD) + edge_bias
        scores = jnp.where(adj_mask[:, None], scores, -jnp.inf)
        attn = jax.nn.softmax(scores, axis=-1)
        out = jnp.einsum('bhij,bhjd->bhid', attn, v)
        out = out.transpose(0, 2, 1, 3).reshape(b, n, D)
        return out @ W_o.T

    def _L1_ffn_ref(x, route_id, Wi, bi, Wr, br, Ws, bs, Wo, bo):
        import jax, jax.numpy as jnp
        import numpy as np
        B, T, IN_DIM = (64, 128, 128)
        HID, OUT_DIM = (256, 128)
        N_LAYERS, N_EXPERTS, N_SHARED = (2, 16, 1)
        flat = x.reshape(-1, x.shape[-1])
        n_tok = flat.shape[0]
        route = jnp.repeat(route_id, n_tok // route_id.shape[0])
        h = jax.nn.relu(flat @ Wi.T + bi)
        n_layers, n_experts = (Wr.shape[0], Wr.shape[1])
        for l in range(n_layers):
            shared = (jnp.einsum('nd,shd->snh', h, Ws[l]) + bs[l][:, None, :]).mean(axis=0)
            routed = jnp.zeros_like(h)
            for e in range(n_experts):
                ye = h @ Wr[l, e].T + br[l, e]
                routed = routed + jnp.where((route == e)[:, None], ye, 0.0)
            h = jax.nn.relu(shared + routed + h)
        out = h @ Wo.T + bo
        return out.reshape(*x.shape[:-1], out.shape[-1])

    def _L2_gnn_ref(x, adjacency_matrix, alpha, W, b):
        import jax, jax.numpy as jnp
        import numpy as np
        B, N, F, OUT = (32, 512, 128, 128)
        A = adjacency_matrix * alpha[0] + jnp.eye(adjacency_matrix.shape[1], dtype=adjacency_matrix.dtype)
        d = jnp.power(A.sum(axis=2), -0.5)
        norm_A = d[:, :, None] * A * d[:, None, :]
        h = jnp.einsum('bij,bjf->bif', norm_A, x)
        return jax.nn.relu(jnp.einsum('bnf,of->bno', h, W) + b)

    def _L2_ffn_ref(x, gamma, beta, Wr, br, W1, b1, W2, b2):
        import jax, jax.numpy as jnp
        import numpy as np
        E = 8
        K = 2
        D = 128
        H = 256
        DOUT = 128
        EPS = 1e-05
        mu = jnp.mean(x, axis=-1, keepdims=True)
        var = jnp.mean(jnp.square(x - mu), axis=-1, keepdims=True)
        xn = (x - mu) * jax.lax.rsqrt(var + EPS) * gamma + beta
        logits = jnp.einsum('bsd,de->bse', xn, Wr) + br
        top_vals, top_idx = jax.lax.top_k(logits, K)
        w = jax.nn.softmax(top_vals, axis=-1)
        w_full = jnp.einsum('bsk,bske->bse', w, jax.nn.one_hot(top_idx, E, dtype=w.dtype))
        y = jnp.zeros(x.shape[:-1] + (DOUT,), x.dtype)
        for e in range(E):
            h = jax.nn.gelu(jnp.einsum('bsd,dh->bsh', xn, W1[e]) + b1[e], approximate=False)
            y_e = jnp.einsum('bsh,hd->bsd', h, W2[e]) + b2[e]
            y = y + y_e * w_full[..., e, None]
        return y

    def _L3_gnn_ref(x, adj, eps, W1, b1, W2, b2):
        import jax, jax.numpy as jnp
        import numpy as np
        D_IN = 128
        D_HID = 256
        aggregated = jnp.einsum('bnm,bmd->bnd', adj, x)
        h = (1.0 + eps) * x + aggregated
        h = jax.nn.relu(h @ W1 + b1)
        return h @ W2 + b2

    def _L3_ffn_ref(x, Wq_pk, pk_keys, Wq, keys_table, values_table, Wo):
        import jax, jax.numpy as jnp
        import numpy as np
        DIM = 128
        HEADS = 8
        NUM_KEYS = 128
        NUM_KV = NUM_KEYS ** 2
        PK_TOPK = 16
        FINAL_TOPK = 16
        DIM_KEY = DIM // 2
        P = 2

        def _pk(x, Wq_pk, pk_keys):
            b, n, _ = x.shape
            q = (x @ Wq_pk).reshape(b, n, P, HEADS, DIM_KEY).transpose(2, 0, 1, 3, 4)
            sim = jnp.einsum('pbnhd,pkhd->pbnhk', q, pk_keys)
            scores, idx = jax.lax.top_k(sim, PK_TOPK)
            idx0 = idx[0]
            idx1 = idx[1] * NUM_KEYS
            index = (idx0[..., :, None] + idx1[..., None, :]).reshape(b, n, HEADS, PK_TOPK * PK_TOPK)
            score = (scores[0][..., :, None] + scores[1][..., None, :]).reshape(b, n, HEADS, PK_TOPK * PK_TOPK)
            final_scores, pk_idx = jax.lax.top_k(score, FINAL_TOPK)
            final_indices = jnp.take_along_axis(index, pk_idx, axis=-1)
            final_scores = jax.nn.softmax(final_scores, axis=-1)
            return (final_scores, final_indices)
        b, n, d = x.shape
        q = (x @ Wq).reshape(b, n, HEADS, DIM) * DIM ** (-0.5)
        kv_scores, indices = _pk(x, Wq_pk, pk_keys)
        offsets = jnp.arange(HEADS, dtype=indices.dtype) * NUM_KV
        ind = indices + offsets[None, None, :, None]
        k = jnp.einsum('bnhk,bnhkd->bnhd', kv_scores, keys_table[ind])
        v = jnp.einsum('bnhk,bnhkd->bnhd', kv_scores, values_table[ind])
        sim = jnp.einsum('bihd,bjhd->bhij', q, k)
        neg = -jnp.finfo(sim.dtype).max
        causal = jnp.tril(jnp.ones((n, n), dtype=bool))
        sim = jnp.where(causal, sim, neg)
        attn = jax.nn.softmax(sim, axis=-1)
        out = jnp.einsum('bhij,bjhd->bhid', attn, v)
        out = out.transpose(0, 2, 1, 3).reshape(b, n, HEADS * DIM)
        return out @ Wo
    x = x + _L0_gnn_ref(_layernorm(x, axis=-1), adj, L0_gnn_epsilon, L0_gnn_W1, L0_gnn_b1, L0_gnn_rms_weight, L0_gnn_W2, L0_gnn_b2)
    x = x + _L0_ffn_ref(_layernorm(x, axis=-1), L0_ffn_W_gat, L0_ffn_att_src, L0_ffn_att_dst, L0_ffn_b_gat, L0_ffn_ln_gamma, L0_ffn_ln_beta, L0_ffn_W1, L0_ffn_b1, L0_ffn_W2, L0_ffn_b2, L0_ffn_edge_index)
    x = x + _L1_gnn_ref(_layernorm(x, axis=-1), adj, adj, L1_gnn_W_q, L1_gnn_W_k, L1_gnn_W_v, L1_gnn_W_e, L1_gnn_W_o)
    x = x + _L1_ffn_ref(_layernorm(x, axis=-1), L1_ffn_route_id, L1_ffn_Wi, L1_ffn_bi, L1_ffn_Wr, L1_ffn_br, L1_ffn_Ws, L1_ffn_bs, L1_ffn_Wo, L1_ffn_bo)
    x = x + _L2_gnn_ref(_layernorm(x, axis=-1), adj, L2_gnn_alpha, L2_gnn_W, L2_gnn_b)
    x = x + _L2_ffn_ref(_layernorm(x, axis=-1), L2_ffn_gamma, L2_ffn_beta, L2_ffn_Wr, L2_ffn_br, L2_ffn_W1, L2_ffn_b1, L2_ffn_W2, L2_ffn_b2)
    x = x + _L3_gnn_ref(_layernorm(x, axis=-1), adj, L3_gnn_eps, L3_gnn_W1, L3_gnn_b1, L3_gnn_W2, L3_gnn_b2)
    x = x + _L3_ffn_ref(_layernorm(x, axis=-1), L3_ffn_Wq_pk, L3_ffn_pk_keys, L3_ffn_Wq, L3_ffn_keys_table, L3_ffn_values_table, L3_ffn_Wo)
    return x

_drawn_inputs = setup_inputs


def setup_inputs(seed=0):
    import zlib

    import numpy as np

    out = dict(_drawn_inputs(seed))
    spreads = {'L0_gnn_b1': (0.0, 0.1),
     'L0_gnn_rms_weight': (1.0, 0.2),
     'L0_gnn_b2': (0.0, 0.1),
     'L0_ffn_b_gat': (0.0, 0.706),
     'L0_ffn_ln_gamma': (1.0, 0.6),
     'L0_ffn_ln_beta': (0.0, 0.63),
     'L0_ffn_b1': (0.0, 0.1),
     'L0_ffn_b2': (0.0, 0.1),
     'L1_ffn_bi': (0.0, 0.382),
     'L1_ffn_bo': (0.0, 0.1),
     'L2_ffn_br': (0.0, 0.418)}
    factors = {'L0_ffn_att_src': 8.0,
     'L0_ffn_att_dst': 8.0,
     'L1_ffn_Wr': 3.206,
     'L1_ffn_br': 7.641,
     'L1_ffn_Ws': 3.483,
     'L1_ffn_bs': 7.485,
     'L2_gnn_b': 8.0,
     'L2_ffn_gamma': 8.0,
     'L2_ffn_beta': 8.0,
     'L2_ffn_Wr': 3.596,
     'L2_ffn_W1': 3.071,
     'L2_ffn_b1': 8.0,
     'L2_ffn_W2': 2.982,
     'L2_ffn_b2': 5.118,
     'L3_gnn_b1': 4.53,
     'L3_ffn_Wq_pk': 26.889,
     'L3_ffn_pk_keys': 26.247,
     'L3_ffn_Wq': 64.0,
     'L3_ffn_keys_table': 64.0,
     'L3_ffn_values_table': 26.693,
     'L3_ffn_Wo': 26.583,
     'L3_gnn_b2': 4.863}
    for name, (base, spread) in spreads.items():
        noise = np.random.default_rng([zlib.crc32(name.encode()), seed]).standard_normal(out[name].shape)
        drawn = base * np.exp(spread * noise) if base else spread * noise
        out[name] = jnp.asarray(drawn.astype(out[name].dtype))
    for name, factor in factors.items():
        out[name] = (out[name] * factor).astype(out[name].dtype)
    return out
```

```python
import concourse.bass as bass
from concourse import mybir
from contextlib import ExitStack

F32, BF16, I32 = mybir.dt.float32, mybir.dt.bfloat16, mybir.dt.int32
ALU = mybir.AluOpType
ACT = mybir.ActivationFunctionType
AX = mybir.AxisListType

P = 128
B, N, D = 64, 128, 128
NODES = B * N
EDGES = 524288
COLS = EDGES // P
LANES = 8
STEPS = COLS // LANES
HI = NODES // P
SRC_BUFS = 4
NCH = 24
FCH = 8
CPAD = 32
CHUNK = 128
FAR = 1.0e6
BIG = 1.0e30
VECTOR_LINKS = 255
EDGE_LINKS = 80


def turns(eng, count, body, own=None, links=0, peeled=1):
    for i in range(peeled):
        body(i)
    with eng.Fori(peeled, count) as i:
        if own:
            own.enter(i - peeled, links)
        body(i)
        if own:
            own.leave(count - peeled)


def wait(eng, sem, value):
    if not isinstance(value, int) or value > 0:
        eng.wait_ge(sem, value)


class Steps:

    def __init__(self, eng, sem):
        self.eng, self.sem, self.base, self.n = eng, sem, 0, 0

    def do(self, ins):
        ins.then_inc(self.sem, 1)
        self.n += 1

    def wait(self):
        self.eng.wait_ge(self.sem, self.base + self.n)

    def link(self, ins):
        self.do(ins)
        self.wait()

    def enter(self, i, each):
        self.total, self.each = self.base + self.n, each
        self.base, self.n = self.total + i * each, 0

    def leave(self, turns):
        assert self.n == self.each, f"the loop's body signals {self.n} times, not {self.each}"
        self.base, self.n = self.total + turns * self.each, 0


def build(nc, io):
    ctx = ExitStack()
    with ctx:
        taken = set()

        def fresh(name):
            while name in taken:
                name += "_"
            taken.add(name)
            return name

        def sb(name, shape, dt=F32, c=ctx):
            return c.enter_context(nc.sbuf_tensor(fresh(name), shape, dt))

        def ps(name, shape, dt=F32, c=ctx):
            return c.enter_context(nc.psum_tensor(fresh(name), shape, dt))

        held = []

        def sem(name, c=ctx):
            held.append(c.enter_context(nc.semaphore(fresh(name))))
            return held[-1]

        def clear():
            with nc.Block() as block:
                @block.sync
                def _(sp):
                    for s in held:
                        sp.sem_clear(s)
            held.clear()

        ident = sb("ident", [P, P])
        identb = sb("identb", [P, P], BF16)
        before = sb("before", [P, P])
        ones = sb("ones", [P, P])
        start = sb("start", [P, HI])
        degree = sb("degree", [P, HI])
        x_all = sb("x_all", [P, B, D])
        node = sb("node", [P, B, NCH])
        gate = sb("gate", [P, B, 4])
        sorted_src = nc.dram_tensor("sorted_src", (EDGES, 1), I32).ap()
        segment_first = nc.dram_tensor("segment_first", (EDGES, FCH), F32).ap()
        node_table = nc.dram_tensor("node_table", (NODES, NCH), F32).ap()
        running = nc.dram_tensor("running", (EDGES, NCH), F32).ap()
        carried_in = nc.dram_tensor("carried_in", (P, 2 * CPAD), F32).ap()

        edge = ExitStack()
        with edge:
            dst_lo = sb("dst_lo", [P, COLS + LANES], BF16, edge)
            dst_hi = sb("dst_hi", [P, COLS + LANES], BF16, edge)
            src = sb("src", [P, COLS], I32, edge)
            digits = sb("digits", [P, P], BF16, edge)
            base_parts = sb("base_parts", [P, 3, LANES * HI], BF16, edge)
            hot_lo = sb("hot_lo", [P, 2, LANES * P], BF16, edge)
            hot_hi = sb("hot_hi", [P, 2, LANES * HI], BF16, edge)
            count_edges(nc, io, locals())
            sort_edges(nc, io, locals())
        edge_softmax(nc, io, locals())
        node_gates(nc, io, locals())
        later_layers(nc, io, locals())


def one_hots(dve, m, g, buf):
    lo = m["dst_lo"][:, bass.ds(g * LANES, LANES)].unsqueeze(2).to_broadcast([P, LANES, P])
    hi = m["dst_hi"][:, bass.ds(g * LANES, LANES)].unsqueeze(2).to_broadcast([P, LANES, HI])
    dig = m["digits"]
    dve.tensor_tensor(m["hot_lo"][:, buf, :].rearrange("p (l d) -> p l d", l=LANES), lo,
                      dig[:, :].unsqueeze(1).to_broadcast([P, LANES, P]), ALU.is_equal)
    return dve.tensor_tensor(m["hot_hi"][:, buf, :].rearrange("p (l d) -> p l d", l=LANES), hi,
                             dig[:, 0:HI].unsqueeze(1).to_broadcast([P, LANES, HI]), ALU.is_equal)


def count_edges(nc, io, m):
    sb, ps, sem = m["sb"], m["ps"], m["sem"]
    W = 512
    with ExitStack() as c:
        raw = sb("raw", [P, 2, W], I32, c)
        part = sb("part", [P, W], I32, c)
        num = sb("num", [P, W], F32, c)
        neg = sb("neg", [P, W], F32, c)
        zero_row = sb("zero_row", [P, 2048], I32, c)
        lane_count = sb("lane_count", [P, LANES * HI], F32, c)
        base = sb("base", [P, LANES * HI], F32, c)
        upto = sb("upto", [P, HI], F32, c)
        counts_ps = ps("counts_ps", [P, LANES * HI], F32, c)
        prefix_ps = ps("prefix_ps", [P, 2 * HI], F32, c)
        consts, s_prefill = sem("consts", c), sem("s_prefill", c)
        raw_in = [sem(f"raw_in{i}", c) for i in range(2)]
        raw_used, s_dve = sem("raw_used", c), sem("count_chain", c)
        hot_ready, hot_used, counted = sem("hot_ready", c), sem("hot_used", c), sem("counted", c)
        degree_ready, prefix_ready = sem("degree_ready", c), sem("prefix_ready", c)
        zeros_ready = sem("zeros_ready", c)
        chunks = [(row, t) for row in (1, 0) for t in range(COLS // W)]
        edges = io["edge_index"].rearrange("r (p t) -> r p t", p=P)
        ones, before, ident, identb, digits = m["ones"], m["before"], m["ident"], m["identb"], m["digits"]
        c.callback(m["clear"])
        block = c.enter_context(nc.Block())

        @block.gpsimd
        def _(pool):
            pool.memset(ident[:, :], 0.0).then_inc(consts, 1)
            pool.memset(identb[:, :], 0.0).then_inc(consts, 1)
            pool.memset(ones[:, :], 1.0).then_inc(consts, 1)
            pool.memset(zero_row[:, :], 0).then_inc(zeros_ready, 1)
            pool.iota(digits[:, :], [[1, P]], base=0, channel_multiplier=0,
                      allow_small_or_imprecise_dtypes=True).then_inc(consts, 1)
            pool.wait_ge(consts, 4)
            for t in (ident, identb):
                pool.affine_select(out=t[:, :], in_=t[:, :], compare_op=ALU.not_equal, fill=1.0, base=0,
                                   pattern=[[-1, P]], channel_multiplier=1).then_inc(consts, 1)
            pool.affine_select(out=before[:, :], in_=ones[:, :], compare_op=ALU.is_gt, fill=0.0, base=0,
                               pattern=[[1, P]], channel_multiplier=-1).then_inc(consts, 1)

        @block.sync
        def _(sp):
            for n, (row, t) in enumerate(chunks):
                if n >= 2:
                    sp.wait_ge(raw_used, n - 1)
                sp.dma_start(raw[:, n % 2, :], edges[row, :, t * W:(t + 1) * W]).then_inc(raw_in[n % 2], 16)
            sp.wait_ge(zeros_ready, 1)
            out = m["sorted_src"].rearrange("(p t) o -> p (t o)", p=P)
            for t in range(COLS // 2048):
                sp.dma_start(out[:, t * 2048:(t + 1) * 2048], zero_row[:, :]).then_inc(s_prefill, 16)
            out = m["segment_first"].rearrange("(p t) c -> p (t c)", p=P)
            for t in range(COLS * FCH // 2048):
                sp.dma_start(out[:, t * 2048:(t + 1) * 2048].bitcast(I32), zero_row[:, :]).then_inc(s_prefill, 16)
            sp.wait_ge(s_prefill, 16 * (COLS + COLS * FCH) // 2048)

        @block.vector
        def _(dve):
            own = Steps(dve, s_dve)
            own.do(dve.memset(m["dst_lo"][:, COLS:], 0.0))
            own.do(dve.memset(m["dst_hi"][:, COLS:], float(HI)))
            own.link(dve.memset(lane_count[:, :], 0.0))
            dve.tensor_copy(base[:, :], lane_count[:, :]).then_inc(counted, 1)
            for n, (row, t) in enumerate(chunks):
                dve.wait_ge(raw_in[n % 2], 16 * (n // 2 + 1))
                cols = slice(t * W, (t + 1) * W)
                r = raw[:, n % 2, :]
                if row:
                    own.link(dve.tensor_scalar(part[:, :], r, 127, None, ALU.bitwise_and))
                    own.link(dve.tensor_copy(m["dst_lo"][:, cols], part[:, :]))
                    own.link(dve.tensor_scalar(part[:, :], r, 7, None, ALU.arith_shift_right))
                    own.link(dve.tensor_scalar(neg[:, :], part[:, :], 0.0, 1.0e9, ALU.is_lt, ALU.mult))
                    own.link(dve.tensor_tensor(num[:, :], part[:, :], neg[:, :], ALU.add))
                    dve.tensor_scalar(m["dst_hi"][:, cols], num[:, :], float(HI), None, ALU.min)\
                        .then_inc(raw_used, 1)
                else:
                    own.link(dve.tensor_scalar(neg[:, :], r, 0.0, float(NODES), ALU.is_lt, ALU.mult))
                    own.link(dve.tensor_tensor(num[:, :], r, neg[:, :], ALU.add))
                    dve.tensor_scalar(m["src"][:, cols], num[:, :], 0.0, float(NODES - 1), ALU.max, ALU.min)\
                        .then_inc(raw_used, 1)
                dve.wait_ge(raw_used, n + 1)
            dve.wait_ge(consts, 7)
            with dve.Fori(0, STEPS // 2) as i:
                for k in range(2):
                    dve.wait_ge(hot_used, 2 * i + k + 1)
                    one_hots(dve, m, 2 * i + k, k).then_inc(hot_ready, 1)
            dve.wait_ge(hot_used, STEPS + 2)
            own.link(dve.tensor_copy(lane_count[:, :], counts_ps[:, :]))
            dve.tensor_reduce(m["degree"][:, :], lane_count[:, :].rearrange("p (l h) -> p h l", l=LANES),
                              AX.X, ALU.add).then_inc(degree_ready, 1)
            dve.wait_ge(prefix_ready, 1)
            own.link(dve.tensor_tensor_scan(upto[:, :], ones[:, 0:HI], prefix_ps[:, HI:], 0.0, ALU.mult, ALU.add))
            own.link(dve.tensor_tensor(upto[:, :], upto[:, :], prefix_ps[:, HI:], ALU.subtract))
            own.link(dve.tensor_tensor(m["start"][:, :], upto[:, :], prefix_ps[:, 0:HI], ALU.add))
            own.link(dve.tensor_copy(base[:, 0:HI], m["start"][:, :]))
            for l in range(1, LANES):
                a, b = slice((l - 1) * HI, l * HI), slice(l * HI, (l + 1) * HI)
                own.link(dve.tensor_tensor(base[:, b], base[:, a], lane_count[:, a], ALU.add))
            for q in range(3):
                own.link(dve.tensor_copy(m["base_parts"][:, q, :], base[:, :]))
                own.link(dve.tensor_tensor(base[:, :], base[:, :], m["base_parts"][:, q, :], ALU.subtract))

        @block.tensor
        def _(pe):
            pe.sem_inc(hot_used, 2)
            pe.wait_ge(counted, 1)
            pe.wait_ge(consts, 7)
            pe.matmul(counts_ps[:, :], ones[:, :], base[:, :], start=True, stop=False, skip_group_check=True)
            with pe.Fori(0, STEPS // 2) as i:
                for k in range(2):
                    pe.wait_ge(hot_ready, 2 * i + k + 1)
                    for l in range(LANES):
                        last = pe.matmul(counts_ps[:, l * HI:(l + 1) * HI], m["hot_lo"][:, k, l * P:(l + 1) * P],
                                         m["hot_hi"][:, k, l * HI:(l + 1) * HI], start=False, stop=False,
                                         skip_group_check=True)
                    last.then_inc(hot_used, 1)
            pe.wait_ge(degree_ready, 1)
            pe.matmul(prefix_ps[:, 0:HI], before[:, :], m["degree"][:, :], start=True, stop=True)
            pe.matmul(prefix_ps[:, HI:], ones[:, :], m["degree"][:, :], start=True, stop=True)\
                .then_inc(prefix_ready, 1)


def sort_edges(nc, io, m):
    sb, ps, sem = m["sb"], m["ps"], m["sem"]
    with ExitStack() as c:
        hot_lo, hot_hi = m["hot_lo"], m["hot_hi"]
        hot_loT = sb("hot_loT", [P, 2, LANES * P], BF16, c)
        same = sb("same", [P, 2, LANES * P], BF16, c)
        count_parts = sb("count_parts", [P, 2, 2, LANES * HI], BF16, c)
        chosen = sb("chosen", [P, LANES * HI], F32, c)
        place_f = sb("place_f", [P, LANES], F32, c)
        absent = sb("absent", [P, LANES], F32, c)
        place = sb("place", [P, SRC_BUFS, LANES], I32, c)
        moved = sb("moved", [P, SRC_BUFS, LANES], I32, c)
        zeros = sb("zeros", [P, LANES * HI], F32, c)
        loT_ps = ps("loT_ps", [P, LANES * P], BF16, c)
        same_ps = ps("same_ps", [P, LANES * P], F32, c)
        place_ps = ps("place_ps", [P, LANES * HI], F32, c)
        count_ps = ps("count_ps", [P, LANES * HI], F32, c)
        hot_ready, loT_made, loT_ready = sem("hot_ready2", c), sem("loT_made", c), sem("loT_ready", c)
        same_made, same_ready = sem("same_made", c), sem("same_ready", c)
        counted, high_ready, parts_ready = sem("counted2", c), sem("high_ready", c), sem("parts_ready", c)
        placed, chosen_done, place_ready = sem("placed", c), sem("chosen_done", c), sem("place_ready", c)
        s_dve = sem("sort_chain", c)
        scattered = [sem(f"scattered{q}", c) for q in range(SRC_BUFS)]
        eps_ident = sb("eps_ident", [P, P], F32, c)
        w1, w2 = sb("gnn0_w1", [P, 4 * D], F32, c), sb("gnn0_w2", [P, 4, D], F32, c)
        rms_w, att = sb("rms_w", [P, 4 * D], F32, c), sb("att", [P, 2, 16], F32, c)
        b1, b2 = sb("gnn0_b1", [1, 4 * D], F32, c), sb("gnn0_b2", [1, D], F32, c)
        w_node, w_att = sb("w_node", [P, NCH], F32, c), sb("w_att", [P, 2, 16], F32, c)
        eps_in = sb("gnn0_eps", [P, 1], F32, c)
        xa, adjT = sb("xa", [P, D], F32, c), sb("adjT0", [P, P], F32, c)
        stats, mv, std, rstd = (sb(n, [P, w], F32, c) for n, w in
                                (("stats0", 6), ("mv0", 2), ("std0", 1), ("rstd0", 1)))
        z, z2, aggT, z2T = (sb(n, [P, D], F32, c) for n in ("z0", "z02", "aggT0", "z2T0"))
        squares, hn, hs = (sb(n, [P, 4 * D], F32, c) for n in ("squares", "hn0", "hs0"))
        hsT, ssq = sb("hsT0", [P, 4 * D], F32, c), sb("ssq0", [P, 1], F32, c)
        eps_rms, eps_ln = sb("eps_rms", [P, 1], F32, c), sb("eps_ln0", [P, 1], F32, c)
        small_ps, h_ps, hsT_ps = (ps(n, [P, 4 * D], F32, c) for n in ("small_ps", "h_ps0", "hsT_ps0"))
        weights_in, x_in, adj_in = sem("weights_in0", c), sem("x_in0", c), sem("adj_in0", c)
        s_var, s_std, s_z, s_agg, s_aggT, s_h, s_sq, s_rms, s_hn, s_hs, s_hsT, s_hsTs, s_y, s_x = (
            sem("a_" + n, c) for n in ("var std z agg aggT h squares rms hn hs hsT hsT_copied y x").split())
        s_var2, s_std2, s_z2, s_z2T, s_z2Ts, s_node, s_kept = (
            sem("a2_" + n, c) for n in ("var std z zT zT_copied node node_kept").split())
        w_ready = sem("w_node_ready", c)
        c.callback(m["clear"])
        block = c.enter_context(nc.Block())
        TURNS, UN = STEPS // 8, 8
        assert TURNS == B

        @block.sync
        def _(sp):
            for dst, name in ((w1, "gnn0_w1"), (w2, "gnn0_w2"), (rms_w, "gnn0_rms"), (att, "gat_att"),
                              (b1, "gnn0_b1"), (b2, "gnn0_b2"), (eps_in, "gnn0_eps")):
                sp.dma_start(dst[tuple([slice(None)] * len(dst.shape))], io[name]).then_inc(weights_in, 16)
            sp.dma_start(w_node[:, 0:16], io["w_gat"]).then_inc(weights_in, 16)

            def load(i):
                wait(sp, s_x, i)
                sp.dma_start(xa[:, :], io["x"][bass.ds(i, 1), :, :].rearrange("o n d -> (o n) d"))\
                    .then_inc(x_in, 16)
                wait(sp, s_agg, i)
                sp.dma_start(adjT[:, :], io["adjT"][bass.ds(i, 1), :, :].rearrange("o n d -> (o n) d"))\
                    .then_inc(adj_in, 16)
            turns(sp, B, load)
            sp.wait_ge(s_kept, B)
            sp.dma_start(m["node_table"].rearrange("(b n) c -> n b c", n=P), m["node"][:, :, :])\
                .then_inc(x_in, 16)
            sp.wait_ge(x_in, 16 * (B + 1))

        def gnn_vector(dve, own, i, k):
            def norm(x, out, got, std_ready, var_ready, z_ready):
                dve.nop(nofuse=True)
                own.link(dve.bn_stats(stats[:, :], x))
                dve.nop(nofuse=True)
                dve.bn_aggr(mv[:, :], stats[:, :]).then_inc(var_ready, 1)
                dve.wait_ge(var_ready, i + 1)
                dve.wait_ge(std_ready, i + 1)
                own.link(dve.reciprocal(rstd[:, :], std[:, :]))
                dve.tensor_scalar(out, x, mv[:, 0:1], rstd[:, :], ALU.subtract, ALU.mult).then_inc(z_ready, 1)
            if k == 0:
                dve.wait_ge(x_in, 16 * (i + 1))
                norm(xa[:, :], z[:, :], x_in, s_std, s_var, s_z)
                dve.wait_ge(s_z, i + 1)
            if k == 2:
                dve.wait_ge(s_rms, i + 1)
                own.link(dve.reciprocal(rstd[:, :], std[:, :]))
                dve.scalar_tensor_tensor(hn[:, :], h_ps[:, :], rstd[:, :], rms_w[:, :], ALU.mult, ALU.mult)\
                    .then_inc(s_hn, 1)
            if k == 5:
                dve.wait_ge(s_y, i + 1)
                dve.wait_ge(s_hn, i + 1)
                x1 = m["x_all"][:, bass.ds(i, 1), :].rearrange("p o d -> p (o d)")
                dve.tensor_tensor(x1, xa[:, :], small_ps[:, D:2 * D], ALU.add).then_inc(s_x, 1)
                dve.wait_ge(s_x, i + 1)
                norm(x1, z2[:, :], None, s_std2, s_var2, s_z2)
                dve.wait_ge(s_z2, i + 1)
            if k == 7:
                dve.wait_ge(s_node, i + 1)
                dve.tensor_copy(m["node"][:, bass.ds(i, 1), :].rearrange("p o c -> p (o c)"),
                                small_ps[:, 3 * D:3 * D + NCH]).then_inc(s_kept, 1)

        def gnn_scalar(act, i, k):
            if k == 0:
                act.wait_ge(s_var, i + 1)
                act.activation(std[:, :], mv[:, 1:2], ACT.Sqrt, bias=eps_ln[:, :]).then_inc(s_std, 1)
            if k == 1:
                act.wait_ge(s_agg, i + 1)
                act.activation(aggT[:, :], small_ps[:, 0:D], ACT.Copy).then_inc(s_aggT, 1)
            if k == 2:
                act.wait_ge(s_h, i + 1)
                act.activation(squares[:, :], h_ps[:, :], ACT.Square, accum_out=ssq[:, :]).then_inc(s_sq, 1)
                act.wait_ge(s_sq, i + 1)
                act.activation(std[:, :], ssq[:, :], ACT.Sqrt, bias=eps_rms[:, :], scale=1.0 / (4 * D))\
                    .then_inc(s_rms, 1)
            if k == 3:
                act.wait_ge(s_hn, i + 1)
                act.activation(hs[:, :], hn[:, :], ACT.Silu).then_inc(s_hs, 1)
            if k == 4:
                act.wait_ge(s_hsT, i + 1)
                act.activation(hsT[:, :], hsT_ps[:, :], ACT.Copy).then_inc(s_hsTs, 1)
            if k == 5:
                act.wait_ge(s_var2, i + 1)
                act.activation(std[:, :], mv[:, 1:2], ACT.Sqrt, bias=eps_ln[:, :]).then_inc(s_std2, 1)
            if k == 6:
                act.wait_ge(s_z2T, i + 1)
                act.activation(z2T[:, :], small_ps[:, 2 * D:3 * D], ACT.Copy).then_inc(s_z2Ts, 1)

        def gnn_tensor(pe, i, k):
            if k == 1:
                pe.wait_ge(s_z, i + 1)
                pe.wait_ge(adj_in, 16 * (i + 1))
                pe.matmul(small_ps[:, 0:D], z[:, :], adjT[:, :], start=True, stop=False)
                pe.matmul(small_ps[:, 0:D], z[:, :], eps_ident[:, :], start=False, stop=True).then_inc(s_agg, 1)
                pe.wait_ge(s_aggT, i + 1)
                pe.matmul(h_ps[:, :], aggT[:, :], w1[:, :], start=True, stop=False)
                pe.matmul(h_ps[:, :], m["ones"][0:1, :], b1[:, :], start=False, stop=True).then_inc(s_h, 1)
            if k == 3:
                pe.wait_ge(s_hs, i + 1)
                for q in range(4):
                    last = pe.transpose(hsT_ps[:, q * D:(q + 1) * D], hs[:, q * D:(q + 1) * D], m["ident"][:, :])
                last.then_inc(s_hsT, 1)
            if k == 4:
                pe.wait_ge(s_hsTs, i + 1)
                for q in range(4):
                    pe.matmul(small_ps[:, D:2 * D], hsT[:, q * D:(q + 1) * D], w2[:, q, :], start=(q == 0), stop=False)
                pe.matmul(small_ps[:, D:2 * D], m["ones"][0:1, :], b2[:, :], start=False, stop=True).then_inc(s_y, 1)
            if k == 6:
                pe.wait_ge(s_z2, i + 1)
                pe.transpose(small_ps[:, 2 * D:3 * D], z2[:, :], m["ident"][:, :]).then_inc(s_z2T, 1)
                pe.wait_ge(s_z2Ts, i + 1)
                pe.matmul(small_ps[:, 3 * D:3 * D + NCH], z2T[:, :], w_node[:, :], start=True, stop=True)\
                    .then_inc(s_node, 1)

        @block.vector
        def _(dve):
            own = Steps(dve, s_dve)
            own.do(dve.memset(zeros[:, :], 0.0))
            own.link(dve.memset(count_parts[:, :, :, :], 0.0))
            own.do(dve.memset(eps_rms[:, :], 1e-6))
            own.link(dve.memset(eps_ln[:, :], 1e-5))
            dve.wait_ge(weights_in, 16 * 8)
            own.link(dve.tensor_scalar(eps_ident[:, :], m["ident"][:, :], eps_in[:, :], None, ALU.mult))
            own.link(dve.tensor_tensor(w_att[:, :, :], att[:, :, :],
                                       w_node[:, 0:16].unsqueeze(1).to_broadcast([P, 2, 16]), ALU.mult))
            dve.tensor_reduce(w_node[:, 16:24], w_att[:, :, :].rearrange("p a (h e) -> p (a h) e", h=4), AX.X, ALU.add)\
                .then_inc(w_ready, 1)
            dve.wait_ge(w_ready, 1)
            dve.nop(nofuse=True).then_inc(parts_ready, 1)
            one_hots(dve, m, 0, 0).then_inc(hot_ready, 1)

            def turn(i):
                for k in range(UN):
                    g = i * UN + k
                    buf, nxt, q = k % 2, (k + 1) % 2, k % SRC_BUFS
                    dve.wait_ge(placed, g + 2)
                    one_hots(dve, m, g + 1, nxt).then_inc(hot_ready, 1)
                    dve.wait_ge(same_made, g + 1)
                    dve.tensor_tensor(same[:, buf, :].rearrange("p (l e) -> p l e", l=LANES),
                                      same_ps[:, :].rearrange("p (l e) -> p l e", l=LANES),
                                      m["before"][:, :].unsqueeze(1).to_broadcast([P, LANES, P]),
                                      ALU.mult).then_inc(same_ready, 1)
                    dve.wait_ge(high_ready, g + 1)
                    dve.tensor_tensor(count_parts[:, nxt, 1, :], count_ps[:, :], count_parts[:, nxt, 0, :],
                                      ALU.subtract).then_inc(parts_ready, 1)
                    dve.wait_ge(placed, g + 3)
                    dve.tensor_tensor(chosen[:, :], place_ps[:, :], hot_hi[:, buf, :], ALU.mult)\
                        .then_inc(chosen_done, 1)
                    dve.wait_ge(chosen_done, g + 1)
                    own.do(dve.tensor_reduce(place_f[:, :], chosen[:, :].rearrange("p (l h) -> p l h", l=LANES),
                                             AX.X, ALU.add))
                    own.link(dve.tensor_scalar(absent[:, :], m["dst_hi"][:, bass.ds(g * LANES, LANES)],
                                               float(HI), FAR, ALU.is_equal, ALU.mult))
                    wait(dve, scattered[q], 16 * LANES * (i * (UN // SRC_BUFS) + k // SRC_BUFS))
                    own.do(dve.tensor_copy(moved[:, q, :], m["src"][:, bass.ds(g * LANES, LANES)]))
                    dve.tensor_tensor(place[:, q, :], place_f[:, :], absent[:, :], ALU.add)\
                        .then_inc(place_ready, 1)
                    dve.wait_ge(place_ready, g + 1)
                    gnn_vector(dve, own, i, k)
            turns(dve, TURNS, turn, own, 3 * UN + 5)

        @block.scalar
        def _(act):
            act.wait_ge(w_ready, 1)

            def turn(i):
                for k in range(UN):
                    g = i * UN + k
                    buf, nxt = k % 2, (k + 1) % 2
                    act.wait_ge(loT_made, g + 1)
                    act.wait_ge(placed, g + 1)
                    act.activation(hot_loT[:, buf, :], loT_ps[:, :], ACT.Copy).then_inc(loT_ready, 1)
                    act.wait_ge(counted, g + 1)
                    act.wait_ge(placed, g + 2)
                    act.activation(count_parts[:, nxt, 0, :], count_ps[:, :], ACT.Copy).then_inc(high_ready, 1)
                    gnn_scalar(act, i, k)
            turns(act, TURNS, turn)

        @block.tensor
        def _(pe):
            pe.sem_inc(placed, 2)
            pe.wait_ge(hot_ready, 1)
            pe.wait_ge(parts_ready, 1)
            pe.wait_ge(w_ready, 1)
            pe.wait_ge(weights_in, 16 * 8)
            pe.matmul(count_ps[:, :], m["ones"][:, :], zeros[:, :], start=True, stop=False, skip_group_check=True)

            def turn(i):
                for k in range(UN):
                    g = i * UN + k
                    buf = k % 2
                    pe.wait_ge(hot_ready, g + 1)
                    wait(pe, loT_ready, g)
                    for l in range(LANES):
                        last = pe.transpose(loT_ps[:, l * P:(l + 1) * P], hot_lo[:, buf, l * P:(l + 1) * P],
                                            m["identb"][:, :])
                    last.then_inc(loT_made, 1)
                    pe.wait_ge(parts_ready, g + 1)
                    for l in range(LANES):
                        last = pe.matmul(count_ps[:, l * HI:(l + 1) * HI], hot_lo[:, buf, l * P:(l + 1) * P],
                                         hot_hi[:, buf, l * HI:(l + 1) * HI], start=False, stop=False,
                                         skip_group_check=True)
                    last.then_inc(counted, 1)
                    pe.wait_ge(loT_ready, g + 1)
                    wait(pe, same_ready, g)
                    for l in range(LANES):
                        lo = hot_loT[:, buf, l * P:(l + 1) * P]
                        last = pe.matmul(same_ps[:, l * P:(l + 1) * P], lo, lo, start=True, stop=True)
                    last.then_inc(same_made, 1)
                    wait(pe, chosen_done, g)
                    pe.wait_ge(same_ready, g + 1)
                    for l in range(LANES):
                        h = slice(l * HI, (l + 1) * HI)
                        lo = hot_loT[:, buf, l * P:(l + 1) * P]
                        out = place_ps[:, h]
                        pe.matmul(out, same[:, buf, l * P:(l + 1) * P], hot_hi[:, buf, h], start=True, stop=False)
                        for q in range(2):
                            pe.matmul(out, lo, count_parts[:, buf, q, h], start=False, stop=False)
                        for q in range(3):
                            last = pe.matmul(out, lo, m["base_parts"][:, q, h], start=False, stop=(q == 2))
                    last.then_inc(placed, 1)
                    gnn_tensor(pe, i, k)
            turns(pe, TURNS, turn)

        @block.gpsimd
        def _(pool):

            def turn(i):
                for k in range(UN):
                    q = k % SRC_BUFS
                    pool.wait_ge(place_ready, i * UN + k + 1)
                    pool.nop(nofuse=True)
                    for l in range(LANES):
                        pool.indirect_dma_start(
                            out=m["sorted_src"],
                            out_offset=bass.IndirectOffsetOnAxis(ap=place[:, q, l:l + 1], axis=0),
                            in_=moved[:, q, l:l + 1], in_offset=None,
                            bounds_check=EDGES - 1, oob_is_err=False).then_inc(scattered[q], 16)
            turns(pool, TURNS, turn)
            for q in range(SRC_BUFS):
                pool.wait_ge(scattered[q], 16 * LANES * (STEPS // SRC_BUFS))
                pool.nop(nofuse=True)


def edge_softmax(nc, io, m):
    sb, ps, sem = m["sb"], m["ps"], m["sem"]
    node, start, degree = m["node"], m["start"], m["degree"]
    H, TURNS = 4, COLS // CHUNK // 2
    with ExitStack() as c:
        bounds = sb("bounds", [P, P], F32, c)
        end = sb("end", [P, HI], F32, c)
        first_row = sb("first_row", [P, HI, FCH], F32, c)
        first_place = sb("first_place", [P, HI], I32, c)
        empty = sb("empty", [P, HI], F32, c)
        over = sb("over", [P, 2, 8, P], F32, c)
        target_in = sb("target_in", [P, H], F32, c)
        index = sb("index", [P, 2, CHUNK], I32, c)
        rows = sb("rows", [P, 2, CHUNK, NCH], F32, c)
        firsts = sb("firsts", [P, 2, CHUNK, FCH], F32, c)
        state = sb("state", [P, 2, CHUNK, NCH], F32, c)
        inside, reset = sb("inside", [P, CHUNK], F32, c), sb("reset", [P, CHUNK], F32, c)
        target, score, leaky, keep, weight = (sb(n, [P, H, CHUNK], F32, c) for n in
                                              ("target", "score", "leaky", "keep", "weight"))
        top = sb("top", [P, H, CHUNK + 1], F32, c)
        feats = sb("feats", [P, 16, CHUNK], F32, c)
        carry = sb("carry", [P, NCH], F32, c)
        any_first, some = sb("any_first", [P, 1], F32, c), sb("some", [P, 1], F32, c)
        ends = sb("ends", [P, 3, CPAD], F32, c)
        endsT = sb("endsT", [CPAD, 3, P], F32, c)
        runT = sb("runT", [CPAD, 2, P + 1], F32, c)
        keepT, weightT, insideT, resetT = (sb(n, [CPAD, P], F32, c) for n in ("keepT", "weightT", "insideT", "resetT"))
        carried = sb("carried", [P, 2, CPAD], F32, c)
        target_ps = ps("target_ps", [P, 512], F32, c)
        ends_ps = ps("ends_ps", [P, 512], F32, c)
        back_ps = ps("back_ps", [P, 512], F32, c)
        s_dve, s_bounds, firsts_ready, scattered = (sem(n, c) for n in
                                                    ("edge_chain", "bounds_ready", "firsts_ready", "firsts_scattered"))
        over_ready, over_used = sem("over_ready", c), sem("over_used", c)
        index_in, gathered, firsts_in, stored = ([sem(f"{n}{q}", c) for q in range(2)] for n in
                                                 ("index_in", "rows_gathered", "firsts_in", "state_stored"))
        consumed, state_ready, exp_in, exp_out = (sem(n, c) for n in ("consumed", "state_ready", "exp_in", "exp_out"))
        ends_ready, ends_T, run_ready, run_T, carried_ready, carried_out = (
            sem(n, c) for n in ("ends_ready", "ends_transposed", "run_ready", "run_transposed", "carried_ready",
                                "carried_out"))
        by_place = lambda ap: ap.rearrange("(p t) c -> p t c", p=P)
        c.callback(m["clear"])
        block = c.enter_context(nc.Block())

        @block.gpsimd
        def _(pool):
            pool.iota(bounds[:, :], [[COLS, P]], base=0, channel_multiplier=0,
                      allow_small_or_imprecise_dtypes=True).then_inc(s_bounds, 1)
            pool.wait_ge(firsts_ready, 1)
            for h in range(HI):
                pool.indirect_dma_start(
                    out=m["segment_first"], out_offset=bass.IndirectOffsetOnAxis(ap=first_place[:, h:h + 1], axis=0),
                    in_=first_row[:, h, :], in_offset=None, bounds_check=EDGES - 1, oob_is_err=False)\
                    .then_inc(scattered, 16)
            with pool.Fori(0, TURNS) as i:
                for q in range(2):
                    pool.wait_ge(index_in[q], 16 * (i + 1))
                    pool.nop(nofuse=True)
                    pool.wait_ge(consumed, 2 * i + q + 1)
                    pool.nop(nofuse=True)
                    for t in range(CHUNK):
                        pool.indirect_dma_start(
                            out=rows[:, q, t, :], out_offset=None, in_=m["node_table"],
                            in_offset=bass.IndirectOffsetOnAxis(ap=index[:, q, t:t + 1], axis=0))\
                            .then_inc(gathered[q], 16)

        @block.sync
        def _(sp):
            sorted_src = m["sorted_src"].rearrange("(p t) o -> p (t o)", p=P)
            sp.wait_ge(scattered, 16 * HI)
            with sp.Fori(0, TURNS) as i:
                for q in range(2):
                    sp.wait_ge(consumed, 2 * i + q + 1)
                    sp.dma_start(index[:, q, :], sorted_src[:, bass.ds((2 * i + q) * CHUNK, CHUNK)])\
                        .then_inc(index_in[q], 16)
                    sp.dma_start(firsts[:, q, :, :],
                                 by_place(m["segment_first"])[:, bass.ds((2 * i + q) * CHUNK, CHUNK), :])\
                        .then_inc(firsts_in[q], 16)

        @block.scalar
        def _(act):
            with act.Fori(0, TURNS) as i:
                for q in range(2):
                    n = 2 * i + q
                    act.wait_ge(exp_in, 2 * n + 1)
                    act.activation(keep[:, :, :], keep[:, :, :], ACT.Exp).then_inc(exp_out, 1)
                    act.wait_ge(exp_in, 2 * n + 2)
                    act.activation(weight[:, :, :], weight[:, :, :], ACT.Exp).then_inc(exp_out, 1)
                    act.wait_ge(state_ready, n + 1)
                    act.dma_start(by_place(m["running"])[:, bass.ds(n * CHUNK, CHUNK), :], state[:, q, :, :])\
                        .then_inc(stored[q], 16)
            K = COLS // CHUNK
            act.wait_ge(exp_in, 2 * K + 1)
            act.activation(keepT[:, :], keepT[:, :], ACT.Exp).then_inc(exp_out, 1)
            act.wait_ge(exp_in, 2 * K + 2)
            act.activation(weightT[:, :], weightT[:, :], ACT.Exp).then_inc(exp_out, 1)
            act.wait_ge(carried_ready, 1)
            act.dma_start(m["carried_in"], carried[:, :, :].rearrange("p a c -> p (a c)")).then_inc(carried_out, 16)
            for q in range(2):
                act.wait_ge(stored[q], 16 * TURNS)
            act.wait_ge(carried_out, 16)

        @block.tensor
        def _(pe):
            for g in range(HI // 8):
                pe.wait_ge(over_ready, g + 1)
                for j in range(8):
                    h = 8 * g + j
                    last = pe.matmul(target_ps[:, 0:H], over[:, g % 2, j, :], node[:, h, 20:24],
                                     start=(h == 0), stop=(h == HI - 1))
                last.then_inc(over_used, 1)
            pe.wait_ge(ends_ready, 1)
            for a in range(3):
                last = pe.transpose(ends_ps[0:CPAD, a * P:(a + 1) * P], ends[:, a, :], m["ident"][:, :])
            last.then_inc(ends_T, 1)
            pe.wait_ge(run_ready, 1)
            for a in range(2):
                last = pe.transpose(back_ps[:, a * CPAD:(a + 1) * CPAD], runT[:, a, 0:P], m["ident"][0:CPAD, 0:CPAD])
            last.then_inc(run_T, 1)

        @block.vector
        def _(dve):
            own = Steps(dve, s_dve)
            own.link(dve.tensor_tensor(end[:, :], start[:, :], degree[:, :], ALU.add))
            own.link(dve.tensor_scalar(empty[:, :], degree[:, :], 0.0, FAR, ALU.is_equal, ALU.mult))
            own.link(dve.tensor_tensor(first_place[:, :], start[:, :], empty[:, :], ALU.add))
            own.do(dve.memset(carry[:, :], 0.0))
            own.link(dve.memset(first_row[:, :, :], 0.0))
            own.do(dve.memset(carry[:, 0:H], -BIG))
            own.do(dve.memset(top[:, :, 0:1], -BIG))
            own.do(dve.memset(any_first[:, :], 0.0))
            own.link(dve.memset(first_row[:, :, 0:1], 1.0))
            own.link(dve.tensor_copy(first_row[:, :, 1:1 + H], node[:, :, 20:24]))
            dve.nop(nofuse=True).then_inc(firsts_ready, 1)
            dve.wait_ge(s_bounds, 1)
            for g in range(HI // 8):
                if g >= 2:
                    dve.wait_ge(over_used, g - 1)
                shape = [P, 8, P]
                cols = slice(8 * g, 8 * g + 8)
                b = bounds[:, :].unsqueeze(1).to_broadcast(shape)
                o = over[:, g % 2, :, :]
                tmp = feats[:, 0:8, :]
                own.do(dve.tensor_tensor(o, b, start[:, cols].unsqueeze(2).to_broadcast(shape), ALU.is_gt))
                own.link(dve.tensor_tensor(tmp, b, end[:, cols].unsqueeze(2).to_broadcast(shape), ALU.is_lt))
                own.do(dve.tensor_tensor(o, o, tmp, ALU.mult))
                own.wait()
                dve.nop(nofuse=True).then_inc(over_ready, 1)
            dve.wait_ge(over_used, HI // 8)
            own.link(dve.tensor_copy(target_in[:, :], target_ps[:, 0:H]))
            dve.sem_inc(consumed, 1)

            def turn(i):
                for q in range(2):
                    n = 2 * i + q
                    first = firsts[:, q, :, :].rearrange("p t c -> p c t")
                    row = rows[:, q, :, :].rearrange("p t c -> p c t")
                    st = state[:, q, :, :].rearrange("p t c -> p c t")
                    flat = lambda ap, k: ap[:, k:k + 1, :].rearrange("p o t -> p (o t)")
                    dve.wait_ge(firsts_in[q], 16 * (i + 1))
                    own.do(dve.tensor_scalar(inside[:, :], flat(first, 0), -1.0, 1.0, ALU.mult, ALU.add))
                    own.do(dve.tensor_scalar(reset[:, :], flat(first, 0), -BIG, None, ALU.mult))
                    own.link(dve.reduce_max(some[:, :], flat(first, 0), AX.X))
                    own.do(dve.tensor_tensor(any_first[:, :], any_first[:, :], some[:, :], ALU.max))
                    for h in range(H):
                        own.do(dve.tensor_tensor_scan(target[:, h, :], inside[:, :], flat(first, 1 + h),
                                                      target_in[:, h:h + 1], ALU.mult, ALU.add))
                    own.wait()
                    own.link(dve.tensor_copy(target_in[:, :], target[:, :, CHUNK - 1:CHUNK].rearrange("p h o -> p (h o)")))
                    dve.wait_ge(gathered[q], 16 * CHUNK * (i + 1))
                    own.link(dve.tensor_tensor(score[:, :, :], row[:, 16:20, :], target[:, :, :], ALU.add))
                    own.link(dve.scalar_tensor_tensor(leaky[:, :, :], score[:, :, :], 0.2, score[:, :, :],
                                                      ALU.mult, ALU.max))
                    for h in range(H):
                        own.do(dve.tensor_tensor_scan(top[:, h, 1:], reset[:, :], leaky[:, h, :], top[:, h, 0:1],
                                                      ALU.add, ALU.max))
                    own.wait()
                    own.link(dve.tensor_tensor(keep[:, :, :], top[:, :, 0:CHUNK], top[:, :, 1:], ALU.subtract))
                    dve.tensor_scalar(keep[:, :, :], keep[:, :, :], 0.0, None, ALU.min).then_inc(exp_in, 1)
                    dve.tensor_tensor(weight[:, :, :], leaky[:, :, :], top[:, :, 1:], ALU.subtract).then_inc(exp_in, 1)
                    dve.wait_ge(exp_out, 2 * n + 1)
                    own.do(dve.tensor_tensor(keep[:, :, :], keep[:, :, :],
                                             inside[:, :].unsqueeze(1).to_broadcast([P, H, CHUNK]), ALU.mult))
                    dve.wait_ge(exp_out, 2 * n + 2)
                    own.link(dve.tensor_tensor(
                        feats[:, :, :].rearrange("p (h e) t -> p h e t", h=H),
                        row[:, 0:16, :].rearrange("p (h e) t -> p h e t", h=H),
                        weight[:, :, :].unsqueeze(2).to_broadcast([P, H, 4, CHUNK]), ALU.mult))
                    wait(dve, stored[q], 16 * i)
                    for k in range(16):
                        own.do(dve.tensor_tensor_scan(flat(st, H + k), keep[:, k // 4, :], feats[:, k, :],
                                                      carry[:, H + k:H + k + 1], ALU.mult, ALU.add))
                    for h in range(H):
                        own.do(dve.tensor_tensor_scan(flat(st, 20 + h), keep[:, h, :], weight[:, h, :],
                                                      carry[:, 20 + h:21 + h], ALU.mult, ALU.add))
                    own.link(dve.tensor_copy(st[:, 0:H, :], top[:, :, 1:]))
                    dve.tensor_copy(carry[:, :], state[:, q, CHUNK - 1, :]).then_inc(state_ready, 1)
                    own.link(dve.tensor_copy(top[:, :, 0:1], top[:, :, CHUNK:CHUNK + 1]))
                    dve.wait_ge(state_ready, n + 1)
                    dve.sem_inc(consumed, 1)
            turns(dve, TURNS, turn, own, EDGE_LINKS)
            K = COLS // CHUNK
            own.link(dve.memset(ends[:, :, :], 0.0))
            own.do(dve.tensor_copy(ends[:, 0, 0:20], carry[:, H:24]))
            own.do(dve.tensor_copy(ends[:, 1, 0:16].rearrange("p (h e) -> p h e", h=H),
                                   carry[:, 0:H].unsqueeze(2).to_broadcast([P, H, 4])))
            own.do(dve.tensor_copy(ends[:, 1, 16:20], carry[:, 0:H]))
            own.link(dve.tensor_copy(ends[:, 2, :], any_first[:, :].to_broadcast([P, CPAD])))
            dve.nop(nofuse=True).then_inc(ends_ready, 1)
            own.do(dve.memset(runT[:, 0, 0:1], 0.0))
            own.do(dve.memset(runT[:, 1, 0:1], -BIG))
            dve.wait_ge(ends_T, 1)
            own.link(dve.tensor_copy(endsT[:, :, :].rearrange("c a p -> c (a p)"), ends_ps[0:CPAD, 0:3 * P]))
            own.do(dve.tensor_scalar(insideT[:, :], endsT[:, 2, :], -1.0, 1.0, ALU.mult, ALU.add))
            own.link(dve.tensor_scalar(resetT[:, :], endsT[:, 2, :], -BIG, None, ALU.mult))
            own.link(dve.tensor_tensor_scan(runT[:, 1, 1:], resetT[:, :], endsT[:, 1, :], -BIG, ALU.add, ALU.max))
            own.link(dve.tensor_tensor(keepT[:, :], runT[:, 1, 0:P], runT[:, 1, 1:], ALU.subtract))
            dve.tensor_scalar(keepT[:, :], keepT[:, :], 0.0, None, ALU.min).then_inc(exp_in, 1)
            dve.tensor_tensor(weightT[:, :], endsT[:, 1, :], runT[:, 1, 1:], ALU.subtract).then_inc(exp_in, 1)
            dve.wait_ge(exp_out, 2 * K + 2)
            own.do(dve.tensor_tensor(keepT[:, :], keepT[:, :], insideT[:, :], ALU.mult))
            own.link(dve.tensor_tensor(weightT[:, :], weightT[:, :], endsT[:, 0, :], ALU.mult))
            own.link(dve.tensor_tensor_scan(runT[:, 0, 1:], keepT[:, :], weightT[:, :], 0.0, ALU.mult, ALU.add))
            dve.nop(nofuse=True).then_inc(run_ready, 1)
            dve.wait_ge(run_T, 1)
            dve.tensor_copy(carried[:, :, :].rearrange("p a c -> p (a c)"), back_ps[:, 0:2 * CPAD])\
                .then_inc(carried_ready, 1)

def node_gates(nc, io, m):
    sb, ps, sem = m["sb"], m["ps"], m["sem"]
    node, start, degree, gate = m["node"], m["start"], m["degree"], m["gate"]
    H, E = 4, 4
    with ExitStack() as c:
        last_place, last_part = sb("last_place", [P, HI], I32, c), sb("last_part", [P, HI], I32, c)
        state, carried = sb("node_state", [P, HI, NCH], F32, c), sb("node_carried", [P, HI, 2 * CPAD], F32, c)
        some, crossing, edge = (sb(n, [P, HI], F32, c) for n in ("has_edges", "crossing", "edge_place"))
        own_score, m_here, m_carried, m_all, tmp = (sb(n, [P, HI, H], F32, c) for n in
                                                    ("own_score", "m_here", "m_carried", "m_all", "tmp_heads"))
        weights = sb("part_weights", [P, 3, HI, H], F32, c)
        sums, tmp16 = sb("sums", [P, HI, 16], F32, c), sb("tmp16", [P, HI, 16], F32, c)
        denom = sb("denom", [P, HI, H], F32, c)
        mean, var, std = (sb(n, [P, HI], F32, c) for n in ("mean16", "var16", "std16"))
        gat = sb("gat_rows", [P, 3, 16], F32, c)
        scores, coded, first, second = (sb(n, [P, HI, E], F32, c) for n in ("scores", "coded", "first", "second"))
        rank = sb("rank", [P, E], F32, c)
        best, next_best, odds, denom2 = (sb(n, [P, HI], F32, c) for n in ("best", "next_best", "odds", "denom2"))
        eps = sb("eps_gat", [P, 1], F32, c)
        s_dve, places, s_rows, s_carried, s_gat, s_rank, exp_in, exp_out, var_ready, std_ready = (
            sem(n, c) for n in ("gate_chain", "places_ready", "state_gathered", "carried_gathered", "gat_in",
                                "rank_ready", "gate_exp_in", "gate_exp_out", "var16_ready", "std16_ready"))
        c.callback(m["clear"])
        block = c.enter_context(nc.Block())

        @block.gpsimd
        def _(pool):
            pool.iota(rank[:, :], [[-1, E]], base=E, channel_multiplier=0,
                      allow_small_or_imprecise_dtypes=True).then_inc(s_rank, 1)
            pool.wait_ge(places, 1)
            for h in range(HI):
                pool.indirect_dma_start(
                    out=state[:, h, :], out_offset=None, in_=m["running"],
                    in_offset=bass.IndirectOffsetOnAxis(ap=last_place[:, h:h + 1], axis=0)).then_inc(s_rows, 16)
                pool.indirect_dma_start(
                    out=carried[:, h, :], out_offset=None, in_=m["carried_in"],
                    in_offset=bass.IndirectOffsetOnAxis(ap=last_part[:, h:h + 1], axis=0)).then_inc(s_carried, 16)

        @block.sync
        def _(sp):
            sp.dma_start(gat[:, :, :], io["gat_rows"]).then_inc(s_gat, 16)

        @block.scalar
        def _(act):
            act.wait_ge(exp_in, 1)
            act.activation(weights[:, :, :, :], weights[:, :, :, :], ACT.Exp).then_inc(exp_out, 1)
            act.wait_ge(var_ready, 1)
            act.activation(std[:, :], var[:, :], ACT.Sqrt, bias=eps[:, :], scale=1.0 / 16).then_inc(std_ready, 1)
            act.wait_ge(exp_in, 2)
            act.activation(odds[:, :], odds[:, :], ACT.Exp).then_inc(exp_out, 1)

        @block.vector
        def _(dve):
            own = Steps(dve, s_dve)
            tt = lambda out, a, b, op: own.link(dve.tensor_tensor(out, a, b, op))
            ts = lambda out, a, s1, s2, op0, op1=None: own.link(
                dve.tensor_scalar(out, a, s1, s2, op0, op1) if op1 is not None else dve.tensor_scalar(out, a, s1, s2, op0))
            over_heads = lambda ap: ap.unsqueeze(2).to_broadcast([P, HI, H])
            by_head = lambda ap: ap.unsqueeze(3).to_broadcast([P, HI, H, 4])
            split = lambda ap: ap.rearrange("p n (h e) -> p n h e", h=H)
            own.link(dve.memset(eps[:, :], 1e-5))
            tt(edge[:, :], start[:, :], degree[:, :], ALU.add)
            ts(edge[:, :], edge[:, :], -1.0, 0.0, ALU.add, ALU.max)
            own.link(dve.tensor_copy(last_place[:, :], edge[:, :]))
            ts(last_part[:, :], last_place[:, :], COLS.bit_length() - 1, None, ALU.arith_shift_right)
            dve.nop(nofuse=True).then_inc(places, 1)
            ts(some[:, :], degree[:, :], 0.0, None, ALU.is_gt)
            ts(crossing[:, :], last_part[:, :], float(COLS), None, ALU.mult)
            tt(crossing[:, :], crossing[:, :], start[:, :], ALU.is_gt)
            tt(crossing[:, :], crossing[:, :], some[:, :], ALU.mult)
            tt(own_score[:, :, :], node[:, :, 16:20], node[:, :, 20:24], ALU.add)
            own.link(dve.scalar_tensor_tensor(own_score[:, :, :], own_score[:, :, :], 0.2, own_score[:, :, :],
                                              ALU.mult, ALU.max))
            dve.wait_ge(s_rows, 16 * HI)
            dve.wait_ge(s_carried, 16 * HI)
            for out, mask, part in ((m_here, some, state[:, :, 0:H]),
                                    (m_carried, crossing, carried[:, :, CPAD + 16:CPAD + 20])):
                tt(out[:, :, :], part, over_heads(mask[:, :]), ALU.mult)
                ts(tmp[:, :, :], over_heads(mask[:, :]), -1.0, BIG, ALU.add, ALU.mult)
                tt(out[:, :, :], out[:, :, :], tmp[:, :, :], ALU.add)
            tt(m_all[:, :, :], m_here[:, :, :], m_carried[:, :, :], ALU.max)
            tt(m_all[:, :, :], m_all[:, :, :], own_score[:, :, :], ALU.max)
            for a, part in enumerate((m_here, m_carried, own_score)):
                tt(weights[:, a, :, :], part[:, :, :], m_all[:, :, :], ALU.subtract)
            dve.nop(nofuse=True).then_inc(exp_in, 1)
            dve.wait_ge(exp_out, 1)
            tt(weights[:, 0, :, :], weights[:, 0, :, :], over_heads(some[:, :]), ALU.mult)
            tt(weights[:, 1, :, :], weights[:, 1, :, :], over_heads(crossing[:, :]), ALU.mult)
            tt(split(sums[:, :, :]), split(node[:, :, 0:16]), by_head(weights[:, 2, :, :]), ALU.mult)
            own.link(dve.tensor_copy(denom[:, :, :], weights[:, 2, :, :]))
            for a, s16, s4 in ((0, state[:, :, 4:20], state[:, :, 20:24]), (1, carried[:, :, 0:16], carried[:, :, 16:20])):
                tt(split(tmp16[:, :, :]), split(s16), by_head(weights[:, a, :, :]), ALU.mult)
                tt(sums[:, :, :], sums[:, :, :], tmp16[:, :, :], ALU.add)
                tt(tmp[:, :, :], s4, weights[:, a, :, :], ALU.mult)
                tt(denom[:, :, :], denom[:, :, :], tmp[:, :, :], ALU.add)
            ts(denom[:, :, :], denom[:, :, :], 1e-16, None, ALU.add)
            own.link(dve.reciprocal(denom[:, :, :], denom[:, :, :]))
            tt(split(sums[:, :, :]), split(sums[:, :, :]), by_head(denom[:, :, :]), ALU.mult)
            row = lambda a: gat[:, a, :].unsqueeze(1).to_broadcast([P, HI, 16])
            over16 = lambda ap: ap.unsqueeze(2).to_broadcast([P, HI, 16])
            dve.wait_ge(s_gat, 16)
            tt(sums[:, :, :], sums[:, :, :], row(0), ALU.add)
            own.link(dve.tensor_reduce(mean[:, :], sums[:, :, :], AX.X, ALU.add))
            ts(mean[:, :], mean[:, :], 1.0 / 16, None, ALU.mult)
            tt(sums[:, :, :], sums[:, :, :], over16(mean[:, :]), ALU.subtract)
            tt(tmp16[:, :, :], sums[:, :, :], sums[:, :, :], ALU.mult)
            own.link(dve.tensor_reduce(var[:, :], tmp16[:, :, :], AX.X, ALU.add))
            dve.nop(nofuse=True).then_inc(var_ready, 1)
            dve.wait_ge(std_ready, 1)
            own.link(dve.reciprocal(std[:, :], std[:, :]))
            tt(sums[:, :, :], sums[:, :, :], over16(std[:, :]), ALU.mult)
            tt(sums[:, :, :], sums[:, :, :], row(1), ALU.mult)
            tt(sums[:, :, :], sums[:, :, :], row(2), ALU.add)
            own.link(dve.tensor_reduce(scores[:, :, :], sums[:, :, :].rearrange("p n (h e) -> p n e h", h=H), AX.X, ALU.add))
            ts(scores[:, :, :], scores[:, :, :], 1.0 / H, None, ALU.mult)
            dve.wait_ge(s_rank, 1)
            over_e = lambda ap: ap.unsqueeze(2).to_broadcast([P, HI, E])

            def take_best(value, hot):
                own.link(dve.tensor_reduce(value[:, :], scores[:, :, :], AX.X, ALU.max))
                tt(coded[:, :, :], scores[:, :, :], over_e(value[:, :]), ALU.is_equal)
                tt(coded[:, :, :], coded[:, :, :], rank[:, :].unsqueeze(1).to_broadcast([P, HI, E]), ALU.mult)
                own.link(dve.tensor_reduce(denom2[:, :], coded[:, :, :], AX.X, ALU.max))
                tt(hot[:, :, :], coded[:, :, :], over_e(denom2[:, :]), ALU.is_equal)

            take_best(best, first)
            own.link(dve.scalar_tensor_tensor(scores[:, :, :], first[:, :, :], -BIG, scores[:, :, :], ALU.mult, ALU.add))
            take_best(next_best, second)
            tt(odds[:, :], next_best[:, :], best[:, :], ALU.subtract)
            dve.nop(nofuse=True).then_inc(exp_in, 1)
            dve.wait_ge(exp_out, 2)
            ts(denom2[:, :], odds[:, :], 1.0, None, ALU.add)
            own.link(dve.reciprocal(denom2[:, :], denom2[:, :]))
            tt(odds[:, :], odds[:, :], denom2[:, :], ALU.mult)
            tt(first[:, :, :], first[:, :, :], over_e(denom2[:, :]), ALU.mult)
            tt(second[:, :, :], second[:, :, :], over_e(odds[:, :]), ALU.mult)
            tt(gate[:, :, :], first[:, :, :], second[:, :, :], ALU.add)


def later_layers(nc, io, m):
    sb, ps, sem = m["sb"], m["ps"], m["sem"]
    ident, ones, gate, x_all = m["ident"], m["ones"], m["gate"], m["x_all"]
    HEADS, TOP, KEYS, RING, HALF = 8, 16, 128, 32, 8
    MHA_HEADS, HID, EXP0, EXP2 = 8, 2 * D, 4, 8
    with ExitStack() as c:
        def tiles(names, shape, dt=F32):
            return [sb(n, shape, dt, c) for n in names.split()]

        moe0_w1, moe0_w2 = sb("moe0_w1", [P, EXP0, HID], F32, c), sb("moe0_w2", [P, EXP0, 2, D], F32, c)
        moe0_b1, moe0_b2 = sb("moe0_b1", [P, EXP0 * 2], F32, c), sb("moe0_b2", [1, EXP0 * D], F32, c)
        wq, wk, wv, wo = tiles("mha_wq mha_wk mha_wv mha_wo", [P, D])
        edge_w = sb("edge_w", [P, MHA_HEADS * P], F32, c)
        w_e = sb("w_e", [P, MHA_HEADS], F32, c)
        head_mask = sb("head_mask", [P, MHA_HEADS], F32, c)
        wi, ws = sb("route_wi", [P, HID], F32, c), sb("route_ws", [P, 4, HID], F32, c)
        bi, bs = sb("route_bi", [P, 2], F32, c), sb("route_bs", [P, 4], F32, c)
        w_out, b_out = sb("route_wo", [P, 2, D], F32, c), sb("route_bo", [1, D], F32, c)
        routed = sb("routed", [P, 4, HID + 1], F32, c)
        routed_rows = sb("routed_rows", [P, B, 4], I32, c)
        routed_index = sb("routed_index", [P, 4], I32, c)
        gcn_w, gcn_b, alpha = sb("gcn_w", [P, D], F32, c), sb("gcn_b", [P, D], F32, c), sb("alpha", [P, 1], F32, c)
        moe2_w1, moe2_w2 = sb("moe2_w1", [P, EXP2, HID], F32, c), sb("moe2_w2", [P, EXP2, 2, D], F32, c)
        moe2_b1, moe2_b2 = sb("moe2_b1", [P, EXP2 * 2], F32, c), sb("moe2_b2", [1, EXP2 * D], F32, c)
        gamma, beta = tiles("gamma beta", [P, D])
        wr, br = sb("moe2_wr", [P, EXP2], F32, c), sb("moe2_br", [1, EXP2], F32, c)
        gin_w1, gin_w2 = sb("gin_w1", [P, HID], F32, c), sb("gin_w2", [P, 2, D], F32, c)
        gin_b1, gin_b2 = sb("gin_b1", [P, 2], F32, c), sb("gin_b2", [1, D], F32, c)
        eps_gin, eps1_ident = sb("eps_gin", [P, 1], F32, c), sb("eps1_ident", [P, P], F32, c)
        w_sim = sb("w_sim", [P, 4, 4 * KEYS], F32, c)
        mem_wq, mem_wo = sb("mem_wq", [P, HEADS * D], F32, c), sb("mem_wo", [P, HEADS, D], F32, c)
        causal = sb("causal", [P, P], F32, c)
        count16 = sb("count16", [P, TOP], F32, c)
        eps_ln = sb("eps_ln", [P, 1], F32, c)
        s_const, s_made, s_folded, s_weights, s_simple = (sem(n, c) for n in (
            "const4", "made4", "folded4", "weights4", "setup4"))

        loads = [(moe0_w1, "moe0_w1"), (moe0_w2, "moe0_w2"), (moe0_b1, "moe0_b1"), (moe0_b2, "moe0_b2"),
                 (wq, "mha_wq"), (wk, "mha_wk"), (wv, "mha_wv"), (wo, "mha_wo"), (w_e, "w_e"),
                 (wi, "route_wi"), (ws, "route_ws"), (bi, "route_bi"), (bs, "route_bs"),
                 (w_out, "route_wo"), (b_out, "route_bo"), (gcn_w, "gcn_w"), (gcn_b, "gcn_b"), (alpha, "alpha"),
                 (moe2_w1, "moe2_w1"), (moe2_w2, "moe2_w2"), (moe2_b1, "moe2_b1"), (moe2_b2, "moe2_b2"),
                 (gamma, "gamma"), (beta, "beta"), (wr, "moe2_wr"), (br, "moe2_br"),
                 (gin_w1, "gin_w1"), (gin_w2, "gin_w2"), (gin_b1, "gin_b1"), (gin_b2, "gin_b2"),
                 (eps_gin, "eps_gin"), (mem_wq, "mem_wq"), (mem_wo, "mem_wo")]

        with ExitStack() as c2:
            wqT, keysT = sb("wqT", [64, 16, P], F32, c2), sb("keysT", [64, 16, KEYS], F32, c2)
            route = sb("route", [P, B], I32, c2)
            route_f, bad = sb("route_f", [P, B], F32, c2), sb("bad", [P, B], F32, c2)
            row_base = sb("row_base", [P, 4], F32, c2)
            rows_f = sb("rows_f", [P, B, 4], F32, c2)
            fold_ps = [ps(f"fold_ps{j}", [P, 4 * KEYS], F32, c2) for j in range(4)]
            block = c2.enter_context(nc.Block())

            @block.sync
            def _(sp):
                for dst, name in loads + [(wqT, "wqT"), (keysT, "keysT"), (route, "route")]:
                    sp.dma_start(dst[tuple([slice(None)] * len(dst.shape))], io[name]).then_inc(s_weights, 16)
                sp.wait_ge(s_weights, 16 * (len(loads) + 3))

            @block.gpsimd
            def _(pool):
                pool.memset(causal[:, :], 0.0).then_inc(s_const, 1)
                pool.iota(count16[:, :], [[1, TOP]], base=0, channel_multiplier=0,
                          allow_small_or_imprecise_dtypes=True).then_inc(s_const, 1)
                pool.iota(row_base[:, :], [[17 * HID, 2], [P, 2]], base=0, channel_multiplier=1,
                          allow_small_or_imprecise_dtypes=True).then_inc(s_const, 1)
                pool.wait_ge(s_const, 3)
                pool.affine_select(out=causal[:, :], in_=causal[:, :], compare_op=ALU.is_ge, fill=-BIG, base=0,
                                   pattern=[[-1, P]], channel_multiplier=1).then_inc(s_const, 1)
                pool.affine_select(out=head_mask[:, :], in_=ones[:, 0:MHA_HEADS], compare_op=ALU.is_ge, fill=0.0,
                                   base=0, pattern=[[-16, MHA_HEADS]], channel_multiplier=1).then_inc(s_const, 1)
                pool.wait_ge(s_const, 5)
                pool.affine_select(out=head_mask[:, :], in_=head_mask[:, :], compare_op=ALU.is_ge, fill=0.0,
                                   base=15, pattern=[[16, MHA_HEADS]], channel_multiplier=-1).then_inc(s_const, 1)
                pool.wait_ge(s_const, 6)

            @block.tensor
            def _(pe):
                pe.wait_ge(s_weights, 16 * (len(loads) + 3))
                for j in range(16):
                    last = pe.matmul(fold_ps[j // 4][:, (j % 4) * KEYS:(j % 4 + 1) * KEYS], wqT[:, j, :], keysT[:, j, :],
                                     start=True, stop=True)
                last.then_inc(s_folded, 1)

            @block.vector
            def _(dve):
                own = Steps(dve, s_simple)
                own.do(dve.memset(eps_ln[:, :], 1e-5))
                dve.wait_ge(s_weights, 16 * (len(loads) + 3))
                own.do(dve.tensor_tensor(edge_w[:, :].rearrange("p (h j) -> p h j", h=MHA_HEADS),
                                         ident[:, :].unsqueeze(1).to_broadcast([P, MHA_HEADS, P]),
                                         w_e[:, :].unsqueeze(2).to_broadcast([P, MHA_HEADS, P]), ALU.mult))
                own.link(dve.tensor_scalar(eps_gin[:, :], eps_gin[:, :], 1.0, None, ALU.add))
                own.do(dve.tensor_scalar(eps1_ident[:, :], ident[:, :], eps_gin[:, :], None, ALU.mult))
                own.link(dve.tensor_scalar(bad[:, :], route[:, :], 0.0, 1.0e9, ALU.is_lt, ALU.mult))
                own.link(dve.tensor_tensor(route_f[:, :], route[:, :], bad[:, :], ALU.add))
                own.link(dve.tensor_scalar(route_f[:, :], route_f[:, :], 16.0, float(HID), ALU.min, ALU.mult))
                dve.wait_ge(s_const, 6)
                own.link(dve.tensor_tensor(routed_rows[:, :, :], route_f[:, :].unsqueeze(2).to_broadcast([P, B, 4]),
                                           row_base[:, :].unsqueeze(1).to_broadcast([P, B, 4]), ALU.add))
                dve.wait_ge(s_folded, 1)
                for j in range(4):
                    own.link(dve.tensor_copy(w_sim[:, j, :], fold_ps[j][:, :]))

        x, z, zn, zT, xo, x_cur, zH, adjT = tiles("x z zn zT xo x_cur zH adjT", [P, D])
        stats, mv = sb("stats", [P, 6], F32, c), sb("mv", [P, 2], F32, c)
        std, rstd, row_sum, row_std, row_scale = tiles("std rstd row_sum row_std row_scale", [P, 1])
        hT = sb("hT", [P, 2, HID], F32, c)
        qT, v_mha, o_mha, oT = tiles("qT v_mha o_mha oT", [P, D])
        k_heads = sb("k_heads", [P, MHA_HEADS * P], F32, c)
        absent = sb("absent_edges", [P, P], F32, c)
        neg_max, sums, inv = tiles("neg_max sums inv", [P, MHA_HEADS])
        e_mha, eT_mha = tiles("e_mha eT_mha", [P, MHA_HEADS * P])
        h_a, h_b = tiles("h_a h_b", [P, HID])
        bias_sum = sb("bias_sum", [P, 4], F32, c)
        za = sb("za", [P, D], F32, c)
        aT = sb("aT", [P, D], F32, c)
        relu_in = sb("relu_in", [P, D], F32, c)
        logits, top8, w_exp, hot = tiles("logits top8 w_exp hot", [P, EXP2])
        top8_i = sb("top8_i", [P, EXP2], mybir.dt.uint32, c)
        top8_f = sb("top8_f", [P, EXP2], F32, c)
        odds, w_best, w_next = tiles("odds4 w_best w_next", [P, 1])
        vals = sb("vals", [P, 4, TOP], F32, c)
        vals_i = sb("vals_i", [P, 4, TOP], mybir.dt.uint32, c)
        vals_f = sb("vals_f", [P, 4, TOP], F32, c)
        rest = sb("rest", [P, 4 * KEYS], F32, c)
        pair_sum, pair_rest = tiles("pair_sum pair_rest", [P, 2 * TOP * TOP])
        best = sb("best16", [P, 2, TOP], F32, c)
        best_i = sb("best_i", [P, 2, TOP], mybir.dt.uint32, c)
        digit = sb("digit", [P, 2, TOP], mybir.dt.uint32, c)
        digit_f = sb("digit_f", [P, 2, TOP], F32, c)
        found = sb("found", [P, 2, 2, TOP], F32, c)
        soft, soft_sum = sb("soft", [P, 2, TOP], F32, c), sb("soft_sum", [P, 2], F32, c)
        index_next, index = sb("index_next", [P, HEADS * TOP], I32, c), sb("index4", [P, HEADS * TOP], I32, c)
        mem_w_next, mem_w = tiles("mem_w_next mem_w", [P, HEADS * TOP])
        ring = sb("ring", [P, RING, 2 * D], F32, c)
        diag = sb("diag", [P, 2, HALF * P], F32, c)
        kT, v_mem, qT_mem, masked, e_mem, eT_mem, oT_mem = tiles("kT v_mem qT_mem masked e_mem eT_mem oT_mem", [P, D])
        m_mem, sum_mem, inv_mem = tiles("m_mem sum_mem inv_mem", [P, 1])
        small = ps("small4", [P, 512], F32, c)
        wide = [ps(f"wide{j}", [P, 512], F32, c) for j in range(4)]
        att_ps, kT_ps, v_ps = ps("att_ps", [P, 512], F32, c), ps("kT_ps", [P, 512], F32, c), ps("v_ps", [P, 512], F32, c)
        zT_ps, y_ps, aT_ps, misc_ps = (small[:, j * D:(j + 1) * D] for j in range(4))

        names = ("adj_in var std z zT_made zT h_made h_ready y_made y_used qkv_made q_v_ready k_ready scores_made "
                 "max_ready exp_ready eT_made eT_act eT_dve o_made o_ready oT_made oT_ready y "
                 "route_h route_relu route_bias row_sum_made row_sum_ready row_std_ready conv_z conv_made conv_ready "
                 "logits_made odds_in odds_out gin_h gin_relu sims_made soft_in soft_out chosen index_taken "
                 "weights_taken zH_ready diag_ready diag_used rows_used kv_ready q_made q_ready sim_made sim_max "
                 "exp_mem eT_mem_made eT_mem_ready out_made out_ready y_mem acc_made stored out_tile routed_in "
                 "routed_used routed_copied index_copied gelu_done own act_own")
        S = {n: sem("l_" + n, c) for n in names.split()}
        rows_in = [sem(f"rows_in{j}", c) for j in range(4)]
        block = c.enter_context(nc.Block())

        def run(eng, body, own=None, links=0):
            turns(eng, B, lambda b: body(b, True, not isinstance(b, int) or b > 0), own, links, peeled=2)
            body(B, False, True)

        @block.sync
        def _(sp):
            def body(b, front, back):
                if front:
                    wait(sp, S["conv_made"], 2 * b)
                    sp.dma_start(adjT[:, :], io["adjT"][bass.ds(b, 1), :, :].rearrange("o n d -> (o n) d"))\
                        .then_inc(S["adj_in"], 16)
                if back:
                    wait(sp, S["out_tile"], b)
                    sp.dma_start(io["out"][bass.ds(b - 1, 1), :, :].rearrange("o n d -> (o n) d"), xo[:, :])\
                        .then_inc(S["stored"], 16)
            run(sp, body)
            sp.wait_ge(S["stored"], 16 * B)

        @block.gpsimd
        def _(pool):
            def body(b, front, back):
                if front:
                    wait(pool, S["routed_used"], b)
                    pool.nop(nofuse=True)
                    pool.tensor_copy(routed_index[:, :], routed_rows[:, bass.ds(b, 1), :].rearrange("p o k -> p (o k)"))\
                        .then_inc(S["routed_copied"], 1)
                    wait(pool, S["routed_copied"], b + 1)
                    pool.nop(nofuse=True)
                    for k in range(4):
                        pool.indirect_dma_start(
                            out=routed[:, k, :], out_offset=None, in_=io["route_wr"],
                            in_offset=bass.IndirectOffsetOnAxis(ap=routed_index[:, k:k + 1], axis=0))\
                            .then_inc(S["routed_in"], 16)
                if back:
                    wait(pool, S["chosen"], b)
                    for j in range(4):
                        wait(pool, rows_in[j], 16 * TOP * 2 * (b - 1))
                    pool.nop(nofuse=True)
                    pool.tensor_copy(index[:, :], index_next[:, :]).then_inc(S["index_copied"], 1)
                    wait(pool, S["index_copied"], b)
                    pool.nop(nofuse=True)
                    for h in range(HEADS):
                        n = HEADS * (b - 1) + h
                        wait(pool, S["rows_used"], n - 1)
                        pool.nop(nofuse=True)
                        for k in range(TOP):
                            pool.indirect_dma_start(
                                out=ring[:, (h % 2) * TOP + k, :], out_offset=None, in_=io["memory"],
                                in_offset=bass.IndirectOffsetOnAxis(ap=index[:, h * TOP + k:h * TOP + k + 1], axis=0))\
                                .then_inc(rows_in[h % 4], 16)
            run(pool, body)

        @block.tensor
        def _(pe):
            def transpose_z(b, u, z_use, src):
                wait(pe, S["z"], 8 * b + z_use + 1)
                pe.transpose(zT_ps, src[:, :], ident[:, :]).then_inc(S["zT_made"], 1)
                wait(pe, S["zT"], 5 * b + u + 1)

            def bias_row(out, row):
                return pe.matmul(out, ones[0:1, :], row, start=False, stop=True)

            def experts(b, first, count, w1, w2, b2):
                def hidden(e):
                    n = 12 * b + first + e
                    wait(pe, S["gelu_done"], n - 1)
                    for half in range(2):
                        last = pe.matmul(wide[e % 2][:, half * D:(half + 1) * D], w1[:, e, half * D:(half + 1) * D],
                                         zT[:, :], start=True, stop=True)
                    last.then_inc(S["h_made"], 1)

                def output(e):
                    n = 12 * b + first + e
                    wait(pe, S["gelu_done"], n + 1)
                    wait(pe, S["y_used"], n - 1)
                    y = wide[2 + e % 2][:, 0:D]
                    for half in range(2):
                        pe.matmul(y, hT[:, e % 2, half * D:(half + 1) * D], w2[:, e, half, :],
                                  start=(half == 0), stop=False)
                    bias_row(y, b2[:, e * D:(e + 1) * D]).then_inc(S["y_made"], 1)

                hidden(0)
                for e in range(count):
                    if e + 1 < count:
                        hidden(e + 1)
                    output(e)

            def mha(b):
                wait(pe, S["adj_in"], 16 * (b + 1))
                transpose_z(b, 1, 1, z)
                for j, (l, r) in enumerate(((wq, zT), (wk, zT), (zT, wv))):
                    out = wide[1][:, 0:D] if j == 1 else wide[0][:, j * D:(j + 1) * D]
                    last = pe.matmul(out, l[:, :], r[:, :], start=True, stop=True)
                last.then_inc(S["qkv_made"], 1)
                wait(pe, S["q_v_ready"], b + 1)
                wait(pe, S["k_ready"], b + 1)
                for j in range(2):
                    half = slice(j * 4 * P, (j + 1) * 4 * P)
                    pe.matmul(wide[2 + j][:, :], qT[:, :], k_heads[:, half], start=True, stop=False)
                    pe.matmul(wide[2 + j][:, :], adjT[:, :], edge_w[:, half], start=False, stop=False)
                    pe.matmul(wide[2 + j][:, :], absent[:, :], ident[:, :].unsqueeze(1).to_broadcast([P, 4, P]),
                              start=False, stop=True).then_inc(S["scores_made"], 1)
                for j in range(2):
                    wait(pe, S["exp_ready"], 2 * b + j + 1)
                    for h in range(4):
                        last = pe.transpose(wide[j][:, h * P:(h + 1) * P], e_mha[:, (4 * j + h) * P:(4 * j + h + 1) * P],
                                            ident[:, :])
                    last.then_inc(S["eT_made"], 1)
                wait(pe, S["eT_act"], b + 1)
                wait(pe, S["eT_dve"], b + 1)
                for h in range(MHA_HEADS):
                    last = pe.matmul(aT_ps[:, 16 * h:16 * h + 16], eT_mha[:, h * P:(h + 1) * P],
                                     v_mha[:, 16 * h:16 * h + 16], start=True, stop=True)
                last.then_inc(S["o_made"], 1)
                wait(pe, S["o_ready"], b + 1)
                pe.transpose(misc_ps, o_mha[:, :], ident[:, :]).then_inc(S["oT_made"], 1)
                wait(pe, S["oT_ready"], b + 1)
                pe.matmul(y_ps, oT[:, :], wo[:, :], start=True, stop=True).then_inc(S["y"], 1)

            def routed_ffn(b):
                transpose_z(b, 2, 2, z)
                for o in range(2):
                    last = pe.matmul(wide[0][:, o * D:(o + 1) * D], wi[:, o * D:(o + 1) * D], zT[:, :],
                                     start=True, stop=True)
                last.then_inc(S["route_h"], 1)
                wait(pe, S["routed_in"], 64 * (b + 1))
                for l in range(2):
                    h = (h_a, h_b)[l]
                    wait(pe, S["route_relu"], 3 * b + l + 1)
                    for o in range(2):
                        cols = slice(o * D, (o + 1) * D)
                        out = wide[1 + l][:, cols]
                        for k in range(2):
                            hk = h[:, k * D:(k + 1) * D]
                            pe.matmul(out, ws[:, 2 * l + k, cols], hk, start=(k == 0), stop=False)
                            pe.matmul(out, routed[:, 2 * l + k, cols], hk, start=False, stop=False)
                        last = pe.matmul(out, ident[:, :], h[:, cols], start=False, stop=True)
                    last.then_inc(S["route_h"], 1)
                wait(pe, S["route_relu"], 3 * b + 3)
                for k in range(2):
                    pe.matmul(y_ps, h_a[:, k * D:(k + 1) * D], w_out[:, k, :], start=(k == 0), stop=False)
                bias_row(y_ps, b_out[:, :]).then_inc(S["y"], 1)

            def gcn(b):
                pe.matmul(wide[3][:, 0:1], adjT[:, :], ones[:, 0:1], start=True, stop=True)\
                    .then_inc(S["row_sum_made"], 1)
                wait(pe, S["conv_z"], b + 1)
                pe.matmul(aT_ps, za[:, :], adjT[:, :], start=True, stop=False)
                pe.matmul(aT_ps, zn[:, :], ident[:, :], start=False, stop=True).then_inc(S["conv_made"], 1)
                wait(pe, S["conv_ready"], 2 * b + 1)
                pe.matmul(y_ps, aT[:, :], gcn_w[:, :], start=True, stop=True).then_inc(S["y"], 1)

            def gated_experts(b):
                transpose_z(b, 3, 5, zn)
                pe.matmul(misc_ps[:, 0:EXP2], zT[:, :], wr[:, :], start=True, stop=False)
                bias_row(misc_ps[:, 0:EXP2], br[:, :]).then_inc(S["logits_made"], 1)
                experts(b, 4, EXP2, moe2_w1, moe2_w2, moe2_b2)

            def gin(b):
                wait(pe, S["z"], 8 * b + 7)
                pe.matmul(aT_ps, z[:, :], adjT[:, :], start=True, stop=False)
                pe.matmul(aT_ps, z[:, :], eps1_ident[:, :], start=False, stop=True).then_inc(S["conv_made"], 1)
                wait(pe, S["conv_ready"], 2 * b + 2)
                for o in range(2):
                    last = pe.matmul(wide[0][:, o * D:(o + 1) * D], gin_w1[:, o * D:(o + 1) * D], aT[:, :],
                                     start=True, stop=True)
                last.then_inc(S["gin_h"], 1)
                wait(pe, S["gin_relu"], b + 1)
                for k in range(2):
                    pe.matmul(y_ps, h_a[:, k * D:(k + 1) * D], gin_w2[:, k, :], start=(k == 0), stop=False)
                bias_row(y_ps, gin_b2[:, :]).then_inc(S["y"], 1)

            def similarities(b):
                transpose_z(b, 4, 7, z)
                for j in range(4):
                    pe.matmul(wide[j][:, :], zT[:, :], w_sim[:, j, :], start=True, stop=True)\
                        .then_inc(S["sims_made"], 1)

            def gathered_products(b, h, k0, k1):
                n = HEADS * (b - 1) + h
                for k in range(k0, k1):
                    if k == 0:
                        pe.wait_ge(rows_in[h % 4], 16 * TOP * (2 * (b - 1) + h // 4 + 1))
                        wait(pe, S["kv_ready"], n)
                    if k % HALF == 0:
                        wait(pe, S["diag_ready"], 2 * n + k // HALF + 1)
                    row = ring[:, (h % 2) * TOP + k, :]
                    d = diag[:, k // HALF, (k % HALF) * P:(k % HALF + 1) * P]
                    pe.matmul(kT_ps[:, 0:D], row[:, 0:D], d, start=(k == 0), stop=(k == TOP - 1))
                    last = pe.matmul(v_ps[:, 0:D], d, row[:, D:2 * D], start=(k == 0), stop=(k == TOP - 1))
                    if k % HALF == HALF - 1:
                        last.then_inc(S["diag_used"], 1)
                if k1 == TOP:
                    pe.nop(nofuse=True)
                    wait(pe, S["diag_used"], 2 * n + 2)
                    pe.sem_inc(S["rows_used"], 1)

            def back_head(b, h):
                n = HEADS * (b - 1) + h - 1
                attend, weigh = h >= 1, h < HEADS
                if attend:
                    wait(pe, S["zH_ready"], b)
                    wait(pe, S["acc_made"], n)
                    pe.matmul(att_ps[:, 0:D], mem_wq[:, (h - 1) * D:h * D], zH[:, :], start=True, stop=True)\
                        .then_inc(S["q_made"], 1)
                if weigh:
                    gathered_products(b, h, 0, 4)
                if attend:
                    wait(pe, S["kv_ready"], n + 1)
                    wait(pe, S["q_ready"], n + 1)
                    pe.matmul(att_ps[:, D:2 * D], qT_mem[:, :], kT[:, :], start=True, stop=True)\
                        .then_inc(S["sim_made"], 1)
                if weigh:
                    gathered_products(b, h, 4, 8)
                if attend:
                    wait(pe, S["exp_mem"], n + 1)
                    pe.transpose(att_ps[:, 2 * D:3 * D], e_mem[:, :], ident[:, :]).then_inc(S["eT_mem_made"], 1)
                if weigh:
                    gathered_products(b, h, 8, 12)
                if attend:
                    wait(pe, S["eT_mem_ready"], n + 1)
                    pe.matmul(att_ps[:, 3 * D:4 * D], v_mem[:, :], eT_mem[:, :], start=True, stop=True)\
                        .then_inc(S["out_made"], 1)
                if weigh:
                    gathered_products(b, h, 12, 16)
                if attend:
                    wait(pe, S["out_ready"], n + 1)
                    pe.matmul(att_ps[:, 0:D], oT_mem[:, :], mem_wo[:, h - 1, :], start=True, stop=True)\
                        .then_inc(S["y_mem"], 1)

            def body(b, front, back):
                for s in range(HEADS + 1):
                    if front:
                        if s == 0:
                            transpose_z(b, 0, 0, z)
                            experts(b, 0, EXP0, moe0_w1, moe0_w2, moe0_b2)
                        elif s < 7:
                            (mha, routed_ffn, gcn, gated_experts, gin, similarities)[s - 1](b)
                    if back:
                        back_head(b, s)
            run(pe, body)

        @block.scalar
        def _(act):
            def std_of(b, u):
                wait(act, S["var"], 8 * b + u + 1)
                act.activation(std[:, :], mv[:, 1:2], ACT.Sqrt, bias=eps_ln[:, :]).then_inc(S["std"], 1)

            def copy_zT(b, u):
                wait(act, S["zT_made"], 5 * b + u + 1)
                act.activation(zT[:, :], zT_ps, ACT.Copy).then_inc(S["zT"], 1)

            def experts(b, first, count, b1):
                for e in range(count):
                    n = 12 * b + first + e
                    wait(act, S["h_made"], n + 1)
                    wait(act, S["y_made"], n - 1)
                    for half in range(2):
                        last = act.activation(hT[:, e % 2, half * D:(half + 1) * D],
                                              wide[e % 2][:, half * D:(half + 1) * D], ACT.Gelu,
                                              bias=b1[:, 2 * e + half:2 * e + half + 1])
                    last.then_inc(S["gelu_done"], 1)

            def mha(b):
                copy_zT(b, 1)
                wait(act, S["qkv_made"], b + 1)
                act.activation(qT[:, :], wide[0][:, 0:D], ACT.Copy, scale=0.25)
                act.activation(v_mha[:, :], wide[0][:, 2 * D:3 * D], ACT.Copy).then_inc(S["q_v_ready"], 1)
                for j in range(2):
                    wait(act, S["max_ready"], 2 * b + j + 1)
                    for h in range(4):
                        g = 4 * j + h
                        last = act.activation(e_mha[:, g * P:(g + 1) * P], wide[2 + j][:, h * P:(h + 1) * P], ACT.Exp,
                                              bias=neg_max[:, g:g + 1], accum_out=sums[:, g:g + 1])
                    last.then_inc(S["exp_ready"], 1)
                wait(act, S["eT_made"], 2 * b + 1)
                act.activation(eT_mha[:, 0:4 * P], wide[0][:, :], ACT.Copy).then_inc(S["eT_act"], 1)
                wait(act, S["oT_made"], b + 1)
                act.activation(oT[:, :], misc_ps, ACT.Copy).then_inc(S["oT_ready"], 1)

            def routed_ffn(b):
                copy_zT(b, 2)
                for l in range(3):
                    wait(act, S["route_h"], 3 * b + l + 1)
                    if l == 1:
                        wait(act, S["route_bias"], b + 1)
                    for o in range(2):
                        bias = bi[:, o:o + 1] if l == 0 else bias_sum[:, 2 * (l - 1) + o:2 * (l - 1) + o + 1]
                        last = act.activation((h_a, h_b, h_a)[l][:, o * D:(o + 1) * D],
                                              wide[l][:, o * D:(o + 1) * D], ACT.Relu, bias=bias)
                    last.then_inc(S["route_relu"], 1)

            def gcn(b):
                wait(act, S["row_sum_ready"], b + 1)
                act.activation(row_std[:, :], row_sum[:, :], ACT.Sqrt).then_inc(S["row_std_ready"], 1)
                wait(act, S["conv_made"], 2 * b + 1)
                act.activation(aT[:, :], aT_ps, ACT.Copy).then_inc(S["conv_ready"], 1)

            def gated_experts(b):
                copy_zT(b, 3)
                wait(act, S["odds_in"], b + 1)
                act.activation(odds[:, :], odds[:, :], ACT.Exp).then_inc(S["odds_out"], 1)
                experts(b, 4, EXP2, moe2_b1)

            def gin(b):
                wait(act, S["conv_made"], 2 * b + 2)
                act.activation(aT[:, :], aT_ps, ACT.Copy).then_inc(S["conv_ready"], 1)
                wait(act, S["gin_h"], b + 1)
                for o in range(2):
                    last = act.activation(h_a[:, o * D:(o + 1) * D], wide[0][:, o * D:(o + 1) * D], ACT.Relu,
                                          bias=gin_b1[:, o:o + 1])
                last.then_inc(S["gin_relu"], 1)

            def soften(b, j):
                wait(act, S["soft_in"], 4 * b + j + 1)
                act.activation(soft[:, :, :], soft[:, :, :], ACT.Exp).then_inc(S["soft_out"], 1)

            def back_head(b, h):
                n = HEADS * (b - 1) + h - 1
                if h == 0:
                    return
                wait(act, S["acc_made"], n)
                wait(act, S["rows_used"], n + 1)
                act.activation(kT[:, :], kT_ps[:, 0:D], ACT.Copy)
                act.activation(v_mem[:, :], v_ps[:, 0:D], ACT.Copy).then_inc(S["kv_ready"], 1)
                wait(act, S["q_made"], n + 1)
                act.activation(qT_mem[:, :], att_ps[:, 0:D], ACT.Copy, scale=float(D) ** -0.5).then_inc(S["q_ready"], 1)
                wait(act, S["sim_max"], n + 1)
                act.activation(e_mem[:, :], masked[:, :], ACT.Exp, bias=m_mem[:, :], accum_out=sum_mem[:, :])\
                    .then_inc(S["exp_mem"], 1)
                wait(act, S["eT_mem_made"], n + 1)
                act.activation(eT_mem[:, :], att_ps[:, 2 * D:3 * D], ACT.Copy).then_inc(S["eT_mem_ready"], 1)
                wait(act, S["out_made"], n + 1)
                act.activation(oT_mem[:, :], att_ps[:, 3 * D:4 * D], ACT.Copy).then_inc(S["out_ready"], 1)

            def body(b, front, back):
                for s in range(HEADS + 1):
                    if front:
                        if s == 0:
                            std_of(b, 0)
                            copy_zT(b, 0)
                            experts(b, 0, EXP0, moe0_b1)
                        elif s == 1:
                            std_of(b, 1)
                            mha(b)
                        elif s == 2:
                            std_of(b, 2)
                            routed_ffn(b)
                        elif s == 3:
                            std_of(b, 3)
                            gcn(b)
                        elif s == 4:
                            std_of(b, 4)
                            std_of(b, 5)
                            gated_experts(b)
                        elif s == 5:
                            std_of(b, 6)
                            gin(b)
                        elif s == 6:
                            std_of(b, 7)
                            copy_zT(b, 4)
                            soften(b, 0)
                            soften(b, 1)
                        elif s == 7:
                            soften(b, 2)
                            soften(b, 3)
                    if back:
                        back_head(b, s)
                if front:
                    if back:
                        wait(act, S["q_made"], HEADS * b)
                    act.activation(zH[:, :], zT[:, :], ACT.Copy).then_inc(S["zH_ready"], 1)
            run(act, body)

        @block.vector
        def _(dve):
            own = Steps(dve, S["own"])

            def link(ins):
                own.link(ins)

            def plain():
                dve.nop(nofuse=True)

            def norm(b, u, src, out):
                plain()
                link(dve.bn_stats(stats[:, :], src[:, :]))
                plain()
                dve.bn_aggr(mv[:, :], stats[:, :]).then_inc(S["var"], 1)
                wait(dve, S["std"], 8 * b + u + 1)
                link(dve.reciprocal(rstd[:, :], std[:, :]))
                return dve.tensor_scalar(out[:, :], src[:, :], mv[:, 0:1], rstd[:, :], ALU.subtract, ALU.mult)

            def norm_z(b, u):
                norm(b, u, x, z).then_inc(S["z"], 1)

            def add_y(b, k):
                wait(dve, S["y"], 4 * b + k + 1)
                link(dve.tensor_tensor(x[:, :], x[:, :], y_ps, ALU.add))

            def experts(b, first, count, weight):
                for e in range(count):
                    n = 12 * b + first + e
                    wait(dve, S["y_made"], n + 1)
                    dve.scalar_tensor_tensor(x[:, :], wide[2 + e % 2][:, 0:D], weight(e), x[:, :],
                                             ALU.mult, ALU.add).then_inc(S["y_used"], 1)
                    wait(dve, S["y_used"], n + 1)

            def mha(b):
                norm_z(b, 1)
                wait(dve, S["adj_in"], 16 * (b + 1))
                dve.tensor_scalar(absent[:, :], adjT[:, :], 0.0, -BIG, ALU.is_equal, ALU.mult)
                wait(dve, S["qkv_made"], b + 1)
                dve.tensor_tensor(k_heads[:, :].rearrange("p (h j) -> p h j", h=MHA_HEADS),
                                  wide[1][:, 0:D].unsqueeze(1).to_broadcast([P, MHA_HEADS, P]),
                                  head_mask[:, :].unsqueeze(2).to_broadcast([P, MHA_HEADS, P]), ALU.mult)\
                    .then_inc(S["k_ready"], 1)
                for j in range(2):
                    wait(dve, S["scores_made"], 2 * b + j + 1)
                    dve.reduce_max(neg_max[:, 4 * j:4 * j + 4], wide[2 + j][:, :].rearrange("p (h j) -> p h j", h=4),
                                   AX.X, negate=True).then_inc(S["max_ready"], 1)
                wait(dve, S["eT_made"], 2 * b + 2)
                dve.tensor_copy(eT_mha[:, 4 * P:8 * P], wide[1][:, :]).then_inc(S["eT_dve"], 1)
                link(dve.reciprocal(inv[:, :], sums[:, :]))
                wait(dve, S["o_made"], b + 1)
                dve.tensor_tensor(o_mha[:, :].rearrange("p (h d) -> p h d", h=MHA_HEADS),
                                  aT_ps.rearrange("p (h d) -> p h d", h=MHA_HEADS),
                                  inv[:, :].unsqueeze(2).to_broadcast([P, MHA_HEADS, 16]), ALU.mult)\
                    .then_inc(S["o_ready"], 1)
                add_y(b, 0)

            def routed_ffn(b):
                norm_z(b, 2)
                wait(dve, S["routed_in"], 64 * (b + 1))
                dve.tensor_tensor(bias_sum[:, :], bs[:, :], routed[:, :, HID:HID + 1].rearrange("p k o -> p (k o)"),
                                  ALU.add).then_inc(S["route_bias"], 1)
                add_y(b, 1)
                dve.sem_inc(S["routed_used"], 1)

            def gcn(b):
                norm_z(b, 3)
                wait(dve, S["z"], 8 * b + 4)
                wait(dve, S["row_sum_made"], b + 1)
                dve.tensor_scalar(row_sum[:, :], wide[3][:, 0:1], alpha[:, :], 1.0, ALU.mult, ALU.add)\
                    .then_inc(S["row_sum_ready"], 1)
                wait(dve, S["row_std_ready"], b + 1)
                link(dve.reciprocal(row_scale[:, :], row_std[:, :]))
                link(dve.tensor_scalar(zn[:, :], z[:, :], row_scale[:, :], None, ALU.mult))
                dve.tensor_scalar(za[:, :], zn[:, :], alpha[:, :], None, ALU.mult).then_inc(S["conv_z"], 1)
                wait(dve, S["y"], 4 * b + 3)
                link(dve.scalar_tensor_tensor(relu_in[:, :], y_ps, row_scale[:, :], gcn_b[:, :], ALU.mult, ALU.add))
                link(dve.scalar_tensor_tensor(x[:, :], relu_in[:, :], 0.0, x[:, :], ALU.max, ALU.add))

            def gated_experts(b):
                norm_z(b, 4)
                wait(dve, S["z"], 8 * b + 5)
                link(norm(b, 5, z, zn))
                link(dve.tensor_tensor(zn[:, :], zn[:, :], gamma[:, :], ALU.mult))
                dve.tensor_tensor(zn[:, :], zn[:, :], beta[:, :], ALU.add).then_inc(S["z"], 1)
                wait(dve, S["logits_made"], b + 1)
                link(dve.tensor_copy(logits[:, :], misc_ps[:, 0:EXP2]))
                plain()
                link(dve.max(top8[:, :], logits[:, :]))
                plain()
                link(dve.max_index(top8_i[:, :], top8[:, :], logits[:, :]))
                dve.tensor_tensor(odds[:, :], top8[:, 1:2], top8[:, 0:1], ALU.subtract).then_inc(S["odds_in"], 1)
                link(dve.tensor_copy(top8_f[:, :], top8_i[:, :]))
                wait(dve, S["odds_out"], b + 1)
                link(dve.tensor_scalar(w_best[:, :], odds[:, :], 1.0, None, ALU.add))
                link(dve.reciprocal(w_best[:, :], w_best[:, :]))
                link(dve.tensor_tensor(w_next[:, :], w_best[:, :], odds[:, :], ALU.mult))
                link(dve.tensor_scalar(hot[:, :], count16[:, 0:EXP2], top8_f[:, 1:2], w_next[:, :], ALU.is_equal, ALU.mult))
                link(dve.tensor_scalar(w_exp[:, :], count16[:, 0:EXP2], top8_f[:, 0:1], w_best[:, :],
                                       ALU.is_equal, ALU.mult))
                link(dve.tensor_tensor(w_exp[:, :], w_exp[:, :], hot[:, :], ALU.add))
                experts(b, 4, EXP2, lambda e: w_exp[:, e:e + 1])

            def gin(b):
                norm_z(b, 6)
                add_y(b, 3)

            def top16(values, value_rest, out, out_i):
                plain()
                link(dve.max(out[:, 0:8], values))
                plain()
                link(dve.match_replace(value_rest, out[:, 0:8], values, -3.0e38))
                plain()
                link(dve.max_index(out_i[:, 0:8], out[:, 0:8], values))
                plain()
                link(dve.max(out[:, 8:16], value_rest))
                plain()
                link(dve.max_index(out_i[:, 8:16], out[:, 8:16], value_rest))

            def choose(b, j):
                wait(dve, S["sims_made"], 4 * b + j + 1)
                for r in range(4):
                    cols = slice(r * KEYS, (r + 1) * KEYS)
                    top16(wide[j][:, cols], rest[:, cols], vals[:, r, :], vals_i[:, r, :])
                link(dve.tensor_copy(vals_f[:, :, :], vals_i[:, :, :]))
                for r in range(4):
                    head, half = 2 * j + r // 2, r % 2
                    if half:
                        link(dve.tensor_scalar(vals_f[:, r, :], vals_f[:, r, :], float(KEYS), None, ALU.mult))
                    else:
                        link(dve.tensor_scalar(vals_f[:, r, :], vals_f[:, r, :], float(head * KEYS * KEYS), None, ALU.add))
                by_half = vals[:, :, :].rearrange("p (h s) k -> p s h k", h=2)
                shape = [P, 2, TOP, TOP]
                grid = lambda t: t[:, :].rearrange("p (h a b) -> p h a b", h=2, a=TOP)
                link(dve.tensor_tensor(grid(pair_sum), by_half[:, 0, :, :].unsqueeze(3).to_broadcast(shape),
                                       by_half[:, 1, :, :].unsqueeze(2).to_broadcast(shape), ALU.add))
                for r in range(2):
                    cols = slice(r * TOP * TOP, (r + 1) * TOP * TOP)
                    top16(pair_sum[:, cols], pair_rest[:, cols], best[:, r, :], best_i[:, r, :])
                dve.tensor_tensor(soft[:, :, :], best[:, :, :], best[:, :, 0:1].to_broadcast([P, 2, TOP]), ALU.subtract)\
                    .then_inc(S["soft_in"], 1)
                halves = vals_f[:, :, :].rearrange("p (h s) k -> p s h k", h=2)
                for s in range(2):
                    if s == 0:
                        link(dve.tensor_scalar(digit[:, :, :], best_i[:, :, :], 4, None, ALU.logical_shift_right))
                    else:
                        link(dve.tensor_scalar(digit[:, :, :], best_i[:, :, :], 15, None, ALU.bitwise_and))
                    link(dve.tensor_copy(digit_f[:, :, :], digit[:, :, :]))
                    link(dve.tensor_tensor(pair_sum[:, :].rearrange("p (k a) -> p k a", a=TOP),
                                           digit_f[:, :, :].rearrange("p h k -> p (h k)").unsqueeze(2)
                                           .to_broadcast([P, 2 * TOP, TOP]),
                                           count16[:, :].unsqueeze(1).to_broadcast([P, 2 * TOP, TOP]), ALU.is_equal))
                    link(dve.tensor_tensor(grid(pair_sum), grid(pair_sum),
                                           halves[:, s, :, :].unsqueeze(2).to_broadcast(shape), ALU.mult))
                    link(dve.tensor_reduce(found[:, s, :, :].rearrange("p h k -> p (h k)"),
                                           pair_sum[:, :].rearrange("p (k a) -> p k a", a=TOP), AX.X, ALU.add))
                if j == 0:
                    wait(dve, S["index_copied"], b)
                cols = slice(2 * j * TOP, 2 * (j + 1) * TOP)
                two = lambda ap: ap.rearrange("p (h k) -> p h k", h=2)
                link(dve.tensor_tensor(two(index_next[:, cols]), found[:, 0, :, :], found[:, 1, :, :], ALU.add))
                wait(dve, S["soft_out"], 4 * b + j + 1)
                link(dve.tensor_reduce(soft_sum[:, :], soft[:, :, :], AX.X, ALU.add))
                link(dve.reciprocal(soft_sum[:, :], soft_sum[:, :]))
                link(dve.tensor_tensor(two(mem_w_next[:, cols]), soft[:, :, :],
                                       soft_sum[:, :].unsqueeze(2).to_broadcast([P, 2, TOP]), ALU.mult))
                if j == 3:
                    dve.sem_inc(S["chosen"], 1)

            def back_head(b, h):
                n = HEADS * (b - 1) + h
                if h < HEADS:
                    for half in range(2):
                        wait(dve, S["diag_used"], 2 * n - 1 + half)
                        w = mem_w[:, h * TOP + half * HALF:h * TOP + (half + 1) * HALF]
                        dve.tensor_tensor(diag[:, half, :].rearrange("p (k t) -> p k t", k=HALF),
                                          ident[:, :].unsqueeze(1).to_broadcast([P, HALF, P]),
                                          w.unsqueeze(2).to_broadcast([P, HALF, P]), ALU.mult)\
                            .then_inc(S["diag_ready"], 1)
                if h >= 1:
                    wait(dve, S["sim_made"], n)
                    link(dve.tensor_tensor(masked[:, :], att_ps[:, D:2 * D], causal[:, :], ALU.add))
                    dve.reduce_max(m_mem[:, :], masked[:, :], AX.X, negate=True).then_inc(S["sim_max"], 1)
                    wait(dve, S["exp_mem"], n)
                    link(dve.reciprocal(inv_mem[:, :], sum_mem[:, :]))
                    wait(dve, S["y_mem"], n)
                    if h == HEADS:
                        wait(dve, S["stored"], 16 * (b - 1))
                    out = xo if h == HEADS else x_cur
                    dve.scalar_tensor_tensor(out[:, :], att_ps[:, 0:D], inv_mem[:, :], x_cur[:, :], ALU.mult, ALU.add)\
                        .then_inc(S["acc_made"], 1)
                    wait(dve, S["acc_made"], n)
                    if h == HEADS:
                        dve.sem_inc(S["out_tile"], 1)

            def body(b, front, back):
                for s in range(HEADS + 1):
                    if front:
                        if s == 0:
                            link(dve.tensor_copy(x[:, :], x_all[:, bass.ds(b, 1), :].rearrange("p o d -> p (o d)")))
                            norm_z(b, 0)
                            experts(b, 0, EXP0, lambda e: gate[:, bass.ds(b, 1), e:e + 1].rearrange("p o e -> p (o e)"))
                        elif s < 6:
                            (mha, routed_ffn, gcn, gated_experts, gin)[s - 1](b)
                        elif s == 6:
                            norm_z(b, 7)
                            choose(b, 0)
                            choose(b, 1)
                        elif s == 7:
                            choose(b, 2)
                            choose(b, 3)
                    if back:
                        back_head(b, s)
                if front:
                    if back:
                        wait(dve, S["diag_ready"], 2 * HEADS * b)
                    link(dve.tensor_copy(mem_w[:, :], mem_w_next[:, :]))
                    link(dve.tensor_copy(x_cur[:, :], x[:, :]))
            run(dve, body, own, VECTOR_LINKS)


def layout(np, v):
    a = {k: np.asarray(x) for k, x in v.items()}
    T = lambda x: np.ascontiguousarray(np.swapaxes(x, -1, -2))
    rep = lambda x, w: np.ascontiguousarray(np.broadcast_to(np.reshape(x, (1, w)), (P, w)))
    halves = lambda x: np.ascontiguousarray(x.reshape(x.shape[:-2] + (-1, P, x.shape[-1])).swapaxes(-3, -2))
    row = lambda x: np.ascontiguousarray(np.reshape(x, (1, -1)))
    column = lambda x: np.ascontiguousarray(np.reshape(x, (-1, P)).T)
    arrays = {
        "x": a["x"], "adjT": T(a["adj"]), "edge_index": a["L0_ffn_edge_index"],
        "gnn0_w1": a["L0_gnn_W1"], "gnn0_w2": halves(a["L0_gnn_W2"]), "gnn0_rms": rep(a["L0_gnn_rms_weight"], 512),
        "gnn0_b1": row(a["L0_gnn_b1"]), "gnn0_b2": row(a["L0_gnn_b2"]), "gnn0_eps": rep(a["L0_gnn_epsilon"], 1),
        "w_gat": a["L0_ffn_W_gat"],
        "gat_att": np.stack([rep(a["L0_ffn_att_src"], 16), rep(a["L0_ffn_att_dst"], 16)], 1),
        "gat_rows": np.stack([rep(a["L0_ffn_b_gat"], 16), rep(a["L0_ffn_ln_gamma"], 16), rep(a["L0_ffn_ln_beta"], 16)], 1),
        "moe0_w1": np.ascontiguousarray(a["L0_ffn_W1"].transpose(1, 0, 2)),
        "moe0_w2": np.ascontiguousarray(a["L0_ffn_W2"].reshape(4, 2, P, D).transpose(2, 0, 1, 3)),
        "moe0_b1": column(a["L0_ffn_b1"]), "moe0_b2": row(a["L0_ffn_b2"]),
        "mha_wq": T(a["L1_gnn_W_q"]), "mha_wk": T(a["L1_gnn_W_k"]), "mha_wv": T(a["L1_gnn_W_v"]),
        "mha_wo": T(a["L1_gnn_W_o"]), "w_e": rep(a["L1_gnn_W_e"], 8),
        "route_wi": T(a["L1_ffn_Wi"]), "route_bi": column(a["L1_ffn_bi"]),
        "route_ws": np.ascontiguousarray(T(a["L1_ffn_Ws"]).reshape(4, P, 2 * D).transpose(1, 0, 2)),
        "route_bs": column(a["L1_ffn_bs"]), "route_wo": halves(T(a["L1_ffn_Wo"])), "route_bo": row(a["L1_ffn_bo"]),
        "gcn_w": T(a["L2_gnn_W"]), "gcn_b": rep(a["L2_gnn_b"], D), "alpha": rep(a["L2_gnn_alpha"], 1),
        "moe2_w1": np.ascontiguousarray(a["L2_ffn_W1"].transpose(1, 0, 2)),
        "moe2_w2": np.ascontiguousarray(a["L2_ffn_W2"].reshape(8, 2, P, D).transpose(2, 0, 1, 3)),
        "moe2_b1": column(a["L2_ffn_b1"]), "moe2_b2": row(a["L2_ffn_b2"]),
        "gamma": rep(a["L2_ffn_gamma"], D), "beta": rep(a["L2_ffn_beta"], D),
        "moe2_wr": a["L2_ffn_Wr"], "moe2_br": row(a["L2_ffn_br"]),
        "gin_w1": a["L3_gnn_W1"], "gin_w2": halves(a["L3_gnn_W2"]), "gin_b1": column(a["L3_gnn_b1"]),
        "gin_b2": row(a["L3_gnn_b2"]), "eps_gin": rep(a["L3_gnn_eps"], 1),
        "mem_wq": a["L3_ffn_Wq"], "mem_wo": np.ascontiguousarray(a["L3_ffn_Wo"].reshape(8, P, D).transpose(1, 0, 2)),
        "wqT": np.ascontiguousarray(a["L3_ffn_Wq_pk"].reshape(D, 2, 8, 64).transpose(3, 2, 1, 0).reshape(64, 16, D)),
        "keysT": np.ascontiguousarray(a["L3_ffn_pk_keys"].transpose(3, 2, 0, 1).reshape(64, 16, 128)),
        "memory": np.concatenate([a["L3_ffn_keys_table"], a["L3_ffn_values_table"]], 1),
        "route": rep(a["L1_ffn_route_id"], B),
    }
    table = np.zeros((2, 17, 2 * D, 2 * D + 1), np.float32)
    table[:, :16, :, :2 * D] = T(a["L1_ffn_Wr"])
    table[:, :16, :, 2 * D] = a["L1_ffn_br"]
    arrays["route_wr"] = table.reshape(-1, 2 * D + 1)
    return arrays


def kernel(**inputs):
    import numpy as np
    import concourse.bacc as bacc
    from concourse.bass_utils import run_bass_kernel_spmd

    nc = bacc.Bacc("TRN2", target_bir_lowering=False, num_devices=1)
    arrays, io = {}, {}
    for name, a in layout(np, inputs).items():
        a = np.ascontiguousarray(a)
        arrays[f"in_{name}"] = a
        io[name] = nc.dram_tensor(f"in_{name}", a.shape, mybir.dt.from_np(a.dtype), kind="ExternalInput").ap()
    io["out"] = nc.dram_tensor("out", (B, N, D), F32, kind="ExternalOutput").ap()
    build(nc, io)
    return run_bass_kernel_spmd(nc, [arrays], core_ids=[0]).results[0]["out"]
```

```python
import concourse.bass as bass
from concourse import mybir
from contextlib import ExitStack

F32, BF16, I32 = mybir.dt.float32, mybir.dt.bfloat16, mybir.dt.int32
ALU = mybir.AluOpType
ACT = mybir.ActivationFunctionType
AX = mybir.AxisListType

P = 128
B, N, D = 64, 128, 128
NODES = B * N
EDGES = 524288
COLS = EDGES // P
LANES = 8
STEPS = COLS // LANES
HI = NODES // P
SRC_BUFS = 4
NCH = 24
FCH = 8
CPAD = 32
CHUNK = 128
FAR = 1.0e6
BIG = 1.0e30
SORT_COLS = 8 * LANES
TO_INTEGER = 1.5 * 2 ** 23
TURN_COLS = 2 * CHUNK
VECTOR_LINKS = 243
EDGE_LINKS = 80


def turns(eng, count, body, own=None, links=0, peeled=1):
    for i in range(peeled):
        body(i)
    with eng.Fori(peeled, count) as i:
        if own:
            own.enter(i - peeled, links)
        body(i)
        if own:
            own.leave(count - peeled)


def wait(eng, sem, value):
    if not isinstance(value, int) or value > 0:
        eng.wait_ge(sem, value)


class Steps:

    def __init__(self, eng, sem):
        self.eng, self.sem, self.base, self.n = eng, sem, 0, 0

    def do(self, ins):
        ins.then_inc(self.sem, 1)
        self.n += 1

    def wait(self):
        self.eng.wait_ge(self.sem, self.base + self.n)

    def link(self, ins):
        self.do(ins)
        self.wait()

    def enter(self, i, each):
        self.total, self.each = self.base + self.n, each
        self.base, self.n = self.total + i * each, 0

    def leave(self, turns):
        assert self.n == self.each, f"the loop's body signals {self.n} times, not {self.each}"
        self.base, self.n = self.total + turns * self.each, 0


def partition_of(dve, own, m, out, place):
    own.link(dve.tensor_scalar(out, place, m["width_inv"][:, :], m["width_shift"][:, :], ALU.mult, ALU.add))
    own.link(dve.tensor_scalar(out, out, TO_INTEGER, None, ALU.add))
    own.link(dve.tensor_scalar(out, out, -TO_INTEGER, None, ALU.add))


def build(nc, io):
    ctx = ExitStack()
    with ctx:
        taken = set()

        def fresh(name):
            while name in taken:
                name += "_"
            taken.add(name)
            return name

        def sb(name, shape, dt=F32, c=ctx):
            return c.enter_context(nc.sbuf_tensor(fresh(name), shape, dt))

        def ps(name, shape, dt=F32, c=ctx):
            return c.enter_context(nc.psum_tensor(fresh(name), shape, dt))

        held = []

        def sem(name, c=ctx):
            held.append(c.enter_context(nc.semaphore(fresh(name))))
            return held[-1]

        def clear():
            with nc.Block() as block:
                @block.sync
                def _(sp):
                    for s in held:
                        sp.sem_clear(s)
            held.clear()

        ident = sb("ident", [P, P])
        identb = sb("identb", [P, P], BF16)
        before = sb("before", [P, P])
        ones = sb("ones", [P, P])
        start = sb("start", [P, HI])
        degree = sb("degree", [P, HI])
        sort_turns = sb("sort_turns", [P, 1], I32)
        turns_used = sb("turns_used", [P, 1], I32)
        width, width_inv, width_shift, width_gap = (
            sb(n, [P, 1]) for n in ("width", "width_inv", "width_shift", "width_gap"))
        x_all = sb("x_all", [P, B, D])
        node = sb("node", [P, B, NCH])
        gate = sb("gate", [P, B, 4])
        sorted_src = nc.dram_tensor("sorted_src", (EDGES, 1), I32).ap()
        segment_first = nc.dram_tensor("segment_first", (EDGES, FCH), F32).ap()
        node_table = nc.dram_tensor("node_table", (NODES, NCH), F32).ap()
        running = nc.dram_tensor("running", (EDGES, NCH), F32).ap()
        carried_in = nc.dram_tensor("carried_in", (P, 2 * CPAD), F32).ap()

        edge = ExitStack()
        with edge:
            dst_lo = sb("dst_lo", [P, COLS + LANES], BF16, edge)
            dst_hi = sb("dst_hi", [P, COLS + LANES], BF16, edge)
            src = sb("src", [P, COLS], I32, edge)
            digits = sb("digits", [P, P], BF16, edge)
            base_parts = sb("base_parts", [P, 3, LANES * HI], BF16, edge)
            hot_lo = sb("hot_lo", [P, 2, LANES * P], BF16, edge)
            hot_hi = sb("hot_hi", [P, 2, LANES * HI], BF16, edge)
            count_edges(nc, io, locals())
            sort_edges(nc, io, locals())
        edge_softmax(nc, io, locals())
        node_gates(nc, io, locals())
        later_layers(nc, io, locals())


def one_hots(dve, m, g, buf):
    lo = m["dst_lo"][:, bass.ds(g * LANES, LANES)].unsqueeze(2).to_broadcast([P, LANES, P])
    hi = m["dst_hi"][:, bass.ds(g * LANES, LANES)].unsqueeze(2).to_broadcast([P, LANES, HI])
    dig = m["digits"]
    dve.tensor_tensor(m["hot_lo"][:, buf, :].rearrange("p (l d) -> p l d", l=LANES), lo,
                      dig[:, :].unsqueeze(1).to_broadcast([P, LANES, P]), ALU.is_equal)
    return dve.tensor_tensor(m["hot_hi"][:, buf, :].rearrange("p (l d) -> p l d", l=LANES), hi,
                             dig[:, 0:HI].unsqueeze(1).to_broadcast([P, LANES, HI]), ALU.is_equal)


def count_edges(nc, io, m):
    sb, ps, sem = m["sb"], m["ps"], m["sem"]
    W = 512
    with ExitStack() as c:
        raw = sb("raw", [P, 2, W], I32, c)
        part = sb("part", [P, W], I32, c)
        num = sb("num", [P, W], F32, c)
        neg = sb("neg", [P, W], F32, c)
        zero_row = sb("zero_row", [P, 2048], I32, c)
        dst_word, mask = sb("dst_word", [P, COLS], I32, c), sb("move_mask", [P, COLS], I32, c)
        shift_by = [sb(f"shift_by{j}", [P, COLS], I32, c) for j in range(2)]
        is_absent = sb("is_absent", [P, COLS], F32, c)
        column = sb("column", [P, COLS], F32, c)
        kept, most = sb("kept_edges", [P, 1], F32, c), sb("most_edges", [P, 1], F32, c)
        kept_ps = ps("kept_ps", [P, P], F32, c)
        lane_count = sb("lane_count", [P, LANES * HI], F32, c)
        base = sb("base", [P, LANES * HI], F32, c)
        upto = sb("upto", [P, HI], F32, c)
        counts_ps = ps("counts_ps", [P, LANES * HI], F32, c)
        prefix_ps = ps("prefix_ps", [P, 2 * HI], F32, c)
        consts, s_prefill = sem("consts", c), sem("s_prefill", c)
        raw_in = [sem(f"raw_in{i}", c) for i in range(2)]
        raw_used, s_dve = sem("raw_used", c), sem("count_chain", c)
        hot_ready, hot_used, counted = sem("hot_ready", c), sem("hot_used", c), sem("counted", c)
        degree_ready, prefix_ready = sem("degree_ready", c), sem("prefix_ready", c)
        zeros_ready = sem("zeros_ready", c)
        kept_ready, kept_T, turns_ready = (sem(n, c) for n in ("kept_ready", "kept_transposed", "turns_ready"))
        chunks = [(row, t) for row in (1, 0) for t in range(COLS // W)]
        edges = io["edge_index"].rearrange("r (p t) -> r p t", p=P)
        ones, before, ident, identb, digits = m["ones"], m["before"], m["ident"], m["identb"], m["digits"]
        c.callback(m["clear"])
        block = c.enter_context(nc.Block())

        @block.gpsimd
        def _(pool):
            pool.memset(ident[:, :], 0.0).then_inc(consts, 1)
            pool.memset(identb[:, :], 0.0).then_inc(consts, 1)
            pool.memset(ones[:, :], 1.0).then_inc(consts, 1)
            pool.memset(zero_row[:, :], 0).then_inc(zeros_ready, 1)
            pool.iota(digits[:, :], [[1, P]], base=0, channel_multiplier=0,
                      allow_small_or_imprecise_dtypes=True).then_inc(consts, 1)
            pool.iota(column[:, :], [[1, COLS]], base=0, channel_multiplier=0,
                      allow_small_or_imprecise_dtypes=True).then_inc(consts, 1)
            pool.wait_ge(consts, 5)
            for t in (ident, identb):
                pool.affine_select(out=t[:, :], in_=t[:, :], compare_op=ALU.not_equal, fill=1.0, base=0,
                                   pattern=[[-1, P]], channel_multiplier=1).then_inc(consts, 1)
            pool.affine_select(out=before[:, :], in_=ones[:, :], compare_op=ALU.is_gt, fill=0.0, base=0,
                               pattern=[[1, P]], channel_multiplier=-1).then_inc(consts, 1)

        @block.sync
        def _(sp):
            for n, (row, t) in enumerate(chunks):
                if n >= 2:
                    sp.wait_ge(raw_used, n - 1)
                sp.dma_start(raw[:, n % 2, :], edges[row, :, t * W:(t + 1) * W]).then_inc(raw_in[n % 2], 16)
            sp.wait_ge(zeros_ready, 1)
            out = m["sorted_src"].rearrange("(p t) o -> p (t o)", p=P)
            for t in range(COLS // 2048):
                sp.dma_start(out[:, t * 2048:(t + 1) * 2048], zero_row[:, :]).then_inc(s_prefill, 16)
            out = m["segment_first"].rearrange("(p t) c -> p (t c)", p=P)
            for t in range(COLS * FCH // 2048):
                sp.dma_start(out[:, t * 2048:(t + 1) * 2048].bitcast(I32), zero_row[:, :]).then_inc(s_prefill, 16)
            sp.wait_ge(s_prefill, 16 * (COLS + COLS * FCH) // 2048)

        @block.vector
        def _(dve):
            own = Steps(dve, s_dve)
            own.do(dve.memset(m["dst_lo"][:, COLS:], 0.0))
            own.do(dve.memset(m["dst_hi"][:, COLS:], float(HI)))
            own.link(dve.memset(lane_count[:, :], 0.0))
            dve.tensor_copy(base[:, :], lane_count[:, :]).then_inc(counted, 1)
            for n, (row, t) in enumerate(chunks):
                dve.wait_ge(raw_in[n % 2], 16 * (n // 2 + 1))
                cols = slice(t * W, (t + 1) * W)
                r = raw[:, n % 2, :]
                if row:
                    own.do(dve.tensor_scalar(dst_word[:, cols], r, NODES - 1, None, ALU.bitwise_and))
                    own.link(dve.tensor_scalar(part[:, :], r, 7, None, ALU.arith_shift_right))
                    own.link(dve.tensor_scalar(neg[:, :], part[:, :], 0.0, 1.0e9, ALU.is_lt, ALU.mult))
                    own.link(dve.tensor_tensor(num[:, :], part[:, :], neg[:, :], ALU.add))
                    dve.tensor_scalar(is_absent[:, cols], num[:, :], float(HI), None, ALU.is_ge)\
                        .then_inc(raw_used, 1)
                else:
                    own.link(dve.tensor_scalar(neg[:, :], r, 0.0, float(NODES), ALU.is_lt, ALU.mult))
                    own.link(dve.tensor_tensor(num[:, :], r, neg[:, :], ALU.add))
                    dve.tensor_scalar(m["src"][:, cols], num[:, :], 0.0, float(NODES - 1), ALU.max, ALU.min)\
                        .then_inc(raw_used, 1)
                dve.wait_ge(raw_used, n + 1)
            src, moving = m["src"], dst_word
            bits = NODES.bit_length() - 1
            gone = mask[:, :].bitcast(F32)
            own.link(dve.tensor_tensor_scan(gone, is_absent[:, :], is_absent[:, :], 0.0, ALU.add, ALU.max))
            own.do(dve.tensor_scalar(kept[:, :], gone[:, COLS - 1:COLS], -1.0, float(COLS), ALU.mult, ALU.add))
            own.do(dve.scalar_tensor_tensor(shift_by[0][:, :], is_absent[:, :], 0.0, gone, ALU.is_equal, ALU.mult))
            own.link(dve.tensor_scalar(src[:, :], src[:, :], bits, None, ALU.logical_shift_left))
            own.link(dve.tensor_tensor(src[:, :], src[:, :], dst_word[:, :], ALU.bitwise_or))
            dve.nop(nofuse=True).then_inc(kept_ready, 1)
            for level in range(COLS.bit_length() - 1):
                by = 1 << level
                now, after = shift_by[level % 2], shift_by[(level + 1) % 2]
                left, right = slice(0, COLS - by), slice(by, COLS)
                own.link(dve.tensor_scalar(mask[:, :], now[:, :], level, 1, ALU.arith_shift_right, ALU.bitwise_and))
                own.link(dve.scalar_tensor_tensor(after[:, :], mask[:, :], 0.0, now[:, :], ALU.is_equal, ALU.mult))
                own.do(dve.copy_predicated(after[:, left], mask[:, right], now[:, right]))
                own.link(dve.copy_predicated(src[:, left], mask[:, right], src[:, right]))
            own.link(dve.tensor_scalar(moving[:, :], src[:, :], P - 1, None, ALU.bitwise_and))
            own.link(dve.tensor_copy(m["dst_lo"][:, 0:COLS], moving[:, :]))
            own.link(dve.tensor_scalar(moving[:, :], src[:, :], P.bit_length() - 1, HI - 1,
                                       ALU.logical_shift_right, ALU.bitwise_and))
            dve.wait_ge(consts, 8)
            own.link(dve.tensor_scalar(is_absent[:, :], column[:, :], kept[:, :], float(HI), ALU.is_ge, ALU.mult))
            own.do(dve.tensor_tensor(m["dst_hi"][:, 0:COLS], moving[:, :], is_absent[:, :], ALU.max))
            own.link(dve.tensor_scalar(src[:, :], src[:, :], bits, None, ALU.logical_shift_right))
            dve.wait_ge(kept_T, 1)
            own.link(dve.reduce_max(most[0:1, :], kept_ps[0:1, :], AX.X))
            own.link(dve.tensor_scalar(most[0:1, :], most[0:1, :], 1.0, float(SORT_COLS - 1), ALU.max, ALU.add))
            own.link(dve.tensor_copy(m["sort_turns"][0:1, :], most[0:1, :]))
            own.link(dve.tensor_scalar(m["sort_turns"][0:1, :], m["sort_turns"][0:1, :], SORT_COLS.bit_length() - 1,
                                       None, ALU.arith_shift_right))
            dve.nop(nofuse=True).then_inc(turns_ready, 1)
            used = dve.value_load(m["sort_turns"][0:1, 0:1], min_val=1, max_val=COLS // SORT_COLS)
            per = SORT_COLS // LANES
            with dve.Fori(0, STEPS // per) as i, dve.If(i < used):
                for k in range(per):
                    dve.wait_ge(hot_used, per * i + k + 1)
                    one_hots(dve, m, per * i + k, k % 2).then_inc(hot_ready, 1)
            dve.wait_ge(hot_used, per * used + 2)
            dve.nop(nofuse=True)
            own.link(dve.tensor_copy(lane_count[:, :], counts_ps[:, :]))
            dve.tensor_reduce(m["degree"][:, :], lane_count[:, :].rearrange("p (l h) -> p h l", l=LANES),
                              AX.X, ALU.add).then_inc(degree_ready, 1)
            dve.wait_ge(prefix_ready, 1)
            own.link(dve.tensor_tensor_scan(upto[:, :], ones[:, 0:HI], prefix_ps[:, HI:], 0.0, ALU.mult, ALU.add))
            width, inv, turns_used = m["width"], m["width_inv"], m["turns_used"]
            per_turn = P * TURN_COLS
            own.link(dve.tensor_scalar(width[:, :], upto[:, HI - 1:HI], float(per_turn - 1), float(per_turn),
                                       ALU.add, ALU.max))
            own.link(dve.tensor_copy(turns_used[:, :], width[:, :]))
            own.link(dve.tensor_scalar(turns_used[:, :], turns_used[:, :], per_turn.bit_length() - 1, None,
                                       ALU.arith_shift_right))
            own.link(dve.tensor_scalar(width[:, :], turns_used[:, :], float(TURN_COLS), None, ALU.mult))
            own.link(dve.reciprocal(inv[:, :], width[:, :]))
            own.link(dve.tensor_scalar(m["width_shift"][:, :], inv[:, :], 0.5, -0.5, ALU.mult, ALU.add))
            own.link(dve.tensor_scalar(m["width_gap"][:, :], width[:, :], -1.0, float(COLS), ALU.mult, ALU.add))
            own.link(dve.tensor_tensor(upto[:, :], upto[:, :], prefix_ps[:, HI:], ALU.subtract))
            own.link(dve.tensor_tensor(m["start"][:, :], upto[:, :], prefix_ps[:, 0:HI], ALU.add))
            own.link(dve.tensor_copy(base[:, 0:HI], m["start"][:, :]))
            for l in range(1, LANES):
                a, b = slice((l - 1) * HI, l * HI), slice(l * HI, (l + 1) * HI)
                own.link(dve.tensor_tensor(base[:, b], base[:, a], lane_count[:, a], ALU.add))
            for q in range(3):
                own.link(dve.tensor_copy(m["base_parts"][:, q, :], base[:, :]))
                own.link(dve.tensor_tensor(base[:, :], base[:, :], m["base_parts"][:, q, :], ALU.subtract))

        @block.tensor
        def _(pe):
            pe.sem_inc(hot_used, 2)
            pe.wait_ge(counted, 1)
            pe.wait_ge(consts, 8)
            pe.wait_ge(kept_ready, 1)
            pe.matmul(kept_ps[0:1, :], kept[:, :], ident[:, :], start=True, stop=True).then_inc(kept_T, 1)
            pe.matmul(counts_ps[:, :], ones[:, :], base[:, :], start=True, stop=False, skip_group_check=True)
            pe.wait_ge(turns_ready, 1)
            used = pe.value_load(m["sort_turns"][0:1, 0:1], min_val=1, max_val=COLS // SORT_COLS)
            per = SORT_COLS // LANES
            with pe.Fori(0, STEPS // per) as i, pe.If(i < used):
                for k in range(per):
                    pe.wait_ge(hot_ready, per * i + k + 1)
                    for l in range(LANES):
                        last = pe.matmul(counts_ps[:, l * HI:(l + 1) * HI], m["hot_lo"][:, k % 2, l * P:(l + 1) * P],
                                         m["hot_hi"][:, k % 2, l * HI:(l + 1) * HI], start=False, stop=False,
                                         skip_group_check=True)
                    last.then_inc(hot_used, 1)
            pe.wait_ge(degree_ready, 1)
            pe.matmul(prefix_ps[:, 0:HI], before[:, :], m["degree"][:, :], start=True, stop=True)
            pe.matmul(prefix_ps[:, HI:], ones[:, :], m["degree"][:, :], start=True, stop=True)\
                .then_inc(prefix_ready, 1)


def sort_edges(nc, io, m):
    sb, ps, sem = m["sb"], m["ps"], m["sem"]
    with ExitStack() as c:
        hot_lo, hot_hi = m["hot_lo"], m["hot_hi"]
        hot_loT = sb("hot_loT", [P, 2, LANES * P], BF16, c)
        same = sb("same", [P, 2, LANES * P], BF16, c)
        count_parts = sb("count_parts", [P, 2, 2, LANES * HI], BF16, c)
        chosen = sb("chosen", [P, LANES * HI], F32, c)
        place_f = sb("place_f", [P, LANES], F32, c)
        part_f = sb("part_f", [P, LANES], F32, c)
        absent = sb("absent", [P, LANES], F32, c)
        place = sb("place", [P, SRC_BUFS, LANES], I32, c)
        moved = sb("moved", [P, SRC_BUFS, LANES], I32, c)
        zeros = sb("zeros", [P, LANES * HI], F32, c)
        loT_ps = ps("loT_ps", [P, LANES * P], BF16, c)
        same_ps = ps("same_ps", [P, LANES * P], F32, c)
        place_ps = ps("place_ps", [P, LANES * HI], F32, c)
        count_ps = ps("count_ps", [P, LANES * HI], F32, c)
        hot_ready, loT_made, loT_ready = sem("hot_ready2", c), sem("loT_made", c), sem("loT_ready", c)
        same_made, same_ready = sem("same_made", c), sem("same_ready", c)
        counted, high_ready, parts_ready = sem("counted2", c), sem("high_ready", c), sem("parts_ready", c)
        placed, chosen_done, place_ready = sem("placed", c), sem("chosen_done", c), sem("place_ready", c)
        s_dve, s_layer, s_running = sem("sort_chain", c), sem("layer_chain", c), sem("running_prefilled", c)
        scattered = [sem(f"scattered{q}", c) for q in range(SRC_BUFS)]
        eps_ident = sb("eps_ident", [P, P], F32, c)
        w1, w2 = sb("gnn0_w1", [P, 4 * D], F32, c), sb("gnn0_w2", [P, 4, D], F32, c)
        rms_w, att = sb("rms_w", [P, 4 * D], F32, c), sb("att", [P, 2, 16], F32, c)
        b1, b2 = sb("gnn0_b1", [1, 4 * D], F32, c), sb("gnn0_b2", [1, D], F32, c)
        w_node, w_att = sb("w_node", [P, NCH], F32, c), sb("w_att", [P, 2, 16], F32, c)
        eps_in = sb("gnn0_eps", [P, 1], F32, c)
        xa, adjT = sb("xa", [P, D], F32, c), sb("adjT0", [P, P], F32, c)
        stats, mv, std, rstd = (sb(n, [P, w], F32, c) for n, w in
                                (("stats0", 6), ("mv0", 2), ("std0", 1), ("rstd0", 1)))
        z, z2, aggT, z2T = (sb(n, [P, D], F32, c) for n in ("z0", "z02", "aggT0", "z2T0"))
        squares, hn, hs = (sb(n, [P, 4 * D], F32, c) for n in ("squares", "hn0", "hs0"))
        hsT, ssq = sb("hsT0", [P, 4 * D], F32, c), sb("ssq0", [P, 1], F32, c)
        eps_rms, eps_ln = sb("eps_rms", [P, 1], F32, c), sb("eps_ln0", [P, 1], F32, c)
        small_ps, h_ps, hsT_ps = (ps(n, [P, 4 * D], F32, c) for n in ("small_ps", "h_ps0", "hsT_ps0"))
        weights_in, x_in, adj_in = sem("weights_in0", c), sem("x_in0", c), sem("adj_in0", c)
        s_var, s_std, s_z, s_agg, s_aggT, s_h, s_sq, s_rms, s_hn, s_hs, s_hsT, s_hsTs, s_y, s_x = (
            sem("a_" + n, c) for n in ("var std z agg aggT h squares rms hn hs hsT hsT_copied y x").split())
        s_var2, s_std2, s_z2, s_z2T, s_z2Ts, s_node, s_kept = (
            sem("a2_" + n, c) for n in ("var std z zT zT_copied node node_kept").split())
        w_ready = sem("w_node_ready", c)
        c.callback(m["clear"])
        block = c.enter_context(nc.Block())
        TURNS, UN = STEPS // 8, 8
        assert TURNS == B

        @block.sync
        def _(sp):
            for dst, name in ((w1, "gnn0_w1"), (w2, "gnn0_w2"), (rms_w, "gnn0_rms"), (att, "gat_att"),
                              (b1, "gnn0_b1"), (b2, "gnn0_b2"), (eps_in, "gnn0_eps")):
                sp.dma_start(dst[tuple([slice(None)] * len(dst.shape))], io[name]).then_inc(weights_in, 16)
            sp.dma_start(w_node[:, 0:16], io["w_gat"]).then_inc(weights_in, 16)

            def load(i):
                wait(sp, s_x, i)
                sp.dma_start(xa[:, :], io["x"][bass.ds(i, 1), :, :].rearrange("o n d -> (o n) d"))\
                    .then_inc(x_in, 16)
                wait(sp, s_agg, i)
                sp.dma_start(adjT[:, :], io["adjT"][bass.ds(i, 1), :, :].rearrange("o n d -> (o n) d"))\
                    .then_inc(adj_in, 16)
            turns(sp, B, load)
            sp.wait_ge(s_kept, B)
            sp.dma_start(m["node_table"].rearrange("(b n) c -> n b c", n=P), m["node"][:, :, :])\
                .then_inc(x_in, 16)
            sp.wait_ge(x_in, 16 * (B + 1))

        def turns_with_layer(eng, sort_turn, layer, *chains):
            used = eng.value_load(m["sort_turns"][0:1, 0:1], min_val=1, max_val=TURNS)
            sort_turn(0)
            with eng.Fori(1, TURNS) as i:
                for own, links in chains:
                    own.enter(i - 1, links)
                with eng.If(i < used):
                    sort_turn(i)
                    eng.nop(nofuse=True)
                if layer:
                    for own, links in chains[1:]:
                        own.n = 0
                    with eng.If(i >= used):
                        for k in range(UN):
                            layer(i, k)
                        eng.nop(nofuse=True)
                for own, links in chains:
                    own.leave(TURNS - 1)
            return used

        def gnn_vector(dve, own, i, k):
            def norm(x, out, got, std_ready, var_ready, z_ready):
                dve.nop(nofuse=True)
                own.link(dve.bn_stats(stats[:, :], x))
                dve.nop(nofuse=True)
                dve.bn_aggr(mv[:, :], stats[:, :]).then_inc(var_ready, 1)
                dve.wait_ge(var_ready, i + 1)
                dve.wait_ge(std_ready, i + 1)
                own.link(dve.reciprocal(rstd[:, :], std[:, :]))
                dve.tensor_scalar(out, x, mv[:, 0:1], rstd[:, :], ALU.subtract, ALU.mult).then_inc(z_ready, 1)
            if k == 0:
                dve.wait_ge(x_in, 16 * (i + 1))
                norm(xa[:, :], z[:, :], x_in, s_std, s_var, s_z)
                dve.wait_ge(s_z, i + 1)
            if k == 2:
                dve.wait_ge(s_rms, i + 1)
                own.link(dve.reciprocal(rstd[:, :], std[:, :]))
                dve.scalar_tensor_tensor(hn[:, :], h_ps[:, :], rstd[:, :], rms_w[:, :], ALU.mult, ALU.mult)\
                    .then_inc(s_hn, 1)
            if k == 5:
                dve.wait_ge(s_y, i + 1)
                dve.wait_ge(s_hn, i + 1)
                x1 = m["x_all"][:, bass.ds(i, 1), :].rearrange("p o d -> p (o d)")
                dve.tensor_tensor(x1, xa[:, :], small_ps[:, D:2 * D], ALU.add).then_inc(s_x, 1)
                dve.wait_ge(s_x, i + 1)
                norm(x1, z2[:, :], None, s_std2, s_var2, s_z2)
                dve.wait_ge(s_z2, i + 1)
            if k == 7:
                dve.wait_ge(s_node, i + 1)
                dve.tensor_copy(m["node"][:, bass.ds(i, 1), :].rearrange("p o c -> p (o c)"),
                                small_ps[:, 3 * D:3 * D + NCH]).then_inc(s_kept, 1)

        def gnn_scalar(act, i, k):
            if k == 0:
                act.wait_ge(s_var, i + 1)
                act.activation(std[:, :], mv[:, 1:2], ACT.Sqrt, bias=eps_ln[:, :]).then_inc(s_std, 1)
            if k == 1:
                act.wait_ge(s_agg, i + 1)
                act.activation(aggT[:, :], small_ps[:, 0:D], ACT.Copy).then_inc(s_aggT, 1)
            if k == 2:
                act.wait_ge(s_h, i + 1)
                act.activation(squares[:, :], h_ps[:, :], ACT.Square, accum_out=ssq[:, :]).then_inc(s_sq, 1)
                act.wait_ge(s_sq, i + 1)
                act.activation(std[:, :], ssq[:, :], ACT.Sqrt, bias=eps_rms[:, :], scale=1.0 / (4 * D))\
                    .then_inc(s_rms, 1)
            if k == 3:
                act.wait_ge(s_hn, i + 1)
                act.activation(hs[:, :], hn[:, :], ACT.Silu).then_inc(s_hs, 1)
            if k == 4:
                act.wait_ge(s_hsT, i + 1)
                act.activation(hsT[:, :], hsT_ps[:, :], ACT.Copy).then_inc(s_hsTs, 1)
            if k == 5:
                act.wait_ge(s_var2, i + 1)
                act.activation(std[:, :], mv[:, 1:2], ACT.Sqrt, bias=eps_ln[:, :]).then_inc(s_std2, 1)
            if k == 6:
                act.wait_ge(s_z2T, i + 1)
                act.activation(z2T[:, :], small_ps[:, 2 * D:3 * D], ACT.Copy).then_inc(s_z2Ts, 1)

        def gnn_tensor(pe, i, k):
            if k == 1:
                pe.wait_ge(s_z, i + 1)
                pe.wait_ge(adj_in, 16 * (i + 1))
                pe.matmul(small_ps[:, 0:D], z[:, :], adjT[:, :], start=True, stop=False)
                pe.matmul(small_ps[:, 0:D], z[:, :], eps_ident[:, :], start=False, stop=True).then_inc(s_agg, 1)
                pe.wait_ge(s_aggT, i + 1)
                pe.matmul(h_ps[:, :], aggT[:, :], w1[:, :], start=True, stop=False)
                pe.matmul(h_ps[:, :], m["ones"][0:1, :], b1[:, :], start=False, stop=True).then_inc(s_h, 1)
            if k == 3:
                pe.wait_ge(s_hs, i + 1)
                for q in range(4):
                    last = pe.transpose(hsT_ps[:, q * D:(q + 1) * D], hs[:, q * D:(q + 1) * D], m["ident"][:, :])
                last.then_inc(s_hsT, 1)
            if k == 4:
                pe.wait_ge(s_hsTs, i + 1)
                for q in range(4):
                    pe.matmul(small_ps[:, D:2 * D], hsT[:, q * D:(q + 1) * D], w2[:, q, :], start=(q == 0), stop=False)
                pe.matmul(small_ps[:, D:2 * D], m["ones"][0:1, :], b2[:, :], start=False, stop=True).then_inc(s_y, 1)
            if k == 6:
                pe.wait_ge(s_z2, i + 1)
                pe.transpose(small_ps[:, 2 * D:3 * D], z2[:, :], m["ident"][:, :]).then_inc(s_z2T, 1)
                pe.wait_ge(s_z2Ts, i + 1)
                pe.matmul(small_ps[:, 3 * D:3 * D + NCH], z2T[:, :], w_node[:, :], start=True, stop=True)\
                    .then_inc(s_node, 1)

        @block.vector
        def _(dve):
            own, layer_own = Steps(dve, s_dve), Steps(dve, s_layer)
            own.do(dve.memset(zeros[:, :], 0.0))
            own.link(dve.memset(count_parts[:, :, :, :], 0.0))
            own.do(dve.memset(eps_rms[:, :], 1e-6))
            own.link(dve.memset(eps_ln[:, :], 1e-5))
            dve.wait_ge(weights_in, 16 * 8)
            own.link(dve.tensor_scalar(eps_ident[:, :], m["ident"][:, :], eps_in[:, :], None, ALU.mult))
            own.link(dve.tensor_tensor(w_att[:, :, :], att[:, :, :],
                                       w_node[:, 0:16].unsqueeze(1).to_broadcast([P, 2, 16]), ALU.mult))
            dve.tensor_reduce(w_node[:, 16:24], w_att[:, :, :].rearrange("p a (h e) -> p (a h) e", h=4), AX.X, ALU.add)\
                .then_inc(w_ready, 1)
            dve.wait_ge(w_ready, 1)
            dve.nop(nofuse=True).then_inc(parts_ready, 1)
            one_hots(dve, m, 0, 0).then_inc(hot_ready, 1)

            def sort_turn(i):
                for k in range(UN):
                    g = i * UN + k
                    buf, nxt, q = k % 2, (k + 1) % 2, k % SRC_BUFS
                    dve.wait_ge(placed, g + 2)
                    one_hots(dve, m, g + 1, nxt).then_inc(hot_ready, 1)
                    dve.wait_ge(same_made, g + 1)
                    dve.tensor_tensor(same[:, buf, :].rearrange("p (l e) -> p l e", l=LANES),
                                      same_ps[:, :].rearrange("p (l e) -> p l e", l=LANES),
                                      m["before"][:, :].unsqueeze(1).to_broadcast([P, LANES, P]),
                                      ALU.mult).then_inc(same_ready, 1)
                    dve.wait_ge(high_ready, g + 1)
                    dve.tensor_tensor(count_parts[:, nxt, 1, :], count_ps[:, :], count_parts[:, nxt, 0, :],
                                      ALU.subtract).then_inc(parts_ready, 1)
                    dve.wait_ge(placed, g + 3)
                    dve.tensor_tensor(chosen[:, :], place_ps[:, :], hot_hi[:, buf, :], ALU.mult)\
                        .then_inc(chosen_done, 1)
                    dve.wait_ge(chosen_done, g + 1)
                    own.do(dve.tensor_reduce(place_f[:, :], chosen[:, :].rearrange("p (l h) -> p l h", l=LANES),
                                             AX.X, ALU.add))
                    own.link(dve.tensor_scalar(absent[:, :], m["dst_hi"][:, bass.ds(g * LANES, LANES)],
                                               float(HI), FAR, ALU.is_equal, ALU.mult))
                    partition_of(dve, own, m, part_f[:, :], place_f[:, :])
                    own.link(dve.scalar_tensor_tensor(place_f[:, :], part_f[:, :], m["width_gap"][:, :],
                                                      place_f[:, :], ALU.mult, ALU.add))
                    wait(dve, scattered[q], 16 * LANES * (i * (UN // SRC_BUFS) + k // SRC_BUFS))
                    own.do(dve.tensor_copy(moved[:, q, :], m["src"][:, bass.ds(g * LANES, LANES)]))
                    dve.tensor_tensor(place[:, q, :], place_f[:, :], absent[:, :], ALU.add)\
                        .then_inc(place_ready, 1)
                    dve.wait_ge(place_ready, g + 1)
                    gnn_vector(dve, layer_own, i, k)
            turns_with_layer(dve, sort_turn, lambda i, k: gnn_vector(dve, layer_own, i, k), (own, 7 * UN), (layer_own, 5))

        @block.scalar
        def _(act):
            act.wait_ge(w_ready, 1)
            W = LANES * HI
            out = m["running"].rearrange("(p t) c -> p (t c)", p=P)
            for t in range(COLS * NCH // (4 * W)):
                act.dma_start(out[:, t * 4 * W:(t + 1) * 4 * W].rearrange("p (a w) -> p a w", a=4),
                              zeros[:, :].unsqueeze(1).to_broadcast([P, 4, W])).then_inc(s_running, 16)

            def turn(i):
                for k in range(UN):
                    g = i * UN + k
                    buf, nxt = k % 2, (k + 1) % 2
                    act.wait_ge(loT_made, g + 1)
                    act.wait_ge(placed, g + 1)
                    act.activation(hot_loT[:, buf, :], loT_ps[:, :], ACT.Copy).then_inc(loT_ready, 1)
                    act.wait_ge(counted, g + 1)
                    act.wait_ge(placed, g + 2)
                    act.activation(count_parts[:, nxt, 0, :], count_ps[:, :], ACT.Copy).then_inc(high_ready, 1)
                    gnn_scalar(act, i, k)
            turns_with_layer(act, turn, lambda i, k: gnn_scalar(act, i, k))
            act.wait_ge(s_running, 16 * COLS * NCH // (4 * W))

        @block.tensor
        def _(pe):
            pe.sem_inc(placed, 2)
            pe.wait_ge(hot_ready, 1)
            pe.wait_ge(parts_ready, 1)
            pe.wait_ge(w_ready, 1)
            pe.wait_ge(weights_in, 16 * 8)
            pe.matmul(count_ps[:, :], m["ones"][:, :], zeros[:, :], start=True, stop=False, skip_group_check=True)

            def turn(i):
                for k in range(UN):
                    g = i * UN + k
                    buf = k % 2
                    pe.wait_ge(hot_ready, g + 1)
                    wait(pe, loT_ready, g)
                    for l in range(LANES):
                        last = pe.transpose(loT_ps[:, l * P:(l + 1) * P], hot_lo[:, buf, l * P:(l + 1) * P],
                                            m["identb"][:, :])
                    last.then_inc(loT_made, 1)
                    pe.wait_ge(parts_ready, g + 1)
                    for l in range(LANES):
                        last = pe.matmul(count_ps[:, l * HI:(l + 1) * HI], hot_lo[:, buf, l * P:(l + 1) * P],
                                         hot_hi[:, buf, l * HI:(l + 1) * HI], start=False, stop=False,
                                         skip_group_check=True)
                    last.then_inc(counted, 1)
                    pe.wait_ge(loT_ready, g + 1)
                    wait(pe, same_ready, g)
                    for l in range(LANES):
                        lo = hot_loT[:, buf, l * P:(l + 1) * P]
                        last = pe.matmul(same_ps[:, l * P:(l + 1) * P], lo, lo, start=True, stop=True)
                    last.then_inc(same_made, 1)
                    wait(pe, chosen_done, g)
                    pe.wait_ge(same_ready, g + 1)
                    for l in range(LANES):
                        h = slice(l * HI, (l + 1) * HI)
                        lo = hot_loT[:, buf, l * P:(l + 1) * P]
                        out = place_ps[:, h]
                        pe.matmul(out, same[:, buf, l * P:(l + 1) * P], hot_hi[:, buf, h], start=True, stop=False)
                        for q in range(2):
                            pe.matmul(out, lo, count_parts[:, buf, q, h], start=False, stop=False)
                        for q in range(3):
                            last = pe.matmul(out, lo, m["base_parts"][:, q, h], start=False, stop=(q == 2))
                    last.then_inc(placed, 1)
                    gnn_tensor(pe, i, k)
            turns_with_layer(pe, turn, lambda i, k: gnn_tensor(pe, i, k))

        @block.gpsimd
        def _(pool):

            def turn(i):
                for k in range(UN):
                    q = k % SRC_BUFS
                    pool.wait_ge(place_ready, i * UN + k + 1)
                    pool.nop(nofuse=True)
                    for l in range(LANES):
                        pool.indirect_dma_start(
                            out=m["sorted_src"],
                            out_offset=bass.IndirectOffsetOnAxis(ap=place[:, q, l:l + 1], axis=0),
                            in_=moved[:, q, l:l + 1], in_offset=None,
                            bounds_check=EDGES - 1, oob_is_err=False).then_inc(scattered[q], 16)
            used = turns_with_layer(pool, turn, None)
            for q in range(SRC_BUFS):
                pool.wait_ge(scattered[q], used * (16 * LANES * (UN // SRC_BUFS)))
                pool.nop(nofuse=True)


def edge_softmax(nc, io, m):
    sb, ps, sem = m["sb"], m["ps"], m["sem"]
    node, start, degree = m["node"], m["start"], m["degree"]
    H, TURNS = 4, COLS // CHUNK // 2
    with ExitStack() as c:
        bounds = sb("bounds", [P, P], F32, c)
        end = sb("end", [P, HI], F32, c)
        first_row = sb("first_row", [P, HI, FCH], F32, c)
        first_place = sb("first_place", [P, HI], I32, c)
        empty, in_part = sb("empty", [P, HI], F32, c), sb("in_part", [P, HI], F32, c)
        over = sb("over", [P, 2, 8, P], F32, c)
        target_in = sb("target_in", [P, H], F32, c)
        index = sb("index", [P, 2, CHUNK], I32, c)
        rows = sb("rows", [P, 2, CHUNK, NCH], F32, c)
        firsts = sb("firsts", [P, 2, CHUNK, FCH], F32, c)
        state = sb("state", [P, 2, CHUNK, NCH], F32, c)
        inside, reset = sb("inside", [P, CHUNK], F32, c), sb("reset", [P, CHUNK], F32, c)
        target, score, leaky, keep, weight = (sb(n, [P, H, CHUNK], F32, c) for n in
                                              ("target", "score", "leaky", "keep", "weight"))
        top = sb("top", [P, H, CHUNK + 1], F32, c)
        feats = sb("feats", [P, 16, CHUNK], F32, c)
        carry = sb("carry", [P, NCH], F32, c)
        any_first, some = sb("any_first", [P, 1], F32, c), sb("some", [P, 1], F32, c)
        ends = sb("ends", [P, 3, CPAD], F32, c)
        endsT = sb("endsT", [CPAD, 3, P], F32, c)
        runT = sb("runT", [CPAD, 2, P + 1], F32, c)
        keepT, weightT, insideT, resetT = (sb(n, [CPAD, P], F32, c) for n in ("keepT", "weightT", "insideT", "resetT"))
        carried = sb("carried", [P, 2, CPAD], F32, c)
        target_ps = ps("target_ps", [P, 512], F32, c)
        ends_ps = ps("ends_ps", [P, 512], F32, c)
        back_ps = ps("back_ps", [P, 512], F32, c)
        s_dve, s_bounds, firsts_ready, scattered = (sem(n, c) for n in
                                                    ("edge_chain", "bounds_ready", "firsts_ready", "firsts_scattered"))
        over_ready, over_used = sem("over_ready", c), sem("over_used", c)
        index_in, gathered, firsts_in, stored = ([sem(f"{n}{q}", c) for q in range(2)] for n in
                                                 ("index_in", "rows_gathered", "firsts_in", "state_stored"))
        consumed, state_ready, exp_in, exp_out = (sem(n, c) for n in ("consumed", "state_ready", "exp_in", "exp_out"))
        ends_ready, ends_T, run_ready, run_T, carried_ready, carried_out = (
            sem(n, c) for n in ("ends_ready", "ends_transposed", "run_ready", "run_transposed", "carried_ready",
                                "carried_out"))
        by_place = lambda ap: ap.rearrange("(p t) c -> p t c", p=P)
        c.callback(m["clear"])
        block = c.enter_context(nc.Block())

        @block.gpsimd
        def _(pool):
            pool.iota(bounds[:, :], [[1, P]], base=0, channel_multiplier=0,
                      allow_small_or_imprecise_dtypes=True).then_inc(s_bounds, 1)
            pool.wait_ge(firsts_ready, 1)
            for h in range(HI):
                pool.indirect_dma_start(
                    out=m["segment_first"], out_offset=bass.IndirectOffsetOnAxis(ap=first_place[:, h:h + 1], axis=0),
                    in_=first_row[:, h, :], in_offset=None, bounds_check=EDGES - 1, oob_is_err=False)\
                    .then_inc(scattered, 16)
            used = pool.value_load(m["turns_used"][0:1, 0:1], min_val=1, max_val=TURNS)
            with pool.Fori(0, TURNS) as i, pool.If(i < used):
                for q in range(2):
                    pool.wait_ge(index_in[q], 16 * (i + 1))
                    pool.nop(nofuse=True)
                    pool.wait_ge(consumed, 2 * i + q + 1)
                    pool.nop(nofuse=True)
                    for t in range(CHUNK):
                        pool.indirect_dma_start(
                            out=rows[:, q, t, :], out_offset=None, in_=m["node_table"],
                            in_offset=bass.IndirectOffsetOnAxis(ap=index[:, q, t:t + 1], axis=0))\
                            .then_inc(gathered[q], 16)

        @block.sync
        def _(sp):
            sorted_src = m["sorted_src"].rearrange("(p t) o -> p (t o)", p=P)
            sp.wait_ge(scattered, 16 * HI)
            used = sp.value_load(m["turns_used"][0:1, 0:1], min_val=1, max_val=TURNS)
            with sp.Fori(0, TURNS) as i, sp.If(i < used):
                for q in range(2):
                    sp.wait_ge(consumed, 2 * i + q + 1)
                    sp.dma_start(index[:, q, :], sorted_src[:, bass.ds((2 * i + q) * CHUNK, CHUNK)])\
                        .then_inc(index_in[q], 16)
                    sp.dma_start(firsts[:, q, :, :],
                                 by_place(m["segment_first"])[:, bass.ds((2 * i + q) * CHUNK, CHUNK), :])\
                        .then_inc(firsts_in[q], 16)

        @block.scalar
        def _(act):
            used = act.value_load(m["turns_used"][0:1, 0:1], min_val=1, max_val=TURNS)
            with act.Fori(0, TURNS) as i, act.If(i < used):
                for q in range(2):
                    n = 2 * i + q
                    act.wait_ge(exp_in, 2 * n + 1)
                    act.activation(keep[:, :, :], keep[:, :, :], ACT.Exp).then_inc(exp_out, 1)
                    act.wait_ge(exp_in, 2 * n + 2)
                    act.activation(weight[:, :, :], weight[:, :, :], ACT.Exp).then_inc(exp_out, 1)
                    act.wait_ge(state_ready, n + 1)
                    act.dma_start(by_place(m["running"])[:, bass.ds(n * CHUNK, CHUNK), :], state[:, q, :, :])\
                        .then_inc(stored[q], 16)
                act.nop(nofuse=True)
            K = 2 * used
            act.wait_ge(exp_in, 2 * K + 1)
            act.activation(keepT[:, :], keepT[:, :], ACT.Exp).then_inc(exp_out, 1)
            act.wait_ge(exp_in, 2 * K + 2)
            act.activation(weightT[:, :], weightT[:, :], ACT.Exp).then_inc(exp_out, 1)
            act.wait_ge(carried_ready, 1)
            act.dma_start(m["carried_in"], carried[:, :, :].rearrange("p a c -> p (a c)")).then_inc(carried_out, 16)
            for q in range(2):
                act.wait_ge(stored[q], 16 * used)
                act.nop(nofuse=True)
            act.wait_ge(carried_out, 16)

        @block.tensor
        def _(pe):
            for g in range(HI // 8):
                pe.wait_ge(over_ready, g + 1)
                for j in range(8):
                    h = 8 * g + j
                    last = pe.matmul(target_ps[:, 0:H], over[:, g % 2, j, :], node[:, h, 20:24],
                                     start=(h == 0), stop=(h == HI - 1))
                last.then_inc(over_used, 1)
            pe.wait_ge(ends_ready, 1)
            for a in range(3):
                last = pe.transpose(ends_ps[0:CPAD, a * P:(a + 1) * P], ends[:, a, :], m["ident"][:, :])
            last.then_inc(ends_T, 1)
            pe.wait_ge(run_ready, 1)
            for a in range(2):
                last = pe.transpose(back_ps[:, a * CPAD:(a + 1) * CPAD], runT[:, a, 0:P], m["ident"][0:CPAD, 0:CPAD])
            last.then_inc(run_T, 1)

        @block.vector
        def _(dve):
            own = Steps(dve, s_dve)
            own.link(dve.tensor_tensor(end[:, :], start[:, :], degree[:, :], ALU.add))
            own.link(dve.tensor_scalar(empty[:, :], degree[:, :], 0.0, FAR, ALU.is_equal, ALU.mult))
            partition_of(dve, own, m, in_part[:, :], start[:, :])
            own.link(dve.scalar_tensor_tensor(in_part[:, :], in_part[:, :], m["width_gap"][:, :], start[:, :],
                                              ALU.mult, ALU.add))
            own.link(dve.tensor_tensor(first_place[:, :], in_part[:, :], empty[:, :], ALU.add))
            own.do(dve.memset(carry[:, :], 0.0))
            own.link(dve.memset(first_row[:, :, :], 0.0))
            own.do(dve.memset(carry[:, 0:H], -BIG))
            own.do(dve.memset(top[:, :, 0:1], -BIG))
            own.do(dve.memset(any_first[:, :], 0.0))
            own.link(dve.memset(first_row[:, :, 0:1], 1.0))
            own.link(dve.tensor_copy(first_row[:, :, 1:1 + H], node[:, :, 20:24]))
            dve.nop(nofuse=True).then_inc(firsts_ready, 1)
            dve.wait_ge(s_bounds, 1)
            own.link(dve.tensor_scalar(bounds[:, :], bounds[:, :], m["width"][:, :], None, ALU.mult))
            for g in range(HI // 8):
                if g >= 2:
                    dve.wait_ge(over_used, g - 1)
                shape = [P, 8, P]
                cols = slice(8 * g, 8 * g + 8)
                b = bounds[:, :].unsqueeze(1).to_broadcast(shape)
                o = over[:, g % 2, :, :]
                tmp = feats[:, 0:8, :]
                own.do(dve.tensor_tensor(o, b, start[:, cols].unsqueeze(2).to_broadcast(shape), ALU.is_gt))
                own.link(dve.tensor_tensor(tmp, b, end[:, cols].unsqueeze(2).to_broadcast(shape), ALU.is_lt))
                own.do(dve.tensor_tensor(o, o, tmp, ALU.mult))
                own.wait()
                dve.nop(nofuse=True).then_inc(over_ready, 1)
            dve.wait_ge(over_used, HI // 8)
            own.link(dve.tensor_copy(target_in[:, :], target_ps[:, 0:H]))
            dve.sem_inc(consumed, 1)

            def turn(i):
                for q in range(2):
                    n = 2 * i + q
                    first = firsts[:, q, :, :].rearrange("p t c -> p c t")
                    row = rows[:, q, :, :].rearrange("p t c -> p c t")
                    st = state[:, q, :, :].rearrange("p t c -> p c t")
                    flat = lambda ap, k: ap[:, k:k + 1, :].rearrange("p o t -> p (o t)")
                    dve.wait_ge(firsts_in[q], 16 * (i + 1))
                    own.do(dve.tensor_scalar(inside[:, :], flat(first, 0), -1.0, 1.0, ALU.mult, ALU.add))
                    own.do(dve.tensor_scalar(reset[:, :], flat(first, 0), -BIG, None, ALU.mult))
                    own.link(dve.reduce_max(some[:, :], flat(first, 0), AX.X))
                    own.do(dve.tensor_tensor(any_first[:, :], any_first[:, :], some[:, :], ALU.max))
                    for h in range(H):
                        own.do(dve.tensor_tensor_scan(target[:, h, :], inside[:, :], flat(first, 1 + h),
                                                      target_in[:, h:h + 1], ALU.mult, ALU.add))
                    own.wait()
                    own.link(dve.tensor_copy(target_in[:, :], target[:, :, CHUNK - 1:CHUNK].rearrange("p h o -> p (h o)")))
                    dve.wait_ge(gathered[q], 16 * CHUNK * (i + 1))
                    own.link(dve.tensor_tensor(score[:, :, :], row[:, 16:20, :], target[:, :, :], ALU.add))
                    own.link(dve.scalar_tensor_tensor(leaky[:, :, :], score[:, :, :], 0.2, score[:, :, :],
                                                      ALU.mult, ALU.max))
                    for h in range(H):
                        own.do(dve.tensor_tensor_scan(top[:, h, 1:], reset[:, :], leaky[:, h, :], top[:, h, 0:1],
                                                      ALU.add, ALU.max))
                    own.wait()
                    own.link(dve.tensor_tensor(keep[:, :, :], top[:, :, 0:CHUNK], top[:, :, 1:], ALU.subtract))
                    dve.tensor_scalar(keep[:, :, :], keep[:, :, :], 0.0, None, ALU.min).then_inc(exp_in, 1)
                    dve.tensor_tensor(weight[:, :, :], leaky[:, :, :], top[:, :, 1:], ALU.subtract).then_inc(exp_in, 1)
                    dve.wait_ge(exp_out, 2 * n + 1)
                    own.do(dve.tensor_tensor(keep[:, :, :], keep[:, :, :],
                                             inside[:, :].unsqueeze(1).to_broadcast([P, H, CHUNK]), ALU.mult))
                    dve.wait_ge(exp_out, 2 * n + 2)
                    own.link(dve.tensor_tensor(
                        feats[:, :, :].rearrange("p (h e) t -> p h e t", h=H),
                        row[:, 0:16, :].rearrange("p (h e) t -> p h e t", h=H),
                        weight[:, :, :].unsqueeze(2).to_broadcast([P, H, 4, CHUNK]), ALU.mult))
                    wait(dve, stored[q], 16 * i)
                    for k in range(16):
                        own.do(dve.tensor_tensor_scan(flat(st, H + k), keep[:, k // 4, :], feats[:, k, :],
                                                      carry[:, H + k:H + k + 1], ALU.mult, ALU.add))
                    for h in range(H):
                        own.do(dve.tensor_tensor_scan(flat(st, 20 + h), keep[:, h, :], weight[:, h, :],
                                                      carry[:, 20 + h:21 + h], ALU.mult, ALU.add))
                    own.link(dve.tensor_copy(st[:, 0:H, :], top[:, :, 1:]))
                    dve.tensor_copy(carry[:, :], state[:, q, CHUNK - 1, :]).then_inc(state_ready, 1)
                    own.link(dve.tensor_copy(top[:, :, 0:1], top[:, :, CHUNK:CHUNK + 1]))
                    dve.wait_ge(state_ready, n + 1)
                    dve.sem_inc(consumed, 1)
            used = dve.value_load(m["turns_used"][0:1, 0:1], min_val=1, max_val=TURNS)
            turn(0)
            with dve.Fori(1, TURNS) as i, dve.If(i < used):
                own.enter(i - 1, EDGE_LINKS)
                turn(i)
                dve.nop(nofuse=True)
            own.leave(used - 1)
            K = 2 * used
            own.link(dve.memset(ends[:, :, :], 0.0))
            own.do(dve.tensor_copy(ends[:, 0, 0:20], carry[:, H:24]))
            own.do(dve.tensor_copy(ends[:, 1, 0:16].rearrange("p (h e) -> p h e", h=H),
                                   carry[:, 0:H].unsqueeze(2).to_broadcast([P, H, 4])))
            own.do(dve.tensor_copy(ends[:, 1, 16:20], carry[:, 0:H]))
            own.link(dve.tensor_copy(ends[:, 2, :], any_first[:, :].to_broadcast([P, CPAD])))
            dve.nop(nofuse=True).then_inc(ends_ready, 1)
            own.do(dve.memset(runT[:, 0, 0:1], 0.0))
            own.do(dve.memset(runT[:, 1, 0:1], -BIG))
            dve.wait_ge(ends_T, 1)
            own.link(dve.tensor_copy(endsT[:, :, :].rearrange("c a p -> c (a p)"), ends_ps[0:CPAD, 0:3 * P]))
            own.do(dve.tensor_scalar(insideT[:, :], endsT[:, 2, :], -1.0, 1.0, ALU.mult, ALU.add))
            own.link(dve.tensor_scalar(resetT[:, :], endsT[:, 2, :], -BIG, None, ALU.mult))
            own.link(dve.tensor_tensor_scan(runT[:, 1, 1:], resetT[:, :], endsT[:, 1, :], -BIG, ALU.add, ALU.max))
            own.link(dve.tensor_tensor(keepT[:, :], runT[:, 1, 0:P], runT[:, 1, 1:], ALU.subtract))
            dve.tensor_scalar(keepT[:, :], keepT[:, :], 0.0, None, ALU.min).then_inc(exp_in, 1)
            dve.tensor_tensor(weightT[:, :], endsT[:, 1, :], runT[:, 1, 1:], ALU.subtract).then_inc(exp_in, 1)
            dve.wait_ge(exp_out, 2 * K + 2)
            own.do(dve.tensor_tensor(keepT[:, :], keepT[:, :], insideT[:, :], ALU.mult))
            own.link(dve.tensor_tensor(weightT[:, :], weightT[:, :], endsT[:, 0, :], ALU.mult))
            own.link(dve.tensor_tensor_scan(runT[:, 0, 1:], keepT[:, :], weightT[:, :], 0.0, ALU.mult, ALU.add))
            dve.nop(nofuse=True).then_inc(run_ready, 1)
            dve.wait_ge(run_T, 1)
            dve.tensor_copy(carried[:, :, :].rearrange("p a c -> p (a c)"), back_ps[:, 0:2 * CPAD])\
                .then_inc(carried_ready, 1)

def node_gates(nc, io, m):
    sb, ps, sem = m["sb"], m["ps"], m["sem"]
    node, start, degree, gate = m["node"], m["start"], m["degree"], m["gate"]
    H, E = 4, 4
    with ExitStack() as c:
        last_place, last_part = sb("last_place", [P, HI], I32, c), sb("last_part", [P, HI], I32, c)
        state, carried = sb("node_state", [P, HI, NCH], F32, c), sb("node_carried", [P, HI, 2 * CPAD], F32, c)
        some, crossing, edge, in_part = (
            sb(n, [P, HI], F32, c) for n in ("has_edges", "crossing", "edge_place", "edge_part"))
        own_score, m_here, m_carried, m_all, tmp = (sb(n, [P, HI, H], F32, c) for n in
                                                    ("own_score", "m_here", "m_carried", "m_all", "tmp_heads"))
        weights = sb("part_weights", [P, 3, HI, H], F32, c)
        sums, tmp16 = sb("sums", [P, HI, 16], F32, c), sb("tmp16", [P, HI, 16], F32, c)
        denom = sb("denom", [P, HI, H], F32, c)
        mean, var, std = (sb(n, [P, HI], F32, c) for n in ("mean16", "var16", "std16"))
        gat = sb("gat_rows", [P, 3, 16], F32, c)
        scores, coded, first, second = (sb(n, [P, HI, E], F32, c) for n in ("scores", "coded", "first", "second"))
        rank = sb("rank", [P, E], F32, c)
        best, next_best, odds, denom2 = (sb(n, [P, HI], F32, c) for n in ("best", "next_best", "odds", "denom2"))
        eps = sb("eps_gat", [P, 1], F32, c)
        s_dve, places, s_rows, s_carried, s_gat, s_rank, exp_in, exp_out, var_ready, std_ready = (
            sem(n, c) for n in ("gate_chain", "places_ready", "state_gathered", "carried_gathered", "gat_in",
                                "rank_ready", "gate_exp_in", "gate_exp_out", "var16_ready", "std16_ready"))
        c.callback(m["clear"])
        block = c.enter_context(nc.Block())

        @block.gpsimd
        def _(pool):
            pool.iota(rank[:, :], [[-1, E]], base=E, channel_multiplier=0,
                      allow_small_or_imprecise_dtypes=True).then_inc(s_rank, 1)
            pool.wait_ge(places, 1)
            for h in range(HI):
                pool.indirect_dma_start(
                    out=state[:, h, :], out_offset=None, in_=m["running"],
                    in_offset=bass.IndirectOffsetOnAxis(ap=last_place[:, h:h + 1], axis=0)).then_inc(s_rows, 16)
                pool.indirect_dma_start(
                    out=carried[:, h, :], out_offset=None, in_=m["carried_in"],
                    in_offset=bass.IndirectOffsetOnAxis(ap=last_part[:, h:h + 1], axis=0)).then_inc(s_carried, 16)

        @block.sync
        def _(sp):
            sp.dma_start(gat[:, :, :], io["gat_rows"]).then_inc(s_gat, 16)

        @block.scalar
        def _(act):
            act.wait_ge(exp_in, 1)
            act.activation(weights[:, :, :, :], weights[:, :, :, :], ACT.Exp).then_inc(exp_out, 1)
            act.wait_ge(var_ready, 1)
            act.activation(std[:, :], var[:, :], ACT.Sqrt, bias=eps[:, :], scale=1.0 / 16).then_inc(std_ready, 1)
            act.wait_ge(exp_in, 2)
            act.activation(odds[:, :], odds[:, :], ACT.Exp).then_inc(exp_out, 1)

        @block.vector
        def _(dve):
            own = Steps(dve, s_dve)
            tt = lambda out, a, b, op: own.link(dve.tensor_tensor(out, a, b, op))
            ts = lambda out, a, s1, s2, op0, op1=None: own.link(
                dve.tensor_scalar(out, a, s1, s2, op0, op1) if op1 is not None else dve.tensor_scalar(out, a, s1, s2, op0))
            over_heads = lambda ap: ap.unsqueeze(2).to_broadcast([P, HI, H])
            by_head = lambda ap: ap.unsqueeze(3).to_broadcast([P, HI, H, 4])
            split = lambda ap: ap.rearrange("p n (h e) -> p n h e", h=H)
            own.link(dve.memset(eps[:, :], 1e-5))
            tt(edge[:, :], start[:, :], degree[:, :], ALU.add)
            ts(edge[:, :], edge[:, :], -1.0, 0.0, ALU.add, ALU.max)
            partition_of(dve, own, m, in_part[:, :], edge[:, :])
            own.link(dve.tensor_copy(last_part[:, :], in_part[:, :]))
            own.link(dve.scalar_tensor_tensor(last_place[:, :], in_part[:, :], m["width_gap"][:, :], edge[:, :],
                                              ALU.mult, ALU.add))
            dve.nop(nofuse=True).then_inc(places, 1)
            ts(some[:, :], degree[:, :], 0.0, None, ALU.is_gt)
            ts(crossing[:, :], in_part[:, :], m["width"][:, :], None, ALU.mult)
            tt(crossing[:, :], crossing[:, :], start[:, :], ALU.is_gt)
            tt(crossing[:, :], crossing[:, :], some[:, :], ALU.mult)
            tt(own_score[:, :, :], node[:, :, 16:20], node[:, :, 20:24], ALU.add)
            own.link(dve.scalar_tensor_tensor(own_score[:, :, :], own_score[:, :, :], 0.2, own_score[:, :, :],
                                              ALU.mult, ALU.max))
            dve.wait_ge(s_rows, 16 * HI)
            dve.wait_ge(s_carried, 16 * HI)
            for out, mask, part in ((m_here, some, state[:, :, 0:H]),
                                    (m_carried, crossing, carried[:, :, CPAD + 16:CPAD + 20])):
                tt(out[:, :, :], part, over_heads(mask[:, :]), ALU.mult)
                ts(tmp[:, :, :], over_heads(mask[:, :]), -1.0, BIG, ALU.add, ALU.mult)
                tt(out[:, :, :], out[:, :, :], tmp[:, :, :], ALU.add)
            tt(m_all[:, :, :], m_here[:, :, :], m_carried[:, :, :], ALU.max)
            tt(m_all[:, :, :], m_all[:, :, :], own_score[:, :, :], ALU.max)
            for a, part in enumerate((m_here, m_carried, own_score)):
                tt(weights[:, a, :, :], part[:, :, :], m_all[:, :, :], ALU.subtract)
            dve.nop(nofuse=True).then_inc(exp_in, 1)
            dve.wait_ge(exp_out, 1)
            tt(weights[:, 0, :, :], weights[:, 0, :, :], over_heads(some[:, :]), ALU.mult)
            tt(weights[:, 1, :, :], weights[:, 1, :, :], over_heads(crossing[:, :]), ALU.mult)
            tt(split(sums[:, :, :]), split(node[:, :, 0:16]), by_head(weights[:, 2, :, :]), ALU.mult)
            own.link(dve.tensor_copy(denom[:, :, :], weights[:, 2, :, :]))
            for a, s16, s4 in ((0, state[:, :, 4:20], state[:, :, 20:24]), (1, carried[:, :, 0:16], carried[:, :, 16:20])):
                tt(split(tmp16[:, :, :]), split(s16), by_head(weights[:, a, :, :]), ALU.mult)
                tt(sums[:, :, :], sums[:, :, :], tmp16[:, :, :], ALU.add)
                tt(tmp[:, :, :], s4, weights[:, a, :, :], ALU.mult)
                tt(denom[:, :, :], denom[:, :, :], tmp[:, :, :], ALU.add)
            ts(denom[:, :, :], denom[:, :, :], 1e-16, None, ALU.add)
            own.link(dve.reciprocal(denom[:, :, :], denom[:, :, :]))
            tt(split(sums[:, :, :]), split(sums[:, :, :]), by_head(denom[:, :, :]), ALU.mult)
            row = lambda a: gat[:, a, :].unsqueeze(1).to_broadcast([P, HI, 16])
            over16 = lambda ap: ap.unsqueeze(2).to_broadcast([P, HI, 16])
            dve.wait_ge(s_gat, 16)
            tt(sums[:, :, :], sums[:, :, :], row(0), ALU.add)
            own.link(dve.tensor_reduce(mean[:, :], sums[:, :, :], AX.X, ALU.add))
            ts(mean[:, :], mean[:, :], 1.0 / 16, None, ALU.mult)
            tt(sums[:, :, :], sums[:, :, :], over16(mean[:, :]), ALU.subtract)
            tt(tmp16[:, :, :], sums[:, :, :], sums[:, :, :], ALU.mult)
            own.link(dve.tensor_reduce(var[:, :], tmp16[:, :, :], AX.X, ALU.add))
            dve.nop(nofuse=True).then_inc(var_ready, 1)
            dve.wait_ge(std_ready, 1)
            own.link(dve.reciprocal(std[:, :], std[:, :]))
            tt(sums[:, :, :], sums[:, :, :], over16(std[:, :]), ALU.mult)
            tt(sums[:, :, :], sums[:, :, :], row(1), ALU.mult)
            tt(sums[:, :, :], sums[:, :, :], row(2), ALU.add)
            own.link(dve.tensor_reduce(scores[:, :, :], sums[:, :, :].rearrange("p n (h e) -> p n e h", h=H), AX.X, ALU.add))
            ts(scores[:, :, :], scores[:, :, :], 1.0 / H, None, ALU.mult)
            dve.wait_ge(s_rank, 1)
            over_e = lambda ap: ap.unsqueeze(2).to_broadcast([P, HI, E])

            def take_best(value, hot):
                own.link(dve.tensor_reduce(value[:, :], scores[:, :, :], AX.X, ALU.max))
                tt(coded[:, :, :], scores[:, :, :], over_e(value[:, :]), ALU.is_equal)
                tt(coded[:, :, :], coded[:, :, :], rank[:, :].unsqueeze(1).to_broadcast([P, HI, E]), ALU.mult)
                own.link(dve.tensor_reduce(denom2[:, :], coded[:, :, :], AX.X, ALU.max))
                tt(hot[:, :, :], coded[:, :, :], over_e(denom2[:, :]), ALU.is_equal)

            take_best(best, first)
            own.link(dve.scalar_tensor_tensor(scores[:, :, :], first[:, :, :], -BIG, scores[:, :, :], ALU.mult, ALU.add))
            take_best(next_best, second)
            tt(odds[:, :], next_best[:, :], best[:, :], ALU.subtract)
            dve.nop(nofuse=True).then_inc(exp_in, 1)
            dve.wait_ge(exp_out, 2)
            ts(denom2[:, :], odds[:, :], 1.0, None, ALU.add)
            own.link(dve.reciprocal(denom2[:, :], denom2[:, :]))
            tt(odds[:, :], odds[:, :], denom2[:, :], ALU.mult)
            tt(first[:, :, :], first[:, :, :], over_e(denom2[:, :]), ALU.mult)
            tt(second[:, :, :], second[:, :, :], over_e(odds[:, :]), ALU.mult)
            tt(gate[:, :, :], first[:, :, :], second[:, :, :], ALU.add)


def later_layers(nc, io, m):
    sb, ps, sem = m["sb"], m["ps"], m["sem"]
    ident, ones, gate, x_all = m["ident"], m["ones"], m["gate"], m["x_all"]
    HEADS, TOP, KEYS, RING, HALF = 8, 16, 128, 32, 8
    MHA_HEADS, HID, EXP0, EXP2 = 8, 2 * D, 4, 8
    HOPS = 4 * (HEADS + 1)
    with ExitStack() as c:
        def tiles(names, shape, dt=F32):
            return [sb(n, shape, dt, c) for n in names.split()]

        moe0_w1, moe0_w2 = sb("moe0_w1", [P, EXP0, HID], F32, c), sb("moe0_w2", [P, EXP0, 2, D], F32, c)
        moe0_b1, moe0_b2 = sb("moe0_b1", [P, EXP0 * 2], F32, c), sb("moe0_b2", [1, EXP0 * D], F32, c)
        wq, wk, wv, wo = tiles("mha_wq mha_wk mha_wv mha_wo", [P, D])
        edge_w = sb("edge_w", [P, MHA_HEADS * P], F32, c)
        w_e = sb("w_e", [P, MHA_HEADS], F32, c)
        head_mask = sb("head_mask", [P, MHA_HEADS], F32, c)
        wi, ws = sb("route_wi", [P, HID], F32, c), sb("route_ws", [P, 4, HID], F32, c)
        bi, bs = sb("route_bi", [P, 2], F32, c), sb("route_bs", [P, 4], F32, c)
        w_out, b_out = sb("route_wo", [P, 2, D], F32, c), sb("route_bo", [1, D], F32, c)
        routed = sb("routed", [P, 4, HID + 1], F32, c)
        routed_rows = sb("routed_rows", [P, B, 4], I32, c)
        routed_index = sb("routed_index", [P, 4], I32, c)
        gcn_w, gcn_b, alpha = sb("gcn_w", [P, D], F32, c), sb("gcn_b", [P, D], F32, c), sb("alpha", [P, 1], F32, c)
        moe2_w1, moe2_w2 = sb("moe2_w1", [P, EXP2, HID], F32, c), sb("moe2_w2", [P, EXP2, 2, D], F32, c)
        moe2_b1, moe2_b2 = sb("moe2_b1", [P, EXP2 * 2], F32, c), sb("moe2_b2", [1, EXP2 * D], F32, c)
        gamma, beta = tiles("gamma beta", [P, D])
        wr, br = sb("moe2_wr", [P, EXP2], F32, c), sb("moe2_br", [1, EXP2], F32, c)
        gin_w1, gin_w2 = sb("gin_w1", [P, HID], F32, c), sb("gin_w2", [P, 2, D], F32, c)
        gin_b1, gin_b2 = sb("gin_b1", [P, 2], F32, c), sb("gin_b2", [1, D], F32, c)
        eps_gin, eps1_ident = sb("eps_gin", [P, 1], F32, c), sb("eps1_ident", [P, P], F32, c)
        w_sim = sb("w_sim", [P, 4, 4 * KEYS], F32, c)
        mem_wq, mem_wo = sb("mem_wq", [P, HEADS * D], F32, c), sb("mem_wo", [P, HEADS, D], F32, c)
        causal = sb("causal", [P, P], F32, c)
        count16 = sb("count16", [P, TOP], F32, c)
        head_base = sb("head_base", [P, HEADS * TOP], F32, c)
        eps_ln = sb("eps_ln", [P, 1], F32, c)
        s_const, s_made, s_folded, s_weights, s_simple = (sem(n, c) for n in (
            "const4", "made4", "folded4", "weights4", "setup4"))

        loads = [(moe0_w1, "moe0_w1"), (moe0_w2, "moe0_w2"), (moe0_b1, "moe0_b1"), (moe0_b2, "moe0_b2"),
                 (wq, "mha_wq"), (wk, "mha_wk"), (wv, "mha_wv"), (wo, "mha_wo"), (w_e, "w_e"),
                 (wi, "route_wi"), (ws, "route_ws"), (bi, "route_bi"), (bs, "route_bs"),
                 (w_out, "route_wo"), (b_out, "route_bo"), (gcn_w, "gcn_w"), (gcn_b, "gcn_b"), (alpha, "alpha"),
                 (moe2_w1, "moe2_w1"), (moe2_w2, "moe2_w2"), (moe2_b1, "moe2_b1"), (moe2_b2, "moe2_b2"),
                 (gamma, "gamma"), (beta, "beta"), (wr, "moe2_wr"), (br, "moe2_br"),
                 (gin_w1, "gin_w1"), (gin_w2, "gin_w2"), (gin_b1, "gin_b1"), (gin_b2, "gin_b2"),
                 (eps_gin, "eps_gin"), (mem_wq, "mem_wq"), (mem_wo, "mem_wo")]

        with ExitStack() as c2:
            wqT, keysT = sb("wqT", [64, 16, P], F32, c2), sb("keysT", [64, 16, KEYS], F32, c2)
            route = sb("route", [P, B], I32, c2)
            route_f, bad = sb("route_f", [P, B], F32, c2), sb("bad", [P, B], F32, c2)
            row_base = sb("row_base", [P, 4], F32, c2)
            rows_f = sb("rows_f", [P, B, 4], F32, c2)
            fold_ps = [ps(f"fold_ps{j}", [P, 4 * KEYS], F32, c2) for j in range(4)]
            block = c2.enter_context(nc.Block())

            @block.sync
            def _(sp):
                for dst, name in loads + [(wqT, "wqT"), (keysT, "keysT"), (route, "route")]:
                    sp.dma_start(dst[tuple([slice(None)] * len(dst.shape))], io[name]).then_inc(s_weights, 16)
                sp.wait_ge(s_weights, 16 * (len(loads) + 3))

            @block.gpsimd
            def _(pool):
                pool.memset(causal[:, :], 0.0).then_inc(s_const, 1)
                pool.iota(count16[:, :], [[1, TOP]], base=0, channel_multiplier=0,
                          allow_small_or_imprecise_dtypes=True).then_inc(s_const, 1)
                pool.iota(row_base[:, :], [[17 * HID, 2], [P, 2]], base=0, channel_multiplier=1,
                          allow_small_or_imprecise_dtypes=True).then_inc(s_const, 1)
                pool.iota(head_base[:, :], [[KEYS * KEYS, HEADS], [0, TOP]], base=0, channel_multiplier=0,
                          allow_small_or_imprecise_dtypes=True).then_inc(s_const, 1)
                pool.wait_ge(s_const, 4)
                pool.affine_select(out=causal[:, :], in_=causal[:, :], compare_op=ALU.is_ge, fill=-BIG, base=0,
                                   pattern=[[-1, P]], channel_multiplier=1).then_inc(s_const, 1)
                pool.affine_select(out=head_mask[:, :], in_=ones[:, 0:MHA_HEADS], compare_op=ALU.is_ge, fill=0.0,
                                   base=0, pattern=[[-16, MHA_HEADS]], channel_multiplier=1).then_inc(s_const, 1)
                pool.wait_ge(s_const, 6)
                pool.affine_select(out=head_mask[:, :], in_=head_mask[:, :], compare_op=ALU.is_ge, fill=0.0,
                                   base=15, pattern=[[16, MHA_HEADS]], channel_multiplier=-1).then_inc(s_const, 1)
                pool.wait_ge(s_const, 7)

            @block.tensor
            def _(pe):
                pe.wait_ge(s_weights, 16 * (len(loads) + 3))
                for j in range(16):
                    last = pe.matmul(fold_ps[j // 4][:, (j % 4) * KEYS:(j % 4 + 1) * KEYS], wqT[:, j, :], keysT[:, j, :],
                                     start=True, stop=True)
                last.then_inc(s_folded, 1)

            @block.vector
            def _(dve):
                own = Steps(dve, s_simple)
                own.do(dve.memset(eps_ln[:, :], 1e-5))
                dve.wait_ge(s_weights, 16 * (len(loads) + 3))
                own.do(dve.tensor_tensor(edge_w[:, :].rearrange("p (h j) -> p h j", h=MHA_HEADS),
                                         ident[:, :].unsqueeze(1).to_broadcast([P, MHA_HEADS, P]),
                                         w_e[:, :].unsqueeze(2).to_broadcast([P, MHA_HEADS, P]), ALU.mult))
                own.link(dve.tensor_scalar(eps_gin[:, :], eps_gin[:, :], 1.0, None, ALU.add))
                own.do(dve.tensor_scalar(eps1_ident[:, :], ident[:, :], eps_gin[:, :], None, ALU.mult))
                own.link(dve.tensor_scalar(bad[:, :], route[:, :], 0.0, 1.0e9, ALU.is_lt, ALU.mult))
                own.link(dve.tensor_tensor(route_f[:, :], route[:, :], bad[:, :], ALU.add))
                own.link(dve.tensor_scalar(route_f[:, :], route_f[:, :], 16.0, float(HID), ALU.min, ALU.mult))
                dve.wait_ge(s_const, 7)
                own.link(dve.tensor_tensor(routed_rows[:, :, :], route_f[:, :].unsqueeze(2).to_broadcast([P, B, 4]),
                                           row_base[:, :].unsqueeze(1).to_broadcast([P, B, 4]), ALU.add))
                dve.wait_ge(s_folded, 1)
                for j in range(4):
                    own.link(dve.tensor_copy(w_sim[:, j, :], fold_ps[j][:, :]))

        x, z, zn, zT, xo, x_cur, zH, zH_next, adjT = tiles("x z zn zT xo x_cur zH zH_next adjT", [P, D])
        stats, mv = sb("stats", [P, 6], F32, c), sb("mv", [P, 2], F32, c)
        std, rstd, row_sum, row_std, row_scale = tiles("std rstd row_sum row_std row_scale", [P, 1])
        hT = sb("hT", [P, 2, HID], F32, c)
        qT, v_mha, o_mha, oT = tiles("qT v_mha o_mha oT", [P, D])
        k_heads = sb("k_heads", [P, MHA_HEADS * P], F32, c)
        absent = sb("absent_edges", [P, P], F32, c)
        neg_max, sums, inv = tiles("neg_max sums inv", [P, MHA_HEADS])
        e_mha, eT_mha = tiles("e_mha eT_mha", [P, MHA_HEADS * P])
        h_a, h_b = tiles("h_a h_b", [P, HID])
        bias_sum = sb("bias_sum", [P, 4], F32, c)
        za = sb("za", [P, D], F32, c)
        aT = sb("aT", [P, D], F32, c)
        relu_in = sb("relu_in", [P, D], F32, c)
        logits, top8, w_exp, hot = tiles("logits top8 w_exp hot", [P, EXP2])
        top8_i = sb("top8_i", [P, EXP2], mybir.dt.uint32, c)
        top8_f = sb("top8_f", [P, EXP2], F32, c)
        odds, w_best, w_next = tiles("odds4 w_best w_next", [P, 1])
        vals = sb("vals", [P, 4, TOP], F32, c)
        vals_i = sb("vals_i", [P, 4, TOP], mybir.dt.uint32, c)
        vals_f = sb("vals_f", [P, 4, TOP], F32, c)
        sims = sb("sims", [P, 4, 4 * KEYS], F32, c)
        rest = sb("rest", [P, 4 * KEYS], F32, c)
        pair_sum, pair_rest = tiles("pair_sum pair_rest", [P, 2 * TOP * TOP])
        best = sb("best16", [P, 2, TOP], F32, c)
        best_i = sb("best_i", [P, 2, TOP], mybir.dt.uint32, c)
        digit = sb("digit", [P, 2, TOP], mybir.dt.uint32, c)
        digit_f = sb("digit_f", [P, 2, TOP], F32, c)
        found = sb("found", [P, 2, 2, TOP], F32, c)
        soft, soft_sum = sb("soft", [P, 2, TOP], F32, c), sb("soft_sum", [P, 2], F32, c)
        index_next, index = sb("index_next", [P, HEADS * TOP], I32, c), sb("index4", [P, HEADS * TOP], I32, c)
        mem_w_next, mem_w = tiles("mem_w_next mem_w", [P, HEADS * TOP])
        ring = sb("ring", [P, RING, 2 * D], F32, c)
        diag = sb("diag", [P, 2, HALF * P], F32, c)
        kT, v_mem, qT_mem, masked, e_mem, eT_mem, oT_mem = tiles("kT v_mem qT_mem masked e_mem eT_mem oT_mem", [P, D])
        m_mem, sum_mem, inv_mem = tiles("m_mem sum_mem inv_mem", [P, 1])
        small = ps("small4", [P, 512], F32, c)
        wide = [ps(f"wide{j}", [P, 512], F32, c) for j in range(4)]
        att_ps, kT_ps, v_ps = ps("att_ps", [P, 512], F32, c), ps("kT_ps", [P, 512], F32, c), ps("v_ps", [P, 512], F32, c)
        zT_ps, y_ps, aT_ps, misc_ps = (small[:, j * D:(j + 1) * D] for j in range(4))

        names = ("adj_in var std z zT_made zT h_made y_made y_used qkv_made q_v_ready k_ready scores_made "
                 "max_ready exp_ready eT_made eT_act eT_dve o_made o_ready oT_made oT_ready y "
                 "route_h route_relu route_bias row_sum_made row_sum_ready row_std_ready conv_z conv_made conv_ready "
                 "logits_made odds_in odds_out gin_h gin_relu sims_made sims_copied soft_in soft_out chosen "
                 "zH_ready zH_kept diag_ready diag2_ready mem_w diag_used rows_used kv_ready q_made q_ready sim_made sim_max "
                 "exp_mem eT_mem_made eT_mem_ready out_made out_ready out_y acc_made stored out_tile routed_in "
                 "routed_used routed_copied index_copied gelu_done own")
        S = {n: sem("l_" + n, c) for n in names.split()}
        rows_in = [sem(f"rows_in{j}", c) for j in range(4)]
        block = c.enter_context(nc.Block())

        def run(eng, body, own=None, links=0):
            turns(eng, B, lambda b: body(b, True, not isinstance(b, int) or b > 0, not isinstance(b, int) or b > 1),
                  own, links, peeled=3)
            body(B, False, True, True)
            body(B + 1, False, False, True)

        def hop_by_hop(front, choice, back):
            for hop in range(HOPS):
                if front:
                    assert next(front, "end") != "end"
                if back:
                    back(hop // 4, hop % 4)
                if choice and 1 <= hop <= 20:
                    choice((hop - 1) // 5, (hop - 1) % 5)
            assert not front or next(front, "end") == "end"

        @block.sync
        def _(sp):
            def body(b, front, choice, back):
                if front:
                    wait(sp, S["conv_made"], 2 * b)
                    sp.dma_start(adjT[:, :], io["adjT"][bass.ds(b, 1), :, :].rearrange("o n d -> (o n) d"))\
                        .then_inc(S["adj_in"], 16)
                if back:
                    wait(sp, S["out_tile"], b - 1)
                    sp.dma_start(io["out"][bass.ds(b - 2, 1), :, :].rearrange("o n d -> (o n) d"), xo[:, :])\
                        .then_inc(S["stored"], 16)
            run(sp, body)
            sp.wait_ge(S["stored"], 16 * B)

        @block.gpsimd
        def _(pool):
            def body(b, front, choice, back):
                if front:
                    wait(pool, S["routed_used"], b)
                    pool.nop(nofuse=True)
                    pool.tensor_copy(routed_index[:, :], routed_rows[:, bass.ds(b, 1), :].rearrange("p o k -> p (o k)"))\
                        .then_inc(S["routed_copied"], 1)
                    wait(pool, S["routed_copied"], b + 1)
                    pool.nop(nofuse=True)
                    for k in range(4):
                        pool.indirect_dma_start(
                            out=routed[:, k, :], out_offset=None, in_=io["route_wr"],
                            in_offset=bass.IndirectOffsetOnAxis(ap=routed_index[:, k:k + 1], axis=0))\
                            .then_inc(S["routed_in"], 16)
                if back:
                    wait(pool, S["chosen"], b - 1)
                    for j in range(4):
                        wait(pool, rows_in[j], 16 * TOP * 2 * (b - 2))
                    pool.nop(nofuse=True)
                    pool.tensor_copy(index[:, :], index_next[:, :]).then_inc(S["index_copied"], 1)
                    wait(pool, S["index_copied"], b - 1)
                    pool.nop(nofuse=True)
                    for h in range(HEADS):
                        n = HEADS * (b - 2) + h
                        wait(pool, S["rows_used"], n - 1)
                        pool.nop(nofuse=True)
                        for k in range(TOP):
                            pool.indirect_dma_start(
                                out=ring[:, (h % 2) * TOP + k, :], out_offset=None, in_=io["memory"],
                                in_offset=bass.IndirectOffsetOnAxis(ap=index[:, h * TOP + k:h * TOP + k + 1], axis=0))\
                                .then_inc(rows_in[h % 4], 16)
            run(pool, body)

        @block.tensor
        def _(pe):
            def transpose_z(b, u, z_use, src):
                wait(pe, S["z"], 8 * b + z_use + 1)
                pe.transpose(zT_ps, src[:, :], ident[:, :]).then_inc(S["zT_made"], 1)
                yield
                wait(pe, S["zT"], 5 * b + u + 1)

            def bias_row(out, row):
                return pe.matmul(out, ones[0:1, :], row, start=False, stop=True)

            def experts(b, first, count, w1, w2, b2):
                for e in range(count + 1):
                    n = 12 * b + first + e
                    if e < count:
                        wait(pe, S["gelu_done"], n - 1)
                        for half in range(2):
                            last = pe.matmul(wide[e % 2][:, half * D:(half + 1) * D],
                                             w1[:, e, half * D:(half + 1) * D], zT[:, :], start=True, stop=True)
                        last.then_inc(S["h_made"], 1)
                    if e > 0:
                        p = e - 1
                        wait(pe, S["gelu_done"], n)
                        wait(pe, S["y_used"], n - 2)
                        y = wide[2 + p % 2][:, 0:D]
                        for half in range(2):
                            pe.matmul(y, hT[:, p % 2, half * D:(half + 1) * D], w2[:, p, half, :],
                                      start=(half == 0), stop=False)
                        bias_row(y, b2[:, p * D:(p + 1) * D]).then_inc(S["y_made"], 1)
                    yield

            def mha(b):
                wait(pe, S["adj_in"], 16 * (b + 1))
                yield from transpose_z(b, 1, 1, z)
                for j, (l, r) in enumerate(((wq, zT), (wk, zT), (zT, wv))):
                    out = wide[1][:, 0:D] if j == 1 else wide[0][:, j * D:(j + 1) * D]
                    last = pe.matmul(out, l[:, :], r[:, :], start=True, stop=True)
                last.then_inc(S["qkv_made"], 1)
                yield
                wait(pe, S["q_v_ready"], b + 1)
                wait(pe, S["k_ready"], b + 1)
                for j in range(2):
                    half = slice(j * 4 * P, (j + 1) * 4 * P)
                    pe.matmul(wide[2 + j][:, :], qT[:, :], k_heads[:, half], start=True, stop=False)
                    pe.matmul(wide[2 + j][:, :], adjT[:, :], edge_w[:, half], start=False, stop=False)
                    pe.matmul(wide[2 + j][:, :], absent[:, :], ident[:, :].unsqueeze(1).to_broadcast([P, 4, P]),
                              start=False, stop=True).then_inc(S["scores_made"], 1)
                yield
                for j in range(2):
                    wait(pe, S["exp_ready"], 2 * b + j + 1)
                    for h in range(4):
                        last = pe.transpose(wide[j][:, h * P:(h + 1) * P], e_mha[:, (4 * j + h) * P:(4 * j + h + 1) * P],
                                            ident[:, :])
                    last.then_inc(S["eT_made"], 1)
                yield
                wait(pe, S["eT_act"], b + 1)
                wait(pe, S["eT_dve"], b + 1)
                for h in range(MHA_HEADS):
                    last = pe.matmul(aT_ps[:, 16 * h:16 * h + 16], eT_mha[:, h * P:(h + 1) * P],
                                     v_mha[:, 16 * h:16 * h + 16], start=True, stop=True)
                last.then_inc(S["o_made"], 1)
                yield
                wait(pe, S["o_ready"], b + 1)
                pe.transpose(misc_ps, o_mha[:, :], ident[:, :]).then_inc(S["oT_made"], 1)
                yield
                wait(pe, S["oT_ready"], b + 1)
                pe.matmul(y_ps, oT[:, :], wo[:, :], start=True, stop=True).then_inc(S["y"], 1)
                yield

            def routed_ffn(b):
                yield from transpose_z(b, 2, 2, z)
                for o in range(2):
                    last = pe.matmul(wide[0][:, o * D:(o + 1) * D], wi[:, o * D:(o + 1) * D], zT[:, :],
                                     start=True, stop=True)
                last.then_inc(S["route_h"], 1)
                yield
                wait(pe, S["routed_in"], 64 * (b + 1))
                for l in range(2):
                    h = (h_a, h_b)[l]
                    wait(pe, S["route_relu"], 3 * b + l + 1)
                    for o in range(2):
                        cols = slice(o * D, (o + 1) * D)
                        out = wide[1 + l][:, cols]
                        for k in range(2):
                            hk = h[:, k * D:(k + 1) * D]
                            pe.matmul(out, ws[:, 2 * l + k, cols], hk, start=(k == 0), stop=False)
                            pe.matmul(out, routed[:, 2 * l + k, cols], hk, start=False, stop=False)
                        last = pe.matmul(out, ident[:, :], h[:, cols], start=False, stop=True)
                    last.then_inc(S["route_h"], 1)
                    yield
                wait(pe, S["route_relu"], 3 * b + 3)
                for k in range(2):
                    pe.matmul(y_ps, h_a[:, k * D:(k + 1) * D], w_out[:, k, :], start=(k == 0), stop=False)
                bias_row(y_ps, b_out[:, :]).then_inc(S["y"], 1)
                pe.matmul(wide[3][:, 0:1], adjT[:, :], ones[:, 0:1], start=True, stop=True)\
                    .then_inc(S["row_sum_made"], 1)
                yield

            def gcn(b):
                wait(pe, S["conv_z"], b + 1)
                pe.matmul(aT_ps, za[:, :], adjT[:, :], start=True, stop=False)
                pe.matmul(aT_ps, zn[:, :], ident[:, :], start=False, stop=True).then_inc(S["conv_made"], 1)
                yield
                wait(pe, S["conv_ready"], 2 * b + 1)
                pe.matmul(y_ps, aT[:, :], gcn_w[:, :], start=True, stop=True).then_inc(S["y"], 1)
                yield

            def gated_experts(b):
                yield from transpose_z(b, 3, 5, zn)
                pe.matmul(misc_ps[:, 0:EXP2], zT[:, :], wr[:, :], start=True, stop=False)
                bias_row(misc_ps[:, 0:EXP2], br[:, :]).then_inc(S["logits_made"], 1)
                yield from experts(b, 4, EXP2, moe2_w1, moe2_w2, moe2_b2)

            def gin(b):
                wait(pe, S["z"], 8 * b + 7)
                pe.matmul(aT_ps, z[:, :], adjT[:, :], start=True, stop=False)
                pe.matmul(aT_ps, z[:, :], eps1_ident[:, :], start=False, stop=True).then_inc(S["conv_made"], 1)
                yield
                wait(pe, S["conv_ready"], 2 * b + 2)
                for o in range(2):
                    last = pe.matmul(wide[0][:, o * D:(o + 1) * D], gin_w1[:, o * D:(o + 1) * D], aT[:, :],
                                     start=True, stop=True)
                last.then_inc(S["gin_h"], 1)
                yield
                wait(pe, S["gin_relu"], b + 1)
                for k in range(2):
                    pe.matmul(y_ps, h_a[:, k * D:(k + 1) * D], gin_w2[:, k, :], start=(k == 0), stop=False)
                bias_row(y_ps, gin_b2[:, :]).then_inc(S["y"], 1)
                yield

            def similarities(b):
                yield from transpose_z(b, 4, 7, z)
                for j in range(4):
                    pe.matmul(wide[j][:, :], zT[:, :], w_sim[:, j, :], start=True, stop=True)\
                        .then_inc(S["sims_made"], 1)
                yield

            def front(b):
                yield
                yield from transpose_z(b, 0, 0, z)
                wait(pe, S["sims_copied"], 4 * b)
                yield from experts(b, 0, EXP0, moe0_w1, moe0_w2, moe0_b2)
                for layer in (mha, routed_ffn, gcn, gated_experts, gin, similarities):
                    yield from layer(b)

            def gathered_products(n, h, k0):
                for k in range(k0, k0 + 4):
                    if k % HALF == 0:
                        wait(pe, S["diag2_ready" if k else "diag_ready"], n + 1)
                    row = ring[:, (h % 2) * TOP + k, :]
                    d = diag[:, k // HALF, (k % HALF) * P:(k % HALF + 1) * P]
                    pe.matmul(kT_ps[:, 0:D], row[:, 0:D], d, start=(k == 0), stop=(k == TOP - 1))
                    last = pe.matmul(v_ps[:, 0:D], d, row[:, D:2 * D], start=(k == 0), stop=(k == TOP - 1))
                    if k % HALF == HALF - 1:
                        last.then_inc(S["diag_used"], 1)

            def back(batch, h, q):
                n = HEADS * batch + h
                attend, weigh = h >= 1, h < HEADS
                if attend and q == 0:
                    wait(pe, S["kv_ready"], n)
                    wait(pe, S["q_ready"], n)
                    pe.matmul(att_ps[:, D:2 * D], qT_mem[:, :], kT[:, :], start=True, stop=True)\
                        .then_inc(S["sim_made"], 1)
                if attend and q == 1:
                    wait(pe, S["exp_mem"], n)
                    pe.transpose(att_ps[:, 2 * D:3 * D], e_mem[:, :], ident[:, :]).then_inc(S["eT_mem_made"], 1)
                if attend and q == 2:
                    wait(pe, S["eT_mem_ready"], n)
                    pe.matmul(att_ps[:, 3 * D:4 * D], v_mem[:, :], eT_mem[:, :], start=True, stop=True)\
                        .then_inc(S["out_made"], 1)
                if attend and q == 3:
                    wait(pe, S["out_ready"], n)
                    pe.matmul(att_ps[:, D:2 * D], oT_mem[:, :], mem_wo[:, h - 1, :], start=True, stop=True)\
                        .then_inc(S["out_y"], 1)
                if weigh and q == 3:
                    wait(pe, S["zH_ready"], batch + 1)
                    wait(pe, S["acc_made"], n if h == 0 else n - 1)
                    pe.matmul(att_ps[:, 0:D], mem_wq[:, h * D:(h + 1) * D], zH[:, :], start=True, stop=True)\
                        .then_inc(S["q_made"], 1)
                if weigh:
                    if q == 0:
                        pe.wait_ge(rows_in[h % 4], 16 * TOP * (2 * batch + h // 4 + 1))
                        wait(pe, S["kv_ready"], n)
                    gathered_products(n, h, 4 * q)
                    if q == 3:
                        pe.nop(nofuse=True)
                        wait(pe, S["diag_used"], 2 * n + 2)
                        pe.sem_inc(S["rows_used"], 1)

            def body(b, has_front, has_choice, has_back):
                hop_by_hop(has_front and front(b), None, has_back and (lambda h, q: back(b - 2, h, q)))
            run(pe, body)

        @block.scalar
        def _(act):
            def std_of(b, u):
                wait(act, S["var"], 8 * b + u + 1)
                act.activation(std[:, :], mv[:, 1:2], ACT.Sqrt, bias=eps_ln[:, :]).then_inc(S["std"], 1)

            def copy_zT(b, u):
                wait(act, S["zT_made"], 5 * b + u + 1)
                act.activation(zT[:, :], zT_ps, ACT.Copy).then_inc(S["zT"], 1)
                yield

            def gelu(b, first, e, b1):
                n = 12 * b + first + e
                wait(act, S["h_made"], n + 1)
                wait(act, S["y_made"], n - 1)
                for half in range(2):
                    last = act.activation(hT[:, e % 2, half * D:(half + 1) * D],
                                          wide[e % 2][:, half * D:(half + 1) * D], ACT.Gelu,
                                          bias=b1[:, 2 * e + half:2 * e + half + 1])
                last.then_inc(S["gelu_done"], 1)

            def mha(b):
                yield from copy_zT(b, 1)
                wait(act, S["qkv_made"], b + 1)
                act.activation(qT[:, :], wide[0][:, 0:D], ACT.Copy, scale=0.25)
                act.activation(v_mha[:, :], wide[0][:, 2 * D:3 * D], ACT.Copy).then_inc(S["q_v_ready"], 1)
                yield
                for j in range(2):
                    wait(act, S["max_ready"], 2 * b + j + 1)
                    for h in range(4):
                        g = 4 * j + h
                        last = act.activation(e_mha[:, g * P:(g + 1) * P], wide[2 + j][:, h * P:(h + 1) * P], ACT.Exp,
                                              bias=neg_max[:, g:g + 1], accum_out=sums[:, g:g + 1])
                    last.then_inc(S["exp_ready"], 1)
                yield
                wait(act, S["eT_made"], 2 * b + 1)
                act.activation(eT_mha[:, 0:4 * P], wide[0][:, :], ACT.Copy).then_inc(S["eT_act"], 1)
                yield
                yield
                wait(act, S["oT_made"], b + 1)
                act.activation(oT[:, :], misc_ps, ACT.Copy).then_inc(S["oT_ready"], 1)
                yield
                std_of(b, 2)
                yield

            def routed_ffn(b):
                yield from copy_zT(b, 2)
                for l in range(3):
                    wait(act, S["route_h"], 3 * b + l + 1)
                    if l == 1:
                        wait(act, S["route_bias"], b + 1)
                    for o in range(2):
                        bias = bi[:, o:o + 1] if l == 0 else bias_sum[:, 2 * (l - 1) + o:2 * (l - 1) + o + 1]
                        last = act.activation((h_a, h_b, h_a)[l][:, o * D:(o + 1) * D],
                                              wide[l][:, o * D:(o + 1) * D], ACT.Relu, bias=bias)
                    last.then_inc(S["route_relu"], 1)
                    yield
                std_of(b, 3)
                wait(act, S["row_sum_ready"], b + 1)
                act.activation(row_std[:, :], row_sum[:, :], ACT.Sqrt).then_inc(S["row_std_ready"], 1)
                yield

            def gcn(b):
                wait(act, S["conv_made"], 2 * b + 1)
                act.activation(aT[:, :], aT_ps, ACT.Copy).then_inc(S["conv_ready"], 1)
                yield
                std_of(b, 4)
                std_of(b, 5)
                yield

            def gated_experts(b):
                yield from copy_zT(b, 3)
                for e in range(EXP2):
                    gelu(b, 4, e, moe2_b1)
                    if e == 0:
                        wait(act, S["odds_in"], b + 1)
                        act.activation(odds[:, :], odds[:, :], ACT.Exp).then_inc(S["odds_out"], 1)
                    yield
                std_of(b, 6)
                yield

            def gin(b):
                wait(act, S["conv_made"], 2 * b + 2)
                act.activation(aT[:, :], aT_ps, ACT.Copy).then_inc(S["conv_ready"], 1)
                yield
                wait(act, S["gin_h"], b + 1)
                for o in range(2):
                    last = act.activation(h_a[:, o * D:(o + 1) * D], wide[0][:, o * D:(o + 1) * D], ACT.Relu,
                                          bias=gin_b1[:, o:o + 1])
                last.then_inc(S["gin_relu"], 1)
                yield
                std_of(b, 7)
                yield

            def similarities(b):
                yield from copy_zT(b, 4)
                wait(act, S["chosen"], b)
                for j in range(4):
                    wait(act, S["sims_made"], 4 * b + j + 1)
                    act.activation(sims[:, j, :], wide[j][:, :], ACT.Copy).then_inc(S["sims_copied"], 1)
                yield

            def front(b):
                std_of(b, 0)
                yield
                yield from copy_zT(b, 0)
                for e in range(EXP0):
                    gelu(b, 0, e, moe0_b1)
                    yield
                std_of(b, 1)
                yield
                for layer in (mha, routed_ffn, gcn, gated_experts, gin, similarities):
                    yield from layer(b)

            def soften(batch, j, part):
                if part == 3:
                    wait(act, S["soft_in"], 4 * batch + j + 1)
                    act.activation(soft[:, :, :], soft[:, :, :], ACT.Exp).then_inc(S["soft_out"], 1)

            def back(batch, h, q):
                n = HEADS * batch + h
                attend, weigh = h >= 1, h < HEADS
                if attend and q == 0:
                    wait(act, S["sim_max"], n)
                    act.activation(e_mem[:, :], masked[:, :], ACT.Exp, bias=m_mem[:, :], accum_out=sum_mem[:, :])\
                        .then_inc(S["exp_mem"], 1)
                if weigh and q == 0:
                    wait(act, S["diag_used"], 2 * n)
                    wait(act, S["mem_w"], batch + 1)
                    for k in range(HALF, TOP):
                        last = act.activation(diag[:, 1, (k - HALF) * P:(k - HALF + 1) * P], ident[:, :], ACT.Copy,
                                              scale=mem_w[:, h * TOP + k:h * TOP + k + 1])
                    last.then_inc(S["diag2_ready"], 1)
                if attend and q == 1:
                    wait(act, S["eT_mem_made"], n)
                    act.activation(eT_mem[:, :], att_ps[:, 2 * D:3 * D], ACT.Copy).then_inc(S["eT_mem_ready"], 1)
                if attend and q == 2:
                    wait(act, S["out_made"], n)
                    act.activation(oT_mem[:, :], att_ps[:, 3 * D:4 * D], ACT.Copy).then_inc(S["out_ready"], 1)
                if weigh and q == 3:
                    wait(act, S["acc_made"], n)
                    wait(act, S["q_made"], n + 1)
                    act.activation(qT_mem[:, :], att_ps[:, 0:D], ACT.Copy, scale=float(D) ** -0.5)\
                        .then_inc(S["q_ready"], 1)
                    wait(act, S["rows_used"], n + 1)
                    act.activation(kT[:, :], kT_ps[:, 0:D], ACT.Copy)
                    act.activation(v_mem[:, :], v_ps[:, 0:D], ACT.Copy).then_inc(S["kv_ready"], 1)

            def body(b, has_front, has_choice, has_back):
                hop_by_hop(has_front and front(b), has_choice and (lambda j, part: soften(b - 1, j, part)),
                           has_back and (lambda h, q: back(b - 2, h, q)))
                if has_choice:
                    if has_back:
                        wait(act, S["q_made"], HEADS * (b - 1))
                    act.activation(zH[:, :], zH_next[:, :], ACT.Copy).then_inc(S["zH_ready"], 1)
                if has_front:
                    wait(act, S["zH_ready"], b)
                    wait(act, S["zT"], 5 * b + 5)
                    act.activation(zH_next[:, :], zT[:, :], ACT.Copy).then_inc(S["zH_kept"], 1)
            run(act, body)

        @block.vector
        def _(dve):
            own = Steps(dve, S["own"])

            def link(ins):
                own.link(ins)

            def plain():
                dve.nop(nofuse=True)

            def norm(b, u, src, out):
                plain()
                link(dve.bn_stats(stats[:, :], src[:, :]))
                plain()
                dve.bn_aggr(mv[:, :], stats[:, :]).then_inc(S["var"], 1)
                wait(dve, S["std"], 8 * b + u + 1)
                link(dve.reciprocal(rstd[:, :], std[:, :]))
                return dve.tensor_scalar(out[:, :], src[:, :], mv[:, 0:1], rstd[:, :], ALU.subtract, ALU.mult)

            def norm_z(b, u):
                norm(b, u, x, z).then_inc(S["z"], 1)

            def add_y(b, k):
                wait(dve, S["y"], 4 * b + k + 1)
                link(dve.tensor_tensor(x[:, :], x[:, :], y_ps, ALU.add))

            def add_expert(b, first, e, weight):
                n = 12 * b + first + e
                wait(dve, S["y_made"], n + 1)
                dve.scalar_tensor_tensor(x[:, :], wide[2 + e % 2][:, 0:D], weight, x[:, :],
                                         ALU.mult, ALU.add).then_inc(S["y_used"], 1)
                wait(dve, S["y_used"], n + 1)

            def first_layer(b):
                plain()
                link(dve.tensor_copy(x[:, :], x_all[:, bass.ds(b, 1), :].rearrange("p o d -> p (o d)")))
                norm_z(b, 0)
                yield
                yield
                yield
                for e in range(EXP0):
                    add_expert(b, 0, e, gate[:, bass.ds(b, 1), e:e + 1].rearrange("p o e -> p (o e)"))
                    if e == EXP0 - 1:
                        norm_z(b, 1)
                    yield

            def mha(b):
                wait(dve, S["adj_in"], 16 * (b + 1))
                dve.tensor_scalar(absent[:, :], adjT[:, :], 0.0, -BIG, ALU.is_equal, ALU.mult)
                yield
                wait(dve, S["qkv_made"], b + 1)
                dve.tensor_tensor(k_heads[:, :].rearrange("p (h j) -> p h j", h=MHA_HEADS),
                                  wide[1][:, 0:D].unsqueeze(1).to_broadcast([P, MHA_HEADS, P]),
                                  head_mask[:, :].unsqueeze(2).to_broadcast([P, MHA_HEADS, P]), ALU.mult)\
                    .then_inc(S["k_ready"], 1)
                yield
                for j in range(2):
                    wait(dve, S["scores_made"], 2 * b + j + 1)
                    dve.reduce_max(neg_max[:, 4 * j:4 * j + 4], wide[2 + j][:, :].rearrange("p (h j) -> p h j", h=4),
                                   AX.X, negate=True).then_inc(S["max_ready"], 1)
                yield
                wait(dve, S["eT_made"], 2 * b + 2)
                dve.tensor_copy(eT_mha[:, 4 * P:8 * P], wide[1][:, :]).then_inc(S["eT_dve"], 1)
                link(dve.reciprocal(inv[:, :], sums[:, :]))
                yield
                wait(dve, S["o_made"], b + 1)
                dve.tensor_tensor(o_mha[:, :].rearrange("p (h d) -> p h d", h=MHA_HEADS),
                                  aT_ps.rearrange("p (h d) -> p h d", h=MHA_HEADS),
                                  inv[:, :].unsqueeze(2).to_broadcast([P, MHA_HEADS, 16]), ALU.mult)\
                    .then_inc(S["o_ready"], 1)
                yield
                yield
                add_y(b, 0)
                norm_z(b, 2)
                yield

            def routed_ffn(b):
                yield
                wait(dve, S["routed_in"], 64 * (b + 1))
                dve.tensor_tensor(bias_sum[:, :], bs[:, :], routed[:, :, HID:HID + 1].rearrange("p k o -> p (k o)"),
                                  ALU.add).then_inc(S["route_bias"], 1)
                yield
                yield
                yield
                add_y(b, 1)
                dve.sem_inc(S["routed_used"], 1)
                norm_z(b, 3)
                wait(dve, S["z"], 8 * b + 4)
                wait(dve, S["row_sum_made"], b + 1)
                dve.tensor_scalar(row_sum[:, :], wide[3][:, 0:1], alpha[:, :], 1.0, ALU.mult, ALU.add)\
                    .then_inc(S["row_sum_ready"], 1)
                wait(dve, S["row_std_ready"], b + 1)
                link(dve.reciprocal(row_scale[:, :], row_std[:, :]))
                link(dve.tensor_scalar(zn[:, :], z[:, :], row_scale[:, :], None, ALU.mult))
                dve.tensor_scalar(za[:, :], zn[:, :], alpha[:, :], None, ALU.mult).then_inc(S["conv_z"], 1)
                yield

            def gcn(b):
                yield
                wait(dve, S["y"], 4 * b + 3)
                link(dve.scalar_tensor_tensor(relu_in[:, :], y_ps, row_scale[:, :], gcn_b[:, :], ALU.mult, ALU.add))
                link(dve.scalar_tensor_tensor(x[:, :], relu_in[:, :], 0.0, x[:, :], ALU.max, ALU.add))
                norm_z(b, 4)
                wait(dve, S["z"], 8 * b + 5)
                link(norm(b, 5, z, zn))
                link(dve.tensor_tensor(zn[:, :], zn[:, :], gamma[:, :], ALU.mult))
                dve.tensor_tensor(zn[:, :], zn[:, :], beta[:, :], ALU.add).then_inc(S["z"], 1)
                yield

            def gated_experts(b):
                yield
                wait(dve, S["logits_made"], b + 1)
                link(dve.tensor_copy(logits[:, :], misc_ps[:, 0:EXP2]))
                plain()
                link(dve.max(top8[:, :], logits[:, :]))
                plain()
                link(dve.max_index(top8_i[:, :], top8[:, :], logits[:, :]))
                dve.tensor_tensor(odds[:, :], top8[:, 1:2], top8[:, 0:1], ALU.subtract).then_inc(S["odds_in"], 1)
                link(dve.tensor_copy(top8_f[:, :], top8_i[:, :]))
                wait(dve, S["odds_out"], b + 1)
                link(dve.tensor_scalar(w_best[:, :], odds[:, :], 1.0, None, ALU.add))
                link(dve.reciprocal(w_best[:, :], w_best[:, :]))
                link(dve.tensor_tensor(w_next[:, :], w_best[:, :], odds[:, :], ALU.mult))
                link(dve.tensor_scalar(hot[:, :], count16[:, 0:EXP2], top8_f[:, 1:2], w_next[:, :], ALU.is_equal, ALU.mult))
                link(dve.tensor_scalar(w_exp[:, :], count16[:, 0:EXP2], top8_f[:, 0:1], w_best[:, :],
                                       ALU.is_equal, ALU.mult))
                link(dve.tensor_tensor(w_exp[:, :], w_exp[:, :], hot[:, :], ALU.add))
                yield
                for e in range(EXP2):
                    add_expert(b, 4, e, w_exp[:, e:e + 1])
                    if e == EXP2 - 1:
                        norm_z(b, 6)
                    yield

            def gin(b):
                yield
                yield
                add_y(b, 3)
                norm_z(b, 7)
                yield

            def similarities(b):
                yield
                plain()
                link(dve.tensor_copy(x_all[:, bass.ds(b, 1), :].rearrange("p o d -> p (o d)"), x[:, :]))
                yield

            def front(b):
                for layer in (first_layer, mha, routed_ffn, gcn, gated_experts, gin, similarities):
                    yield from layer(b)

            def top16(*searches):
                def step(*ops):
                    plain()
                    for values, value_rest, out, out_i in searches:
                        for op in ops:
                            own.do(op(values, value_rest, out, out_i))
                    own.wait()
                step(lambda v, r, o, i: dve.max(o[:, 0:8], v))
                step(lambda v, r, o, i: dve.match_replace(r, o[:, 0:8], v, -3.0e38),
                     lambda v, r, o, i: dve.max_index(i[:, 0:8], o[:, 0:8], v))
                step(lambda v, r, o, i: dve.max(o[:, 8:16], r))
                step(lambda v, r, o, i: dve.max_index(i[:, 8:16], o[:, 8:16], r))

            def choose(batch, j, part):
                by_half = vals[:, :, :].rearrange("p (h s) k -> p s h k", h=2)
                halves = vals_f[:, :, :].rearrange("p (h s) k -> p s h k", h=2)
                shape = [P, 2, TOP, TOP]
                grid = lambda t: t[:, :].rearrange("p (h a b) -> p h a b", h=2, a=TOP)
                two = lambda ap: ap.rearrange("p (h k) -> p h k", h=2)
                if part == 0 and j == 0:
                    wait(dve, S["sims_copied"], 4 * (batch + 1))
                if part < 2:
                    cols = lambda r: slice(r * KEYS, (r + 1) * KEYS)
                    top16(*((sims[:, j, cols(r)], rest[:, cols(r)], vals[:, r, :], vals_i[:, r, :])
                            for r in (2 * part, 2 * part + 1)))
                if part == 1:
                    own.do(dve.tensor_copy(vals_f[:, :, :], vals_i[:, :, :]))
                    link(dve.tensor_tensor(grid(pair_sum), by_half[:, 0, :, :].unsqueeze(3).to_broadcast(shape),
                                           by_half[:, 1, :, :].unsqueeze(2).to_broadcast(shape), ALU.add))
                if part == 2:
                    cols = lambda r: slice(r * TOP * TOP, (r + 1) * TOP * TOP)
                    top16(*((pair_sum[:, cols(r)], pair_rest[:, cols(r)], best[:, r, :], best_i[:, r, :])
                            for r in range(2)))
                    dve.tensor_tensor(soft[:, :, :], best[:, :, :], best[:, :, 0:1].to_broadcast([P, 2, TOP]), ALU.subtract)\
                        .then_inc(S["soft_in"], 1)
                if part >= 3:
                    s = part - 3
                    if s == 0:
                        link(dve.tensor_scalar(digit[:, :, :], best_i[:, :, :], 4, None, ALU.logical_shift_right))
                    else:
                        link(dve.tensor_scalar(digit[:, :, :], best_i[:, :, :], 15, None, ALU.bitwise_and))
                    link(dve.tensor_copy(digit_f[:, :, :], digit[:, :, :]))
                    link(dve.tensor_tensor(pair_sum[:, :].rearrange("p (k a) -> p k a", a=TOP),
                                           digit_f[:, :, :].rearrange("p h k -> p (h k)").unsqueeze(2)
                                           .to_broadcast([P, 2 * TOP, TOP]),
                                           count16[:, :].unsqueeze(1).to_broadcast([P, 2 * TOP, TOP]), ALU.is_equal))
                    link(dve.tensor_tensor(grid(pair_sum), grid(pair_sum),
                                           halves[:, s, :, :].unsqueeze(2).to_broadcast(shape), ALU.mult))
                    link(dve.tensor_reduce(found[:, s, :, :].rearrange("p h k -> p (h k)"),
                                           pair_sum[:, :].rearrange("p (k a) -> p k a", a=TOP), AX.X, ALU.add))
                if part == 4:
                    if j == 0:
                        wait(dve, S["index_copied"], batch)
                    cols = slice(2 * j * TOP, 2 * (j + 1) * TOP)
                    link(dve.scalar_tensor_tensor(found[:, 1, :, :], found[:, 1, :, :], float(KEYS),
                                                  found[:, 0, :, :], ALU.mult, ALU.add))
                    own.do(dve.tensor_tensor(two(index_next[:, cols]), found[:, 1, :, :], two(head_base[:, cols]),
                                             ALU.add))
                    wait(dve, S["soft_out"], 4 * batch + j + 1)
                    link(dve.tensor_reduce(soft_sum[:, :], soft[:, :, :], AX.X, ALU.add))
                    link(dve.reciprocal(soft_sum[:, :], soft_sum[:, :]))
                    link(dve.tensor_tensor(two(mem_w_next[:, cols]), soft[:, :, :],
                                           soft_sum[:, :].unsqueeze(2).to_broadcast([P, 2, TOP]), ALU.mult))
                    if j == 3:
                        dve.sem_inc(S["chosen"], 1)

            def weights_on_diagonals(n, h):
                wait(dve, S["diag_used"], 2 * n - 1)
                w = mem_w[:, h * TOP:h * TOP + HALF]
                dve.tensor_tensor(diag[:, 0, :].rearrange("p (k t) -> p k t", k=HALF),
                                  ident[:, :].unsqueeze(1).to_broadcast([P, HALF, P]),
                                  w.unsqueeze(2).to_broadcast([P, HALF, P]), ALU.mult).then_inc(S["diag_ready"], 1)

            def take_weights(batch, attending):
                if attending:
                    wait(dve, S["diag_ready"], HEADS * batch)
                    wait(dve, S["diag2_ready"], HEADS * batch)
                    plain()
                dve.tensor_copy(mem_w[:, :], mem_w_next[:, :]).then_inc(S["mem_w"], 1)
                wait(dve, S["mem_w"], batch + 1)
                weights_on_diagonals(HEADS * batch, 0)

            def back(batch, h, q, has_choice):
                n = HEADS * batch + h
                attend, weigh = h >= 1, h < HEADS
                if attend and q == 0:
                    wait(dve, S["sim_made"], n)
                    link(dve.tensor_tensor(masked[:, :], att_ps[:, D:2 * D], causal[:, :], ALU.add))
                    dve.reduce_max(m_mem[:, :], masked[:, :], AX.X, negate=True).then_inc(S["sim_max"], 1)
                if attend and q == 1:
                    wait(dve, S["exp_mem"], n)
                    link(dve.reciprocal(inv_mem[:, :], sum_mem[:, :]))
                if h + 1 < HEADS and q == 2:
                    weights_on_diagonals(n + 1, h + 1)
                if h + 1 == HEADS and q == 2 and has_choice:
                    take_weights(batch + 1, True)
                if attend and q == 3:
                    wait(dve, S["out_y"], n)
                    if h == HEADS:
                        wait(dve, S["stored"], 16 * batch)
                    else:
                        wait(dve, S["q_made"], n + 1)
                    out = xo if h == HEADS else x_cur
                    dve.scalar_tensor_tensor(out[:, :], att_ps[:, D:2 * D], inv_mem[:, :], x_cur[:, :],
                                             ALU.mult, ALU.add).then_inc(S["acc_made"], 1)
                    wait(dve, S["acc_made"], n)
                    if h == HEADS:
                        dve.sem_inc(S["out_tile"], 1)

            def body(b, has_front, has_choice, has_back):
                hop_by_hop(has_front and front(b), has_choice and (lambda j, part: choose(b - 1, j, part)),
                           has_back and (lambda h, q: back(b - 2, h, q, has_choice)))
                if has_choice:
                    if not has_back:
                        take_weights(b - 1, False)
                    plain()
                    link(dve.tensor_copy(x_cur[:, :], x_all[:, bass.ds(b - 1, 1), :].rearrange("p o d -> p (o d)")))
            run(dve, body, own, VECTOR_LINKS)


def layout(np, v):
    a = {k: np.asarray(x) for k, x in v.items()}
    T = lambda x: np.ascontiguousarray(np.swapaxes(x, -1, -2))
    rep = lambda x, w: np.ascontiguousarray(np.broadcast_to(np.reshape(x, (1, w)), (P, w)))
    halves = lambda x: np.ascontiguousarray(x.reshape(x.shape[:-2] + (-1, P, x.shape[-1])).swapaxes(-3, -2))
    row = lambda x: np.ascontiguousarray(np.reshape(x, (1, -1)))
    column = lambda x: np.ascontiguousarray(np.reshape(x, (-1, P)).T)
    arrays = {
        "x": a["x"], "adjT": T(a["adj"]), "edge_index": a["L0_ffn_edge_index"],
        "gnn0_w1": a["L0_gnn_W1"], "gnn0_w2": halves(a["L0_gnn_W2"]), "gnn0_rms": rep(a["L0_gnn_rms_weight"], 512),
        "gnn0_b1": row(a["L0_gnn_b1"]), "gnn0_b2": row(a["L0_gnn_b2"]), "gnn0_eps": rep(a["L0_gnn_epsilon"], 1),
        "w_gat": a["L0_ffn_W_gat"],
        "gat_att": np.stack([rep(a["L0_ffn_att_src"], 16), rep(a["L0_ffn_att_dst"], 16)], 1),
        "gat_rows": np.stack([rep(a["L0_ffn_b_gat"], 16), rep(a["L0_ffn_ln_gamma"], 16), rep(a["L0_ffn_ln_beta"], 16)], 1),
        "moe0_w1": np.ascontiguousarray(a["L0_ffn_W1"].transpose(1, 0, 2)),
        "moe0_w2": np.ascontiguousarray(a["L0_ffn_W2"].reshape(4, 2, P, D).transpose(2, 0, 1, 3)),
        "moe0_b1": column(a["L0_ffn_b1"]), "moe0_b2": row(a["L0_ffn_b2"]),
        "mha_wq": T(a["L1_gnn_W_q"]), "mha_wk": T(a["L1_gnn_W_k"]), "mha_wv": T(a["L1_gnn_W_v"]),
        "mha_wo": T(a["L1_gnn_W_o"]), "w_e": rep(a["L1_gnn_W_e"], 8),
        "route_wi": T(a["L1_ffn_Wi"]), "route_bi": column(a["L1_ffn_bi"]),
        "route_ws": np.ascontiguousarray(T(a["L1_ffn_Ws"]).reshape(4, P, 2 * D).transpose(1, 0, 2)),
        "route_bs": column(a["L1_ffn_bs"]), "route_wo": halves(T(a["L1_ffn_Wo"])), "route_bo": row(a["L1_ffn_bo"]),
        "gcn_w": T(a["L2_gnn_W"]), "gcn_b": rep(a["L2_gnn_b"], D), "alpha": rep(a["L2_gnn_alpha"], 1),
        "moe2_w1": np.ascontiguousarray(a["L2_ffn_W1"].transpose(1, 0, 2)),
        "moe2_w2": np.ascontiguousarray(a["L2_ffn_W2"].reshape(8, 2, P, D).transpose(2, 0, 1, 3)),
        "moe2_b1": column(a["L2_ffn_b1"]), "moe2_b2": row(a["L2_ffn_b2"]),
        "gamma": rep(a["L2_ffn_gamma"], D), "beta": rep(a["L2_ffn_beta"], D),
        "moe2_wr": a["L2_ffn_Wr"], "moe2_br": row(a["L2_ffn_br"]),
        "gin_w1": a["L3_gnn_W1"], "gin_w2": halves(a["L3_gnn_W2"]), "gin_b1": column(a["L3_gnn_b1"]),
        "gin_b2": row(a["L3_gnn_b2"]), "eps_gin": rep(a["L3_gnn_eps"], 1),
        "mem_wq": a["L3_ffn_Wq"], "mem_wo": np.ascontiguousarray(a["L3_ffn_Wo"].reshape(8, P, D).transpose(1, 0, 2)),
        "wqT": np.ascontiguousarray(a["L3_ffn_Wq_pk"].reshape(D, 2, 8, 64).transpose(3, 2, 1, 0).reshape(64, 16, D)),
        "keysT": np.ascontiguousarray(a["L3_ffn_pk_keys"].transpose(3, 2, 0, 1).reshape(64, 16, 128)),
        "memory": np.concatenate([a["L3_ffn_keys_table"], a["L3_ffn_values_table"]], 1),
        "route": rep(a["L1_ffn_route_id"], B),
    }
    table = np.zeros((2, 17, 2 * D, 2 * D + 1), np.float32)
    table[:, :16, :, :2 * D] = T(a["L1_ffn_Wr"])
    table[:, :16, :, 2 * D] = a["L1_ffn_br"]
    arrays["route_wr"] = table.reshape(-1, 2 * D + 1)
    return arrays


def kernel(**inputs):
    import numpy as np
    import concourse.bacc as bacc
    from concourse.bass_utils import run_bass_kernel_spmd

    nc = bacc.Bacc("TRN2", target_bir_lowering=False, num_devices=1)
    arrays, io = {}, {}
    for name, a in layout(np, inputs).items():
        a = np.ascontiguousarray(a)
        arrays[f"in_{name}"] = a
        io[name] = nc.dram_tensor(f"in_{name}", a.shape, mybir.dt.from_np(a.dtype), kind="ExternalInput").ap()
    io["out"] = nc.dram_tensor("out", (B, N, D), F32, kind="ExternalOutput").ap()
    build(nc, io)
    return run_bass_kernel_spmd(nc, [arrays], core_ids=[0]).results[0]["out"]
```
